# Optimizing a Trainium2 kernel written in Bass

```python
import numpy as np
import jax
import jax.numpy as jnp

def _softmax(x, axis=-1):
    return jax.nn.softmax(x, axis=axis)

def _gelu(x):
    return jax.nn.gelu(x, approximate=True)

def _silu(x):
    return jax.nn.silu(x)

def _sigmoid(x):
    return jax.nn.sigmoid(x)

def _layernorm(x, axis=-1, eps=1e-05):
    m = jnp.mean(x, axis=axis, keepdims=True)
    v = jnp.var(x, axis=axis, keepdims=True)
    return (x - m) / jnp.sqrt(v + eps)

def _scatter_add(tgt, idx, src, axis=0):
    return tgt.at[idx].add(src)

def _segment_sum(src, seg, n):
    return jax.ops.segment_sum(src, seg, n)
kernel_name = 'mk_gnn_ffn_d2_gnn_r8_08fe4e'

def setup_inputs(seed: int=0):
    np.random.seed(seed)
    _w = jnp.asarray

    def _rec_inputs():
        import jax
        import jax.numpy as jnp
        _gk = jax.random.key(seed)
        x = -8.776e-05 + 1 * jax.random.normal(jax.random.fold_in(_gk, 1), (6250, 256), jnp.float32)
        _s = jax.random.randint(jax.random.fold_in(_gk, 2), (50000,), 0, 6250, jnp.int32)
        _d = jax.random.randint(jax.random.fold_in(_gk, 3), (50000,), 0, 6250, jnp.int32)
        _loop = jnp.arange(6250, dtype=jnp.int32)
        src = jnp.concatenate([_s, _d, _loop])
        dst = jnp.concatenate([_d, _s, _loop])
        _o = jnp.argsort(dst, stable=True)
        src = src[_o]
        dst = dst[_o]
        edge_attr_64 = 0.000279952 + 1.00013 * jax.random.normal(jax.random.fold_in(_gk, 11), (106250, 64), jnp.float32)
        edge_weight = jax.random.uniform(jax.random.fold_in(_gk, 13), (106250,), jnp.float32, 0.0, 0.999999)
        return (x, src, dst, edge_attr_64, edge_weight)
    x, src, dst, edge_attr_64, edge_weight = _rec_inputs()

    def _L0_gnn_setup():
        import jax, jax.numpy as jnp
        import numpy as np
        N, E = (2500, 40000)
        IN, OUT, EC = (256, 256, 64)
        BN_EPS = 1e-05
        key = jax.random.key(seed)
        ks = jax.random.split(key, 8)

        def lin(k, fan_in, fan_out):
            bound = 1.0 / np.sqrt(fan_in)
            return jax.random.uniform(k, (fan_in, fan_out), jnp.float32, -bound, bound)
        return {'x': jax.random.normal(ks[0], (N, IN), jnp.float32), 'edge_index': jax.random.randint(ks[1], (2, E), 0, N), 'edge_attr': jax.random.normal(ks[2], (E, EC), jnp.float32), 'W_edge': lin(ks[3], EC, IN), 'W_rel': lin(ks[4], IN, OUT), 'b_rel': jnp.zeros((OUT,), jnp.float32), 'W_root': lin(ks[5], IN, OUT), 'gamma': jnp.ones((OUT,), jnp.float32), 'beta': jnp.zeros((OUT,), jnp.float32), 'W_res': lin(ks[6], IN, OUT)}
    _L0_gnn_all = _L0_gnn_setup()
    _L0_gnn_in = {k: v for k, v in _L0_gnn_all.items() if k in ('W_edge', 'W_rel', 'b_rel', 'W_root', 'gamma', 'beta', 'W_res')}
    del _L0_gnn_all

    def _L0_ffn_setup():
        import jax, jax.numpy as jnp
        import numpy as np
        B, S, D, E, H, K = (4, 512, 256, 8, 512, 2)
        key = jax.random.key(seed)
        ks = jax.random.split(key, 6)
        x = jax.random.normal(ks[0], (B, S, D), jnp.float32)
        Wg = jax.random.normal(ks[1], (D, E), jnp.float32) * 0.02
        bg = jnp.zeros((E,), jnp.float32)
        W1 = jax.random.normal(ks[2], (E, D, H), jnp.float32) * 0.02
        b1 = jnp.zeros((E, H), jnp.float32)
        W2 = jax.random.normal(ks[3], (E, H, D), jnp.float32) * 0.02
        b2 = jnp.zeros((E, D), jnp.float32)
        return {'x': x, 'Wg': Wg, 'bg': bg, 'W1': W1, 'b1': b1, 'W2': W2, 'b2': b2}
    _L0_ffn_all = _L0_ffn_setup()
    _L0_ffn_in = {k: v for k, v in _L0_ffn_all.items() if k in ('Wg', 'bg', 'W1', 'b1', 'W2', 'b2')}
    del _L0_ffn_all

    def _L1_gnn_setup():
        import jax, jax.numpy as jnp
        import numpy as np
        N_NODES = 12500
        N_EDGES = 200000
        D = 256
        key = jax.random.key(seed)
        ks = jax.random.split(key, 8)
        h6_all = jax.random.normal(ks[0], (N_NODES, D), dtype=jnp.float32)
        edge_index = jax.random.randint(ks[1], (2, N_EDGES), 0, N_NODES, dtype=jnp.int64)
        edge_weight = jax.random.uniform(ks[2], (N_EDGES,), dtype=jnp.float32)
        s = 1.0 / np.sqrt(D)
        W = jax.random.normal(ks[3], (D, D), dtype=jnp.float32) * s
        b = jnp.zeros((D,), dtype=jnp.float32)
        W1 = jax.random.normal(ks[4], (D, D), dtype=jnp.float32) * s
        b1 = jnp.zeros((D,), dtype=jnp.float32)
        W2 = jax.random.normal(ks[5], (D, D), dtype=jnp.float32) * s
        b2 = jnp.zeros((D,), dtype=jnp.float32)
        return {'h6_all': h6_all, 'edge_index': edge_index, 'edge_weight': edge_weight, 'W': W, 'b': b, 'W1': W1, 'b1': b1, 'W2': W2, 'b2': b2}
    _L1_gnn_all = _L1_gnn_setup()
    _L1_gnn_in = {k: v for k, v in _L1_gnn_all.items() if k in ('W', 'b', 'W1', 'b1', 'W2', 'b2')}
    del _L1_gnn_all

    def _L1_ffn_setup():
        import jax, jax.numpy as jnp
        import numpy as np
        C = 256
        HID = 1024
        E = 8
        TEMP = 1.0
        key = jax.random.key(seed)
        ks = jax.random.split(key, 7)
        x = jax.random.normal(ks[0], (8, 2048, C), dtype=jnp.float32)
        W1 = jax.random.normal(ks[1], (C, HID), dtype=jnp.float32) * 0.02
        b1 = jnp.zeros((HID,), dtype=jnp.float32)
        Wg = jax.random.normal(ks[2], (HID, E), dtype=jnp.float32) * 0.02
        bg = jnp.zeros((E,), dtype=jnp.float32)
        Wd = jax.random.normal(ks[3], (E, HID, C), dtype=jnp.float32) * 0.02
        bd = jnp.zeros((E, C), dtype=jnp.float32)
        return {'x': x, 'W1': W1, 'b1': b1, 'Wg': Wg, 'bg': bg, 'Wd': Wd, 'bd': bd}
    _L1_ffn_all = _L1_ffn_setup()
    _L1_ffn_in = {k: v for k, v in _L1_ffn_all.items() if k in ('W1', 'b1', 'Wg', 'bg', 'Wd', 'bd')}
    del _L1_ffn_all
    return {'x': x, 'src': src, 'dst': dst, 'edge_attr_64': edge_attr_64, 'edge_weight': edge_weight, 'L0_gnn_W_edge': _L0_gnn_in['W_edge'], 'L0_gnn_W_rel': _L0_gnn_in['W_rel'], 'L0_gnn_b_rel': _L0_gnn_in['b_rel'], 'L0_gnn_W_root': _L0_gnn_in['W_root'], 'L0_gnn_gamma': _L0_gnn_in['gamma'], 'L0_gnn_beta': _L0_gnn_in['beta'], 'L0_gnn_W_res': _L0_gnn_in['W_res'], 'L0_ffn_Wg': _L0_ffn_in['Wg'], 'L0_ffn_bg': _L0_ffn_in['bg'], 'L0_ffn_W1': _L0_ffn_in['W1'], 'L0_ffn_b1': _L0_ffn_in['b1'], 'L0_ffn_W2': _L0_ffn_in['W2'], 'L0_ffn_b2': _L0_ffn_in['b2'], 'L1_gnn_W': _L1_gnn_in['W'], 'L1_gnn_b': _L1_gnn_in['b'], 'L1_gnn_W1': _L1_gnn_in['W1'], 'L1_gnn_b1': _L1_gnn_in['b1'], 'L1_gnn_W2': _L1_gnn_in['W2'], 'L1_gnn_b2': _L1_gnn_in['b2'], 'L1_ffn_W1': _L1_ffn_in['W1'], 'L1_ffn_b1': _L1_ffn_in['b1'], 'L1_ffn_Wg': _L1_ffn_in['Wg'], 'L1_ffn_bg': _L1_ffn_in['bg'], 'L1_ffn_Wd': _L1_ffn_in['Wd'], 'L1_ffn_bd': _L1_ffn_in['bd']}

def reference(x, src, dst, edge_attr_64, edge_weight, L0_gnn_W_edge, L0_gnn_W_rel, L0_gnn_b_rel, L0_gnn_W_root, L0_gnn_gamma, L0_gnn_beta, L0_gnn_W_res, L0_ffn_Wg, L0_ffn_bg, L0_ffn_W1, L0_ffn_b1, L0_ffn_W2, L0_ffn_b2, L1_gnn_W, L1_gnn_b, L1_gnn_W1, L1_gnn_b1, L1_gnn_W2, L1_gnn_b2, L1_ffn_W1, L1_ffn_b1, L1_ffn_Wg, L1_ffn_bg, L1_ffn_Wd, L1_ffn_bd):
    import jax
    import jax.numpy as jnp

    def _L0_gnn_ref(x, edge_index, edge_attr, W_edge, W_rel, b_rel, W_root, gamma, beta, W_res):
        import jax, jax.numpy as jnp
        import numpy as np
        N, E = (2500, 40000)
        IN, OUT, EC = (256, 256, 64)
        BN_EPS = 1e-05
        src, dst = (edge_index[0], edge_index[1])
        e = edge_attr @ W_edge
        msg = x[src] * e
        agg = jax.ops.segment_sum(msg, dst, num_segments=x.shape[0])
        h = agg @ W_rel + b_rel + x @ W_root
        h = jax.nn.relu(h)
        mean = h.mean(axis=0)
        var = ((h - mean) ** 2).mean(axis=0)
        h = (h - mean) * jax.lax.rsqrt(var + BN_EPS) * gamma + beta
        return h + x @ W_res

    def _L0_ffn_ref(x, Wg, bg, W1, b1, W2, b2):
        import jax, jax.numpy as jnp
        import numpy as np
        B, S, D, E, H, K = (4, 512, 256, 8, 512, 2)
        Bv, Sv, Dv = x.shape
        gate_scores = x @ Wg + bg
        _, idx = jax.lax.top_k(gate_scores, K)
        mask = jax.nn.one_hot(idx, E, dtype=x.dtype).sum(axis=-2)
        xf = x.reshape(-1, Dv)
        mf = mask.reshape(-1, E)
        h = jax.nn.gelu(jnp.einsum('td,edh->teh', xf, W1) + b1[None], approximate=False)
        y = jnp.einsum('teh,ehd->ted', h, W2) + b2[None]
        out = jnp.einsum('ted,te->td', y, mf)
        return out.reshape(Bv, Sv, Dv)

    def _L1_gnn_ref(h6_all, edge_index, edge_weight, W, b, W1, b1, W2, b2):
        import jax, jax.numpy as jnp
        import numpy as np
        N_NODES = 12500
        N_EDGES = 200000
        D = 256
        'GCNConv(256->256, weighted, self-loops, symmetric norm) + 2-layer MLP head.'
        N = h6_all.shape[0]
        row, col = (edge_index[0], edge_index[1])
        sl = jnp.arange(N, dtype=edge_index.dtype)
        row_sl = jnp.concatenate([row, sl])
        col_sl = jnp.concatenate([col, sl])
        ew_sl = jnp.concatenate([edge_weight, jnp.ones((N,), dtype=edge_weight.dtype)])
        deg = jax.ops.segment_sum(ew_sl, row_sl, num_segments=N)
        dinv = jnp.where(deg > 0, jax.lax.rsqrt(deg), 0.0)
        norm = dinv[row_sl] * ew_sl * dinv[col_sl]
        xw = h6_all @ W
        msgs = xw[col_sl] * norm[:, None]
        h7 = jax.ops.segment_sum(msgs, row_sl, num_segments=N) + b
        h = jax.nn.relu(h7 @ W1 + b1)
        out = h @ W2 + b2
        return out

    def _L1_ffn_ref(x, W1, b1, Wg, bg, Wd, bd):
        import jax, jax.numpy as jnp
        import numpy as np
        C = 256
        HID = 1024
        E = 8
        TEMP = 1.0
        orig_shape = x.shape
        xf = x.reshape(-1, orig_shape[-1])
        H = jax.nn.gelu(xf @ W1 + b1, approximate=False)
        probs = jax.nn.softmax((H @ Wg + bg) / TEMP, axis=-1)
        assign = jnp.argmax(probs, axis=-1)
        out = jnp.zeros_like(xf)
        for e in range(Wd.shape[0]):
            y = H @ Wd[e] + bd[e]
            sel = (assign == e)[:, None]
            out = out + jnp.where(sel, probs[:, e:e + 1] * y, 0.0)
        return out.reshape(orig_shape)
    edge_index = jnp.stack([src, dst])
    x = x + _L0_gnn_ref(_layernorm(x, axis=-1), edge_index, edge_attr_64, L0_gnn_W_edge, L0_gnn_W_rel, L0_gnn_b_rel, L0_gnn_W_root, L0_gnn_gamma, L0_gnn_beta, L0_gnn_W_res)
    x = x + _L0_ffn_ref(_layernorm(x, axis=-1)[None], L0_ffn_Wg, L0_ffn_bg, L0_ffn_W1, L0_ffn_b1, L0_ffn_W2, L0_ffn_b2)[0]
    x = x + _L1_gnn_ref(_layernorm(x, axis=-1), edge_index, edge_weight, L1_gnn_W, L1_gnn_b, L1_gnn_W1, L1_gnn_b1, L1_gnn_W2, L1_gnn_b2)
    x = x + _L1_ffn_ref(_layernorm(x, axis=-1)[None], L1_ffn_W1, L1_ffn_b1, L1_ffn_Wg, L1_ffn_bg, L1_ffn_Wd, L1_ffn_bd)[0]
    return x

_drawn_inputs = setup_inputs


def setup_inputs(seed=0):
    import zlib

    import numpy as np

    out = dict(_drawn_inputs(seed))
    spreads = {'L0_gnn_b_rel': (0.0, 0.1),
     'L0_gnn_gamma': (1.0, 0.2),
     'L0_gnn_beta': (0.0, 0.1),
     'L0_ffn_bg': (0.0, 0.1),
     'L0_ffn_b1': (0.0, 0.34),
     'L0_ffn_b2': (0.0, 0.1),
     'L1_gnn_b': (0.0, 0.1),
     'L1_gnn_b1': (0.0, 0.1),
     'L1_gnn_b2': (0.0, 0.1),
     'L1_ffn_b1': (0.0, 0.8),
     'L1_ffn_bg': (0.0, 0.543),
     'L1_ffn_bd': (0.0, 0.8)}
    factors = {'L1_ffn_W1': 4.089, 'L1_ffn_Wg': 4.177, 'L1_ffn_Wd': 4.991}
    for name, (base, spread) in spreads.items():
        noise = np.random.default_rng([zlib.crc32(name.encode()), seed]).standard_normal(out[name].shape)
        drawn = base * np.exp(spread * noise) if base else spread * noise
        out[name] = jnp.asarray(drawn.astype(out[name].dtype))
    for name, factor in factors.items():
        out[name] = (out[name] * factor).astype(out[name].dtype)
    return out
```

```python
from contextlib import ExitStack

import numpy as np
import concourse.bass as bass
from concourse import mybir

FP32 = mybir.dt.float32
BF16 = mybir.dt.bfloat16
I32 = mybir.dt.int32
ALU = mybir.AluOpType
ACT = mybir.ActivationFunctionType
AX = mybir.AxisListType
EngineType = mybir.EngineType

P = 128
D = 256
KD = D // P
NODES = 6250
TILES = -(-NODES // P)
NODES_PAD = TILES * P
SLOTS = TILES + 1
EDGES = 106250
COLS = 832
EDGES_PAD = COLS * P
ATTR = 64
UNROLL = 16
STEPS = -(-(EDGES // P + TILES) // UNROLL) * UNROLL
EPS = 1e-5
HALVES = 2
HALF = EDGES_PAD // HALVES
RANK_BLOCKS = 16
RANK_COLS = COLS // HALVES // RANK_BLOCKS
RANK_LEN = RANK_COLS * P
GROUP = 7
GROUPS = TILES // GROUP
WIDE = NODES_PAD // 14
WIDES = 14
EXPERTS = 8
TOP0, TOP1 = 2, 1
HID0, HID1 = 512, 1024
CHUNKS0 = -(-((NODES_PAD * TOP0 + EXPERTS * (P - 1)) // P) // 2) * 2
CHUNKS1 = -(-((NODES_PAD * TOP1 + EXPERTS * (P - 1)) // P) // 2) * 2
REC0 = 2
REC1 = 4


def static(t):
    return isinstance(t, int)


def pairs(eng, n, body):
    body(0, 0)
    body(1, 1)
    if n >= 4:
        with eng.Fori(1, n // 2) as i:
            body(i * 2, 0)
            body(i * 2 + 1, 1)
    if n % 2:
        body(n - 1, 0)


def unrolled(eng, n, body):
    body(0, 0)
    with eng.Fori(1, n // UNROLL) as i:
        body(i * UNROLL, i)


class Core:

    def __init__(self, nc, ctx):
        self.nc, self.ctx, self.live = nc, ctx, []

    def sb(self, ctx, name, shape, dt):
        return ctx.enter_context(self.nc.sbuf_tensor(name, shape, dt))

    def ps(self, ctx, name, shape, dt=FP32):
        return ctx.enter_context(self.nc.psum_tensor(name, shape, dt))

    def sem(self, name):
        s = self.nc.alloc_semaphore(name=name)
        self.live.append(s)
        return s

    def clear(self, first):
        self.nc.clear_and_free_semaphores(self.live[first:])
        self.nc.all_engine_barrier()
        del self.live[first:]

    def dram(self, name, shape, dt):
        return self.nc.dram_tensor(name, shape, dt, kind="Internal").ap()


def phase(f):
    def run(c, *args, **kwargs):
        first = len(c.live)
        f(c, *args, **kwargs)
        c.clear(first)
    return run


def tiles_view(a):
    return a.rearrange("(g a p) d -> g p a d", a=GROUP, p=P)


@phase
def normalize(c, name, src, dst, eps, row_scale=None, beside=None):
    nc = c.nc
    with ExitStack() as ctx:
        x = c.sb(ctx, name + "_x", [P, 2, GROUP, D], FP32)
        y = c.sb(ctx, name + "_y", [P, 2, GROUP, D], FP32)
        st = c.sb(ctx, name + "_st", [P, 2, GROUP, 6], FP32)
        mv = c.sb(ctx, name + "_mv", [P, 2, GROUP, 2], FP32)
        sd = c.sb(ctx, name + "_sd", [P, 2, GROUP], FP32)
        rs = c.sb(ctx, name + "_rs", [P, 2, GROUP], FP32)
        loaded = [c.sem(f"{name}_loaded{u}") for u in range(2)]
        stored = [c.sem(f"{name}_stored{u}") for u in range(2)]
        stats = c.sem(name + "_stats")
        moments = c.sem(name + "_moments")
        root = c.sem(name + "_root")
        inverse = c.sem(name + "_inverse")
        normed = c.sem(name + "_normed")
        passed = c.sem(name + "_passed")
        block = ctx.enter_context(nc.Block())
        if beside is not None:
            beside(block)
        src_g, dst_g = tiles_view(src), tiles_view(dst)

        def half(g):
            return g // 2 if static(g) else g // 2

        @block.sync
        def _(sp):
            def load(g, u, k):
                if not (static(k) and k < 1):
                    sp.wait_ge(normed, k * 2 + u - 1)
                sp.dma_start(x[:, u], src_g[bass.ds(g, 1)].rearrange("o p a d -> p (o a) d")).then_inc(loaded[u], 16)

            def store(g, u, k):
                sp.wait_ge(normed, k * 2 + u + 1)
                sp.dma_start(dst_g[bass.ds(g, 1)].rearrange("o p a d -> p (o a) d"), y[:, u]).then_inc(stored[u], 16)

            load(0, 0, 0)
            load(1, 1, 0)
            with sp.Fori(0, (GROUPS - 1) // 2 - 1) as k:
                for u in range(2):
                    store(k * 2 + u, u, k)
                    load(k * 2 + 2 + u, u, k + 1)
            last = (GROUPS - 1) // 2
            store(GROUPS - 3, 0, last - 1)
            load(GROUPS - 1, 0, last)
            store(GROUPS - 2, 1, last - 1)
            store(GROUPS - 1, 0, last)
            sp.wait_ge(stored[0], 16 * (last + 1))
            sp.wait_ge(stored[1], 16 * last)

        def each_group(eng, body):
            for u in range(2):
                body(u, u, 0)
            with eng.Fori(1, GROUPS // 2) as k:
                for u in range(2):
                    body(k * 2 + u, u, k)
            body(GROUPS - 1, 0, GROUPS // 2)

        @block.vector
        def _(dve):
            def body(g, u, k):
                dve.wait_ge(loaded[u], k * 16 + 16)
                for a in range(GROUP):
                    last = nc.vector.bn_stats(st[:, u, a], x[:, u, a])
                last.then_inc(stats, 1)
                dve.wait_ge(stats, g + 1)
                if not (static(g) and g < 2):
                    dve.wait_ge(root, g - 1)
                dve.sem_inc(passed, 1)
                for a in range(GROUP):
                    last = nc.vector.bn_aggr(mv[:, u, a], st[:, u, a])
                last.then_inc(moments, 1)
                dve.wait_ge(root, g + 1)
                nc.vector.reciprocal(rs[:, u], sd[:, u]).then_inc(inverse, 1)
                dve.wait_ge(inverse, g * 1 + 1) if row_scale is None else dve.wait_ge(inverse, g * 2 + 1)
                if row_scale is not None:
                    nc.vector.tensor_tensor(rs[:, u], rs[:, u], row_scale[:, bass.ds(g * GROUP, GROUP)],
                                            ALU.mult).then_inc(inverse, 1)
                    dve.wait_ge(inverse, g * 2 + 2)
                if not (static(g) and g < 2):
                    dve.wait_ge(stored[u], k * 16)
                for a in range(GROUP):
                    last = nc.vector.tensor_scalar(y[:, u, a], x[:, u, a], mv[:, u, a, 0:1], rs[:, u, a:a + 1],
                                                   ALU.subtract, ALU.mult)
                last.then_inc(normed, 1)
            each_group(dve, body)

        @block.scalar
        def _(act):
            def body(g, u, k):
                act.wait_ge(moments, g + 1)
                if not (static(g) and g < 2):
                    act.wait_ge(inverse, (g - 1) * (1 if row_scale is None else 2))
                nc.scalar.activation(sd[:, u], mv[:, u, :, 1], ACT.Sqrt, bias=eps[:, 0:1]).then_inc(root, 1)
            each_group(act, body)


@phase
def read_transposed(c, name, src, dst_t, ident, beside=None):
    nc = c.nc
    with ExitStack() as ctx:
        x = c.sb(ctx, name + "_x", [P, 2, D], FP32)
        pt = [c.ps(ctx, f"{name}_pt{u}", [P, KD, P]) for u in range(2)]
        loaded = [c.sem(f"{name}_loaded{u}") for u in range(2)]
        turned = c.sem(name + "_turned")
        copied = c.sem(name + "_copied")
        passed = c.sem(name + "_passed")
        block = ctx.enter_context(nc.Block())
        if beside is not None:
            beside(block)

        @block.sync
        def _(sp):
            def body(t, u):
                if not (static(t) and t < 2):
                    sp.wait_ge(turned, t - 1)
                sp.dma_start(x[:, u], src[bass.ds(t * P, P), :]).then_inc(loaded[u], 16)
            pairs(sp, TILES, body)

        @block.tensor
        def _(pe):
            def body(t, u):
                pe.wait_ge(loaded[u], (t // 2) * 16 + 16)
                if not (static(t) and t < 2):
                    pe.wait_ge(copied, t - 1)
                for k in range(KD):
                    last = nc.tensor.transpose(pt[u][:, k], x[:, u, k * P:(k + 1) * P], ident[:])
                last.then_inc(turned, 1)
            pairs(pe, TILES, body)

        @block.scalar
        def _(act):
            def body(t, u):
                act.wait_ge(turned, t + 1)
                act.sem_inc(passed, 1)
                nc.scalar.activation(dst_t[:, :, bass.ds(t * P, P)], pt[u][:], ACT.Copy).then_inc(copied, 1)
            pairs(act, TILES, body)


@phase
def tile_ids(c, src_flat, dst_flat, ids_src, ids_dst, rec0, posrec, src_cols, dst_cols, ew_cols):
    nc = c.nc
    with ExitStack() as ctx:
        s_i = c.sb(ctx, "ids_s", [P, COLS], I32)
        d_i = c.sb(ctx, "ids_d", [P, COLS], I32)
        t_i = c.sb(ctx, "ids_t", [P, 2, COLS], I32)
        t_b = c.sb(ctx, "ids_b", [P, 2, COLS], BF16)
        r0 = c.sb(ctx, "ids_r0", [P, COLS, REC0], I32)
        sc = c.sb(ctx, "ids_sc", [P, COLS], I32)
        dc = c.sb(ctx, "ids_dc", [P, COLS], I32)
        ec = c.sb(ctx, "ids_ec", [P, COLS], FP32)
        loaded = c.sem("ids_loaded")
        loaded_cols = c.sem("ids_loaded_cols")
        shifted = c.sem("ids_shifted")
        made = c.sem("ids_made")
        stored = c.sem("ids_stored")
        block = ctx.enter_context(nc.Block())

        @block.sync
        def _(sp):
            sp.dma_start(s_i[:], src_flat.rearrange("(p j) -> p j", p=P)).then_inc(loaded, 16)
            sp.dma_start(d_i[:], dst_flat.rearrange("(p j) -> p j", p=P)).then_inc(loaded, 16)
            sp.dma_start(sc[:], src_cols).then_inc(loaded_cols, 16)
            sp.dma_start(dc[:], dst_cols).then_inc(loaded_cols, 16)
            sp.dma_start(ec[:], ew_cols).then_inc(loaded_cols, 16)
            sp.wait_ge(made, 1)
            sp.dma_start(ids_src.rearrange("(p j) -> p j", p=P), t_b[:, 0]).then_inc(stored, 16)
            sp.dma_start(ids_dst.rearrange("(p j) -> p j", p=P), t_b[:, 1]).then_inc(stored, 16)
            sp.wait_ge(made, 2)
            sp.dma_start(rec0.rearrange("(p j) w -> p (j w)", p=P), r0[:].rearrange("p j w -> p (j w)")).then_inc(stored, 16)
            sp.wait_ge(stored, 48)

        @block.vector
        def _(dve):
            dve.wait_ge(loaded, 32)
            nc.vector.tensor_scalar(t_i[:, 0], s_i[:], 7, None, ALU.arith_shift_right)
            nc.vector.tensor_scalar(t_i[:, 1], d_i[:], 7, None, ALU.arith_shift_right).then_inc(shifted, 1)
            dve.wait_ge(shifted, 1)
            nc.vector.tensor_copy(t_b[:], t_i[:]).then_inc(made, 1)
            nc.vector.tensor_scalar(r0[:, :, 0], s_i[:], NODES_PAD - 1, None, ALU.min)
            nc.vector.tensor_copy(r0[:, :, 1].bitcast(FP32), d_i[:]).then_inc(made, 1)
            dve.wait_ge(loaded_cols, 48)
            nc.vector.tensor_copy(posrec[:, :, 1].bitcast(FP32), sc[:])
            nc.vector.tensor_scalar(posrec[:, :, 2], dc[:], NODES_PAD - 1, None, ALU.min)
            nc.vector.tensor_copy(posrec[:, :, 3], ec[:].bitcast(I32))
            nc.vector.memset(posrec[:, :, 4], 0)


@phase
def count(c, name, ids, consts, tab, base):
    nc = c.nc
    with ExitStack() as ctx:
        ids_b = c.sb(ctx, name + "_ids", [P, 2, RANK_LEN], BF16)
        hit = c.sb(ctx, name + "_hit", [P, 2, RANK_LEN], BF16)
        part = c.sb(ctx, name + "_part", [P, RANK_BLOCKS], FP32)
        cnt = c.sb(ctx, name + "_cnt", [P, 1], FP32)
        small = c.sb(ctx, name + "_small", [P, 8], FP32)
        small_i = c.sb(ctx, name + "_small_i", [P, 2], I32)
        ge = c.sb(ctx, name + "_ge", [P, STEPS], FP32)
        rows = c.sb(ctx, name + "_rows", [1, 2, STEPS], FP32)
        pm = c.ps(ctx, name + "_pm", [P, 512])
        pt = [c.ps(ctx, f"{name}_pt{i}", [1, 512]) for i in range(4)]
        loaded = [c.sem(f"{name}_loaded{u}") for u in range(2)]
        counted = c.sem(name + "_counted")
        small_done = c.sem(name + "_small_done")
        product = c.sem(name + "_product")
        table = c.sem(name + "_table")
        passed = c.sem(name + "_passed")
        bucket, fold, before, lower, diff, ones, steps = (consts[k] for k in (
            "bucket", "fold", "before", "lower", "diff", "ones", "steps"))
        ids_h = ids.rearrange("(h n) -> h n", h=HALVES)

        block = ctx.enter_context(nc.Block())

        @block.sync
        def _(sp):
            def body(k, u):
                if not (static(k) and k < 2):
                    sp.wait_ge(counted, k - 1)
                for h in range(HALVES):
                    sp.dma_start(ids_b[h * 64:h * 64 + 64, u],
                                 ids_h[h:h + 1, bass.ds(k * RANK_LEN, RANK_LEN)].broadcast_to([64, RANK_LEN])).then_inc(loaded[u], 16)
            pairs(sp, RANK_BLOCKS, body)

        @block.vector
        def _(dve):
            def body(k, u):
                dve.wait_ge(loaded[u], (k // 2) * 32 + 32)
                if not (static(k) and k < 2):
                    dve.wait_ge(counted, k - 1)
                nc.vector.tensor_scalar(hit[:, u], ids_b[:, u], bucket[:, 0:1], 0.0, ALU.is_equal, ALU.add,
                                        accum_out=part[:, bass.ds(k, 1)]).then_inc(counted, 1)
            pairs(dve, RANK_BLOCKS, body)
            dve.wait_ge(counted, RANK_BLOCKS)
            nc.vector.reduce_sum(cnt[:], part[:], AX.X).then_inc(small_done, 1)
            dve.wait_ge(product, 1)
            nc.vector.tensor_copy(small[:, 0:2], pm[:, 0:2]).then_inc(small_done, 1)
            nc.vector.tensor_scalar(base[:], pm[:, 0:1], -1.0, None, ALU.add)
            dve.wait_ge(small_done, 2)
            nc.vector.tensor_scalar(small_i[:, 0:1], small[:, 1:2], float(P - 1), None, ALU.add).then_inc(small_done, 1)
            dve.wait_ge(small_done, 3)
            nc.vector.tensor_scalar(small_i[:, 1:2], small_i[:, 0:1], 7, None, ALU.arith_shift_right).then_inc(small_done, 1)
            dve.wait_ge(small_done, 4)
            nc.vector.tensor_copy(small[:, 2:3], small_i[:, 1:2]).then_inc(small_done, 1)
            dve.wait_ge(product, 2)
            nc.vector.tensor_copy(small[:, 3:4], pm[:, 2:3]).then_inc(small_done, 1)
            dve.wait_ge(small_done, 6)
            nc.vector.scalar_tensor_tensor(small[:, 4:5], small[:, 3:4], -float(P), small[:, 0:1],
                                           ALU.mult, ALU.add).then_inc(small_done, 1)
            nc.vector.tensor_scalar(ge[:], steps[:], small[:, 3:4], None, ALU.is_ge)
            dve.wait_ge(product, 3)
            nc.vector.tensor_copy(small[:, 5:6], pm[:, 3:4]).then_inc(small_done, 1)
            dve.wait_ge(product, 4)
            for i in range(2):
                s = slice(i * (STEPS // 2), (i + 1) * (STEPS // 2))
                nc.vector.scalar_tensor_tensor(rows[:, 0, s], steps[0:1, s], float(P), pt[i][:, 0:STEPS // 2],
                                               ALU.mult, ALU.add)
                last = nc.vector.tensor_scalar(rows[:, 1, s], pt[2 + i][:, 0:STEPS // 2], -1.0, None, ALU.add)
            last.then_inc(small_done, 1)
            dve.wait_ge(small_done, 9)
            nc.vector.tensor_scalar(tab[:, 0], rows[:, 0], float(EDGES_PAD - P), None, ALU.min)
            nc.vector.tensor_scalar(tab[:, 1], rows[:, 1], float(P), None, ALU.mult).then_inc(table, 1)

        @block.tensor
        def _(pe):
            pe.wait_ge(small_done, 1)
            nc.tensor.matmul(pm[:, 0:1], before[:], cnt[:], start=True, stop=True)
            nc.tensor.matmul(pm[:, 1:2], fold[:], cnt[:], start=True, stop=True).then_inc(product, 1)
            pe.wait_ge(small_done, 5)
            nc.tensor.matmul(pm[:, 2:3], lower[:], small[:, 2:3], start=True, stop=True).then_inc(product, 1)
            pe.wait_ge(small_done, 7)
            nc.tensor.matmul(pm[:, 3:4], diff[:], small[:, 4:5], start=True, stop=True).then_inc(product, 1)
            pe.wait_ge(small_done, 8)
            for i in range(2):
                s = slice(i * (STEPS // 2), (i + 1) * (STEPS // 2))
                nc.tensor.matmul(pt[i][:, 0:STEPS // 2], small[0:SLOTS, 5:6], ge[0:SLOTS, s], start=True, stop=True)
                last = nc.tensor.matmul(pt[2 + i][:, 0:STEPS // 2], ones[0:SLOTS, 0:1], ge[0:SLOTS, s],
                                        start=True, stop=True)
            last.then_inc(product, 1)


@phase
def rank(c, name, ids, consts, base, posrec):
    nc = c.nc
    with ExitStack() as ctx:
        ids_b = c.sb(ctx, name + "_ids", [P, 2, RANK_LEN], BF16)
        hit = c.sb(ctx, name + "_hit", [P, RANK_LEN], BF16)
        run = c.sb(ctx, name + "_run", [P, 2, RANK_LEN], FP32)
        place = c.sb(ctx, name + "_place", [P, 2, RANK_LEN], FP32)
        unit = c.sb(ctx, name + "_unit", [P, RANK_LEN], BF16)
        pp = [c.ps(ctx, f"{name}_pp{u}", [P, RANK_COLS, HALVES]) for u in range(2)]
        loaded = [c.sem(f"{name}_loaded{u}") for u in range(2)]
        hits = c.sem(name + "_hits")
        scanned = c.sem(name + "_scanned")
        placed = c.sem(name + "_placed")
        summed = c.sem(name + "_summed")
        kept = c.sem(name + "_kept")
        unit_set = c.sem(name + "_unit_set")
        passed = c.sem(name + "_passed")
        bucket, halves = consts["bucket"], consts["halves"]
        ids_h = ids.rearrange("(h n) -> h n", h=HALVES)
        block = ctx.enter_context(nc.Block())

        @block.sync
        def _(sp):
            def body(k, u):
                if not (static(k) and k < 2):
                    sp.wait_ge(hits, k - 1)
                for h in range(HALVES):
                    sp.dma_start(ids_b[h * 64:h * 64 + 64, u],
                                 ids_h[h:h + 1, bass.ds(k * RANK_LEN, RANK_LEN)].broadcast_to([64, RANK_LEN])).then_inc(loaded[u], 16)
            pairs(sp, RANK_BLOCKS, body)

        @block.vector
        def _(dve):
            nc.vector.memset(unit[:], 1.0).then_inc(unit_set, 1)
            dve.wait_ge(unit_set, 1)

            def body(k, u):
                dve.wait_ge(loaded[u], (k // 2) * 32 + 32)
                if not (static(k) and k < 1):
                    dve.wait_ge(placed, k)
                nc.vector.tensor_scalar(hit[:], ids_b[:, u], bucket[:, 0:1], None, ALU.is_equal).then_inc(hits, 1)
                dve.wait_ge(hits, k + 1)
                if not (static(k) and k < 1):
                    dve.wait_ge(scanned, k)
                start = 0.0 if static(k) and k == 0 else run[:, 1 - u, RANK_LEN - 1:RANK_LEN]
                nc.vector.tensor_tensor_scan(run[:, u], unit[:], hit[:], start, ALU.mult, ALU.add).then_inc(scanned, 1)
                dve.wait_ge(scanned, k + 1)
                if not (static(k) and k < 2):
                    dve.wait_ge(summed, k - 1)
                nc.vector.scalar_tensor_tensor(place[:, u], run[:, u], base[:, 0:1], hit[:],
                                               ALU.add, ALU.mult).then_inc(placed, 1)
                if not (static(k) and k < 1):
                    keep(k - 1, 1 - u)

            def keep(k, u):
                dve.wait_ge(summed, k + 1)
                dve.sem_inc(passed, 1)
                for h in range(HALVES):
                    last = nc.vector.tensor_copy(posrec[:, bass.ds(k * RANK_COLS + h * (COLS // 2), RANK_COLS), 0],
                                                 pp[u][:, :, h])
                last.then_inc(kept, 1)
            pairs(dve, RANK_BLOCKS, body)
            keep(RANK_BLOCKS - 1, 1)

        @block.tensor
        def _(pe):
            def body(k, u):
                pe.wait_ge(placed, k + 1)
                if not (static(k) and k < 2):
                    pe.wait_ge(kept, k - 1)
                for j in range(RANK_COLS):
                    last = nc.tensor.matmul(pp[u][:, j], place[:, u, j * P:(j + 1) * P], halves[:],
                                            start=True, stop=True)
                last.then_inc(summed, 1)
            pairs(pe, RANK_BLOCKS, body)


@phase
def aggregate_edges(c, name, table, rec, rec_words, tab, node_ids, agg_t, attr_t=None, w_edge=None):
    nc = c.nc
    U = UNROLL
    with ExitStack() as ctx:
        with_attr = attr_t is not None
        rb = c.sb(ctx, name + "_rec", [P, U, rec_words], I32)
        rows = c.sb(ctx, name + "_rows", [P, U, D], FP32)
        pick = c.sb(ctx, name + "_pick", [P, U, P], FP32)
        if with_attr:
            at = c.sb(ctx, name + "_attr", [ATTR, U, P], FP32)
            msg = c.sb(ctx, name + "_msg", [P, U, D], FP32)
            pe_edge = [c.ps(ctx, f"{name}_pe{u}", [P, 512]) for u in range(2)]
            got_at = [c.sem(f"{name}_got_at{u}") for u in range(U)]
            edge_done = [c.sem(f"{name}_edge_done{u}") for u in range(U)]
            msg_done = [c.sem(f"{name}_msg_done{u}") for u in range(U)]
        else:
            msg = rows
            picked = [c.sem(f"{name}_picked{u}") for u in range(U)]
        pa = [c.ps(ctx, f"{name}_pa{u}", [P, KD, P]) for u in range(2)]
        got_rec = [c.sem(f"{name}_got_rec{u}") for u in range(U)]
        got_rows = [c.sem(f"{name}_got_rows{u}") for u in range(U)]
        summed = [c.sem(f"{name}_summed{u}") for u in range(U)]
        added = [c.sem(f"{name}_added{u}") for u in range(U)]
        zeroed = c.sem(name + "_zeroed")
        passed = c.sem(name + "_passed")
        block = ctx.enter_context(nc.Block())

        def wait_steps_before(eng, sem, u, i, back):
            if u >= back:
                eng.wait_ge(sem[u - back], i + 1)
            elif not static(i):
                eng.wait_ge(sem[u - back + U], i * 1)

        def numbers(engine, row, s0, top):
            return nc.values_load_multi_w_load_instructions(
                tab[0:1, row, bass.ds(s0, 4)], engines=(engine,), min_val=0, max_val=top,
                skip_runtime_bounds_check_because="the table is clamped to this range when it is made")[1]

        @block.sync
        def _(sp):
            def body(s0, i):
                for u in range(U):
                    if u % 4 == 0:
                        start = numbers(EngineType.SP, 0, s0 + u, EDGES_PAD - P)
                    wait_steps_before(sp, summed, u, i, U)
                    sp.dma_start(rb[:, u], rec[bass.ds(start[u % 4], P), :]).then_inc(got_rec[u], 16)
            unrolled(sp, STEPS, body)

        if with_attr:
            @block.scalar
            def _(act):
                def body(s0, i):
                    for u in range(U):
                        if u % 4 == 0:
                            start = numbers(EngineType.Activation, 0, s0 + u, EDGES_PAD - P)
                        wait_steps_before(act, summed, u, i, U)
                        act.dma_start(at[:, u], attr_t[:, bass.ds(start[u % 4], P)]).then_inc(got_at[u], 16)
                unrolled(act, STEPS, body)

        @block.gpsimd
        def _(pool):
            row_word = 0 if with_attr else 1

            def body(s0, i):
                for u in range(U):
                    wait_steps_before(pool, summed, u, i, U)
                    if not static(i):
                        pool.sem_inc(passed, 1)
                    pool.wait_ge(got_rec[u], i * 16 + 16)
                    pool.sem_inc(passed, 1)
                    pool.indirect_dma_start(
                        out=rows[:, u], out_offset=None, in_=table,
                        in_offset=bass.IndirectOffsetOnAxis(ap=rb[:, u, row_word:row_word + 1], axis=0),
                    ).then_inc(got_rows[u], 16)
            unrolled(pool, STEPS, body)

        @block.vector
        def _(dve):
            nc.vector.memset(agg_t[:], 0.0).then_inc(zeroed, 1)
            dve.wait_ge(zeroed, 1)

            def front(u, i, shift):
                dve.wait_ge(got_rec[u], i * 16 + 16)
                wait_steps_before(dve, summed, u, i, U)
                if with_attr:
                    nc.vector.tensor_scalar(pick[:, u], node_ids[:, bass.ds(shift, P)], rb[:, u, 1:2].bitcast(FP32),
                                            None, ALU.is_equal)
                    dve.wait_ge(got_rows[u], i * 16 + 16)
                    dve.wait_ge(edge_done[u], i + 1)
                    nc.vector.tensor_tensor(msg[:, u], rows[:, u], pe_edge[u % 2][:, 0:D], ALU.mult).then_inc(msg_done[u], 1)
                else:
                    nc.vector.tensor_scalar(pick[:, u], node_ids[:, bass.ds(shift, P)], rb[:, u, 0:1].bitcast(FP32),
                                            rb[:, u, 2:3].bitcast(FP32), ALU.is_equal, ALU.mult).then_inc(picked[u], 1)

            def back(u, i, shift):
                dve.wait_ge(summed[u], i + 1)
                wait_steps_before(dve, added, u, i, 1)
                at_tile = agg_t[:, :, bass.ds(shift, P)]
                nc.vector.tensor_tensor(at_tile, at_tile, pa[u % 2][:], ALU.add).then_inc(added[u], 1)

            def body(s0, i):
                shifts = []
                for u in range(U):
                    if u % 4 == 0:
                        shifts += numbers(EngineType.DVE, 1, s0 + u, TILES * P)
                    front(u, i, shifts[u])
                    if u:
                        back(u - 1, i, shifts[u - 1])
                back(U - 1, i, shifts[-1])
            unrolled(dve, STEPS, body)

        @block.tensor
        def _(pe):
            def edge(u, i):
                pe.wait_ge(got_at[u], i * 16 + 16)
                wait_steps_before(pe, msg_done, u, i, 2)
                nc.tensor.matmul(pe_edge[u % 2][:, 0:D], at[:, u], w_edge[:], start=True, stop=True).then_inc(edge_done[u], 1)

            def add_up(u, i):
                if with_attr:
                    pe.wait_ge(msg_done[u], i + 1)
                else:
                    pe.wait_ge(got_rows[u], i * 16 + 16)
                    pe.wait_ge(picked[u], i + 1)
                wait_steps_before(pe, added, u, i, 2)
                for k in range(KD):
                    last = nc.tensor.matmul(pa[u % 2][:, k], msg[:, u, k * P:(k + 1) * P], pick[:, u],
                                            start=True, stop=True)
                last.then_inc(summed[u], 1)

            def body(s0, i):
                for u in range(U):
                    if with_attr:
                        edge(u, i)
                        if u:
                            add_up(u - 1, i)
                    else:
                        add_up(u, i)
                if with_attr:
                    add_up(U - 1, i)
            unrolled(pe, STEPS, body)


@phase
def first_dense(c, agg_t, xn_t, w_rel, w_root, b_rel, gamma, beta, eps, beside=None):
    nc = c.nc
    with ExitStack() as ctx:
        ph = [[c.ps(ctx, f"fd_ph{u}{m}", [P, 512]) for m in range(KD)] for u in range(2)]
        st = c.sb(ctx, "fd_st", [P, KD, WIDES, 6], FP32)
        mv = c.sb(ctx, "fd_mv", [P, KD, 2], FP32)
        sd = c.sb(ctx, "fd_sd", [P, KD], FP32)
        rs = c.sb(ctx, "fd_rs", [P, KD], FP32)
        scale = c.sb(ctx, "fd_scale", [P, KD], FP32)
        shift = c.sb(ctx, "fd_shift", [P, KD], FP32)
        tmp = c.sb(ctx, "fd_tmp", [P, KD], FP32)
        multiplied = c.sem("fd_multiplied")
        relued = c.sem("fd_relued")
        passed = c.sem("fd_passed")
        stats = c.sem("fd_stats")
        small = c.sem("fd_small")
        root = c.sem("fd_root")
        block = ctx.enter_context(nc.Block())
        if beside is not None:
            beside(block)

        @block.tensor
        def _(pe):
            def body(g, u):
                if not (static(g) and g < 2):
                    pe.wait_ge(relued, g * 2 - 2)
                for m in range(KD):
                    steps = [(w, x, k) for w, x in ((w_rel, agg_t), (w_root, xn_t)) for k in range(KD)]
                    for n, (w, x, k) in enumerate(steps):
                        last = nc.tensor.matmul(ph[u][m][:, 0:WIDE], w[:, k, m * P:(m + 1) * P],
                                                x[:, k, bass.ds(g * WIDE, WIDE)], start=n == 0, stop=n == len(steps) - 1)
                last.then_inc(multiplied, 1)
            pairs(pe, WIDES, body)

        @block.scalar
        def _(act):
            def body(g, u):
                act.wait_ge(multiplied, g + 1)
                act.sem_inc(passed, 1)
                for m in range(KD):
                    nc.scalar.activation(agg_t[:, m, bass.ds(g * WIDE, WIDE)], ph[u][m][:, 0:WIDE], ACT.Relu,
                                         bias=b_rel[:, m:m + 1]).then_inc(relued, 1)
            pairs(act, WIDES, body)
            act.wait_ge(small, 1)
            nc.scalar.activation(sd[:], mv[:, :, 1], ACT.Sqrt, bias=eps[:, 0:1]).then_inc(root, 1)

        @block.vector
        def _(dve):
            for g in range(WIDES):
                n = min(WIDE, NODES - g * WIDE)
                dve.wait_ge(relued, g * 2 + 2)
                for m in range(KD):
                    last = nc.vector.bn_stats(st[:, m, g], agg_t[:, m, g * WIDE:g * WIDE + n])
            last.then_inc(stats, 1)
            dve.wait_ge(stats, 1)
            for m in range(KD):
                last = nc.vector.bn_aggr(mv[:, m], st[:, m].rearrange("p g s -> p (g s)"))
            last.then_inc(small, 1)
            dve.wait_ge(root, 1)
            nc.vector.reciprocal(rs[:], sd[:]).then_inc(small, 1)
            dve.wait_ge(small, 2)
            nc.vector.tensor_tensor(scale[:], rs[:], gamma[:], ALU.mult).then_inc(small, 1)
            dve.wait_ge(small, 3)
            nc.vector.tensor_tensor(tmp[:], mv[:, :, 0], scale[:], ALU.mult).then_inc(small, 1)
            dve.wait_ge(small, 4)
            nc.vector.tensor_tensor(shift[:], beta[:], tmp[:], ALU.subtract).then_inc(small, 1)
            dve.wait_ge(small, 5)
            for m in range(KD):
                nc.vector.tensor_scalar(agg_t[:, m], agg_t[:, m], scale[:, m:m + 1], shift[:, m:m + 1],
                                        ALU.mult, ALU.add)


@phase
def add_block_output(c, name, x_in, z_t, xn, w, ident, x_out, beside=None):
    nc = c.nc
    with ExitStack() as ctx:
        x = c.sb(ctx, name + "_x", [P, 2, D], FP32)
        n_rows = c.sb(ctx, name + "_n", [P, 2, D], FP32)
        n_t = c.sb(ctx, name + "_nt", [P, 2, KD, P], FP32)
        z = c.sb(ctx, name + "_z", [P, 2, KD, P], FP32)
        y = c.sb(ctx, name + "_y", [P, 2, D], FP32)
        pt = [c.ps(ctx, f"{name}_pt{u}", [P, KD, P]) for u in range(2)]
        po = [c.ps(ctx, f"{name}_po{u}", [P, 512]) for u in range(2)]
        loaded = [c.sem(f"{name}_loaded{u}") for u in range(2)]
        stored = [c.sem(f"{name}_stored{u}") for u in range(2)]
        turned = c.sem(name + "_turned")
        copied = c.sem(name + "_copied")
        staged = c.sem(name + "_staged")
        multiplied = c.sem(name + "_multiplied")
        added = c.sem(name + "_added")
        passed = c.sem(name + "_passed")
        block = ctx.enter_context(nc.Block())
        if beside is not None:
            beside(block)

        @block.sync
        def _(sp):
            def body(t, u):
                if not (static(t) and t < 2):
                    sp.wait_ge(added, t - 1)
                sp.dma_start(x[:, u], x_in[bass.ds(t * P, P), :]).then_inc(loaded[u], 16)
                sp.dma_start(n_rows[:, u], xn[bass.ds(t * P, P), :]).then_inc(loaded[u], 16)
            pairs(sp, TILES, body)

        @block.scalar
        def _(act):
            def body(t, u):
                act.wait_ge(turned, t + 1)
                if not (static(t) and t < 2):
                    act.wait_ge(multiplied, t - 1)
                nc.scalar.activation(n_t[:, u], pt[u][:], ACT.Copy).then_inc(copied, 1)
                act.wait_ge(added, t + 1)
                act.sem_inc(passed, 1)
                act.dma_start(x_out[bass.ds(t * P, P), :], y[:, u]).then_inc(stored[u], 16)
            pairs(act, TILES, body)
            act.wait_ge(stored[0], 16 * ((TILES + 1) // 2))
            act.wait_ge(stored[1], 16 * (TILES // 2))

        @block.vector
        def _(dve):
            def body(t, u):
                if not (static(t) and t < 2):
                    dve.wait_ge(multiplied, t - 1)
                    dve.sem_inc(passed, 1)
                nc.vector.tensor_copy(z[:, u], z_t[:, :, bass.ds(t * P, P)]).then_inc(staged, 1)
                dve.wait_ge(loaded[u], (t // 2) * 32 + 32)
                dve.wait_ge(multiplied, t + 1)
                if not (static(t) and t < 2):
                    dve.wait_ge(stored[u], (t // 2) * 16)
                nc.vector.tensor_tensor(y[:, u], x[:, u], po[u][:, 0:D], ALU.add).then_inc(added, 1)
            pairs(dve, TILES, body)

        @block.tensor
        def _(pe):
            def body(t, u):
                pe.wait_ge(loaded[u], (t // 2) * 32 + 32)
                if not (static(t) and t < 2):
                    pe.wait_ge(copied, t - 1)
                for k in range(KD):
                    last = nc.tensor.transpose(pt[u][:, k], n_rows[:, u, k * P:(k + 1) * P], ident[:])
                last.then_inc(turned, 1)
                pe.wait_ge(copied, t + 1)
                pe.wait_ge(staged, t + 1)
                if not (static(t) and t < 2):
                    pe.wait_ge(added, t - 1)
                for k in range(KD):
                    nc.tensor.matmul(po[u][:, 0:D], n_t[:, u, k], w[:, k], start=k == 0, stop=False)
                for k in range(KD):
                    last = nc.tensor.matmul(po[u][:, k * P:(k + 1) * P], z[:, u, k], ident[:], start=False,
                                            stop=k == KD - 1)
                last.then_inc(multiplied, 1)
            pairs(pe, TILES, body)


class RecordScatter:

    def __init__(self, c, ctx, posrec, rec1):
        self.c, self.posrec, self.rec1 = c, posrec, rec1
        self.stage = c.sb(ctx, "sr_stage", [P, 2, UNROLL, 1 + REC1], I32)
        self.at = 0

    def part(self, block, name, groups):
        c, stage, first = self.c, self.stage, self.at
        groups = min(groups, COLS // UNROLL - first)
        if groups < 1:
            return
        self.at += groups
        staged = c.sem(name + "_sr_staged")
        gone = [c.sem(f"{name}_sr_gone{u}") for u in range(2)]
        passed = c.sem(name + "_sr_passed")

        @block.gpsimd
        def _(pool):
            def body(g, u):
                if not (static(g) and g < 2):
                    pool.wait_ge(gone[u], (g // 2) * (16 * UNROLL))
                    pool.sem_inc(passed, 1)
                pool.tensor_copy(stage[:, u], self.posrec[:, bass.ds((g + first) * UNROLL, UNROLL)]).then_inc(staged, 1)
                pool.wait_ge(staged, g + 1)
                pool.sem_inc(passed, 1)
                for j in range(UNROLL):
                    pool.indirect_dma_start(
                        out=self.rec1, out_offset=bass.IndirectOffsetOnAxis(ap=stage[:, u, j, 0:1], axis=0),
                        in_=stage[:, u, j, 1:1 + REC1], in_offset=None,
                    ).then_inc(gone[u], 16)
            if groups == 1:
                body(0, 0)
            else:
                pairs(pool, groups, body)
                pool.wait_ge(gone[1], 16 * UNROLL * (groups // 2))
            pool.wait_ge(gone[0], 16 * UNROLL * ((groups + 1) // 2))


@phase
def degrees(c, posrec, dinv, dinv_row, ident, consts):
    nc = c.nc
    with ExitStack() as ctx:
        hi_ids = c.sb(ctx, "dg_hi_ids", [P, TILES], FP32)
        lo_ids = c.sb(ctx, "dg_lo_ids", [P, P], FP32)
        s_i = c.sb(ctx, "dg_si", [P, COLS], I32)
        hl_i = c.sb(ctx, "dg_hli", [P, 2, COLS], I32)
        hl = c.sb(ctx, "dg_hl", [P, 2, COLS], FP32)
        lo = c.sb(ctx, "dg_lo", [P, 2, UNROLL, P], FP32)
        hi = c.sb(ctx, "dg_hi", [P, 2, UNROLL, TILES], FP32)
        hw = c.sb(ctx, "dg_hw", [P, 2, UNROLL, TILES], FP32)
        deg = c.sb(ctx, "dg_deg", [P, 2, TILES], FP32)
        sd = c.sb(ctx, "dg_sd", [P, TILES], FP32)
        pos = c.sb(ctx, "dg_pos", [P, TILES], FP32)
        inv = c.sb(ctx, "dg_inv", [P, TILES], FP32)
        turned = c.sb(ctx, "dg_turned", [TILES, P], FP32)
        pd = c.ps(ctx, "dg_pd", [P, 512])
        pt = c.ps(ctx, "dg_pt", [P, 512])
        ids_set = c.sem("dg_ids_set")
        split = c.sem("dg_split")
        made = c.sem("dg_made")
        weighted = c.sem("dg_weighted")
        multiplied = c.sem("dg_multiplied")
        small = c.sem("dg_small")
        root = c.sem("dg_root")
        stored = c.sem("dg_stored")
        block = ctx.enter_context(nc.Block())
        ew = posrec[:, :, 3].bitcast(FP32)

        @block.vector
        def _(dve):
            nc.vector.tensor_copy(s_i[:], posrec[:, :, 1].bitcast(FP32)).then_inc(split, 1)
            nc.vector.tensor_copy(lo_ids[:], consts["node_ids"][:, 0:P])
            nc.vector.tensor_copy(hi_ids[:], consts["node_ids"][:, 0:TILES])
            dve.wait_ge(split, 1)
            nc.vector.tensor_scalar(hl_i[:, 0], s_i[:], 7, None, ALU.arith_shift_right)
            nc.vector.tensor_scalar(hl_i[:, 1], s_i[:], P - 1, None, ALU.bitwise_and).then_inc(split, 1)
            dve.wait_ge(split, 2)
            nc.vector.tensor_copy(hl[:], hl_i[:]).then_inc(split, 1)
            dve.wait_ge(split, 3)

            def body(g, u):
                if not (static(g) and g < 2):
                    dve.wait_ge(multiplied, g - 1)
                j = bass.ds(g * UNROLL, UNROLL)
                nc.vector.tensor_tensor(lo[:, u], lo_ids[:].unsqueeze(1).broadcast_to([P, UNROLL, P]),
                                        hl[:, 1, j].unsqueeze(2).broadcast_to([P, UNROLL, P]), ALU.is_equal)
                nc.vector.tensor_tensor(hi[:, u], hi_ids[:].unsqueeze(1).broadcast_to([P, UNROLL, TILES]),
                                        hl[:, 0, j].unsqueeze(2).broadcast_to([P, UNROLL, TILES]), ALU.is_equal).then_inc(made, 1)
                dve.wait_ge(made, g + 1)
                nc.vector.tensor_tensor(hw[:, u], hi[:, u], ew[:, j].unsqueeze(2).broadcast_to([P, UNROLL, TILES]),
                                        ALU.mult).then_inc(weighted, 1)
            pairs(dve, COLS // UNROLL, body)
            dve.wait_ge(multiplied, COLS // UNROLL)
            nc.vector.tensor_scalar(deg[:, 0], pd[:, 0:TILES], 1.0, None, ALU.add).then_inc(small, 1)
            dve.wait_ge(small, 1)
            nc.vector.tensor_scalar(deg[:, 1], deg[:, 0], 1e-30, None, ALU.max).then_inc(small, 1)
            nc.vector.tensor_scalar(pos[:], deg[:, 0], 0.0, None, ALU.is_gt)
            dve.wait_ge(root, 1)
            nc.vector.reciprocal(inv[:], sd[:]).then_inc(small, 1)
            dve.wait_ge(small, 3)
            nc.vector.tensor_tensor(dinv[:], inv[:], pos[:], ALU.mult).then_inc(small, 1)
            dve.wait_ge(multiplied, COLS // UNROLL + 1)
            nc.vector.tensor_copy(turned[:], pt[0:TILES, 0:P]).then_inc(small, 1)

        @block.scalar
        def _(act):
            act.wait_ge(small, 2)
            nc.scalar.activation(sd[:], deg[:, 1], ACT.Sqrt).then_inc(root, 1)
            act.wait_ge(small, 5)
            act.dma_start(dinv_row.rearrange("(t p) -> t p", p=P), turned[:]).then_inc(stored, 16)
            act.wait_ge(stored, 16)

        @block.tensor
        def _(pe):
            def body(g, u):
                pe.wait_ge(weighted, g + 1)
                for j in range(UNROLL):
                    last = nc.tensor.matmul(pd[:, 0:TILES], lo[:, u, j], hw[:, u, j],
                                            start=static(g) and g == 0 and j == 0, stop=False, skip_group_check=True)
                last.then_inc(multiplied, 1)
            pairs(pe, COLS // UNROLL, body)
            pe.wait_ge(small, 4)
            nc.tensor.transpose(pt[0:TILES, 0:P], dinv[:], ident[:]).then_inc(multiplied, 1)


@phase
def second_dense(c, agg_t, y_t, dinv_b, w, b, w1, b1):
    nc = c.nc
    with ExitStack() as ctx:
        ph = [[c.ps(ctx, f"sd_ph{s}{m}", [P, 512]) for m in range(KD)] for s in range(2)]
        h7 = c.sb(ctx, "sd_h7", [P, KD, WIDE], FP32)
        summed = c.sem("sd_summed")
        scaled = c.sem("sd_scaled")
        first = c.sem("sd_first")
        second = c.sem("sd_second")
        h7_done = c.sem("sd_h7_done")
        out_done = c.sem("sd_out_done")
        passed = c.sem("sd_passed")
        block = ctx.enter_context(nc.Block())

        @block.vector
        def _(dve):
            def body(g, u):
                n = bass.ds(g * WIDE, WIDE)
                nc.vector.tensor_tensor(agg_t[:, :, n], agg_t[:, :, n], y_t[:, :, n], ALU.add).then_inc(summed, 1)
                dve.wait_ge(summed, g + 1)
                nc.vector.tensor_tensor(agg_t[:, :, n], agg_t[:, :, n],
                                        dinv_b[:, n].unsqueeze(1).broadcast_to([P, KD, WIDE]), ALU.mult).then_inc(scaled, 1)
            pairs(dve, WIDES, body)

        @block.tensor
        def _(pe):
            def body(g, u):
                pe.wait_ge(scaled, g + 1)
                if not (static(g) and g < 1):
                    pe.wait_ge(h7_done, g * 2)
                for m in range(KD):
                    for k in range(KD):
                        last = nc.tensor.matmul(ph[0][m][:, 0:WIDE], w[:, k, m * P:(m + 1) * P],
                                                agg_t[:, k, bass.ds(g * WIDE, WIDE)], start=k == 0, stop=k == KD - 1)
                last.then_inc(first, 1)
                pe.wait_ge(h7_done, g * 2 + 2)
                if not (static(g) and g < 1):
                    pe.wait_ge(out_done, g * 2)
                for m in range(KD):
                    for k in range(KD):
                        last = nc.tensor.matmul(ph[1][m][:, 0:WIDE], w1[:, k, m * P:(m + 1) * P], h7[:, k],
                                                start=k == 0, stop=k == KD - 1)
                last.then_inc(second, 1)
            pairs(pe, WIDES, body)

        @block.scalar
        def _(act):
            def body(g, u):
                act.wait_ge(first, g + 1)
                if not (static(g) and g < 1):
                    act.wait_ge(second, g)
                for m in range(KD):
                    nc.scalar.activation(h7[:, m], ph[0][m][:, 0:WIDE], ACT.Identity, bias=b[:, m:m + 1]).then_inc(h7_done, 1)
                act.wait_ge(second, g + 1)
                act.sem_inc(passed, 1)
                for m in range(KD):
                    nc.scalar.activation(agg_t[:, m, bass.ds(g * WIDE, WIDE)], ph[1][m][:, 0:WIDE], ACT.Relu,
                                         bias=b1[:, m:m + 1]).then_inc(out_done, 1)
            pairs(act, WIDES, body)


@phase
def add_projection(c, name, x_in, z_t, w, b_row, x_out):
    nc = c.nc
    with ExitStack() as ctx:
        x = c.sb(ctx, name + "_x", [P, 2, D], FP32)
        z = c.sb(ctx, name + "_z", [P, 2, KD, P], FP32)
        s = c.sb(ctx, name + "_s", [P, 2, D], FP32)
        y = c.sb(ctx, name + "_y", [P, 2, D], FP32)
        po = [c.ps(ctx, f"{name}_po{u}", [P, 512]) for u in range(2)]
        loaded = [c.sem(f"{name}_loaded{u}") for u in range(2)]
        stored = [c.sem(f"{name}_stored{u}") for u in range(2)]
        staged = c.sem(name + "_staged")
        multiplied = c.sem(name + "_multiplied")
        biased = c.sem(name + "_biased")
        added = c.sem(name + "_added")
        passed = c.sem(name + "_passed")
        block = ctx.enter_context(nc.Block())

        @block.sync
        def _(sp):
            def body(t, u):
                if not (static(t) and t < 2):
                    sp.wait_ge(added, t - 1)
                sp.dma_start(x[:, u], x_in[bass.ds(t * P, P), :]).then_inc(loaded[u], 16)
            pairs(sp, TILES, body)

        @block.scalar
        def _(act):
            def body(t, u):
                act.wait_ge(added, t + 1)
                act.sem_inc(passed, 1)
                act.dma_start(x_out[bass.ds(t * P, P), :], y[:, u]).then_inc(stored[u], 16)
            pairs(act, TILES, body)
            act.wait_ge(stored[0], 16 * ((TILES + 1) // 2))
            act.wait_ge(stored[1], 16 * (TILES // 2))

        @block.vector
        def _(dve):
            def body(t, u):
                if not (static(t) and t < 2):
                    dve.wait_ge(multiplied, t - 1)
                    dve.sem_inc(passed, 1)
                nc.vector.tensor_copy(z[:, u], z_t[:, :, bass.ds(t * P, P)]).then_inc(staged, 1)
                dve.wait_ge(loaded[u], (t // 2) * 16 + 16)
                if not (static(t) and t < 2):
                    dve.wait_ge(added, t - 1)
                nc.vector.tensor_tensor(s[:, u], x[:, u], b_row[:], ALU.add).then_inc(biased, 1)
                dve.wait_ge(biased, t + 1)
                dve.wait_ge(multiplied, t + 1)
                if not (static(t) and t < 2):
                    dve.wait_ge(stored[u], (t // 2) * 16)
                nc.vector.tensor_tensor(y[:, u], s[:, u], po[u][:, 0:D], ALU.add).then_inc(added, 1)
            pairs(dve, TILES, body)

        @block.tensor
        def _(pe):
            def body(t, u):
                pe.wait_ge(staged, t + 1)
                if not (static(t) and t < 2):
                    pe.wait_ge(added, t - 1)
                for k in range(KD):
                    last = nc.tensor.matmul(po[u][:, 0:D], z[:, u, k], w[:, k], start=k == 0, stop=k == KD - 1)
                last.then_inc(multiplied, 1)
            pairs(pe, TILES, body)


@phase
def gate_scores(c, name, xn, scores, ident, wg, bg_row, w1=None, b1=None, beside=None):
    nc = c.nc
    km = KD if w1 is None else HID1 // P
    with ExitStack() as ctx:
        x = c.sb(ctx, name + "_x", [P, 2, D], FP32)
        x_t = c.sb(ctx, name + "_xt", [P, 2, KD, P], FP32)
        pt = [c.ps(ctx, f"{name}_pt{u}", [P, KD, P]) for u in range(2)]
        pg = [c.ps(ctx, f"{name}_pg{u}", [P, 512]) for u in range(2)]
        if w1 is not None:
            h_t = c.sb(ctx, name + "_ht", [P, 2, km, P], FP32)
            ph = [c.ps(ctx, f"{name}_ph{n}", [P, 4, P]) for n in range(4)]
            hidden = c.sem(name + "_hidden")
            active = c.sem(name + "_active")
        loaded = [c.sem(f"{name}_loaded{u}") for u in range(2)]
        turned = c.sem(name + "_turned")
        copied = c.sem(name + "_copied")
        gated = c.sem(name + "_gated")
        kept = c.sem(name + "_kept")
        block = ctx.enter_context(nc.Block())
        if beside is not None:
            beside(block)

        @block.sync
        def _(sp):
            def body(t, u):
                if not (static(t) and t < 2):
                    sp.wait_ge(turned, t - 1)
                sp.dma_start(x[:, u], xn[bass.ds(t * P, P), :]).then_inc(loaded[u], 16)
            pairs(sp, TILES, body)

        @block.vector
        def _(dve):
            def body(t, u):
                dve.wait_ge(turned, t + 1)
                if not (static(t) and t < 2):
                    dve.wait_ge(gated, t - 1)
                nc.vector.tensor_copy(x_t[:, u], pt[u][:]).then_inc(copied, 1)
                dve.wait_ge(gated, t + 1)
                nc.vector.tensor_tensor(scores[:, bass.ds(t, 1)].rearrange("p o e -> p (o e)"), pg[u][:, 0:EXPERTS],
                                        bg_row[:], ALU.add).then_inc(kept, 1)
            pairs(dve, TILES, body)

        if w1 is not None:
            @block.scalar
            def _(act):
                def body(t, u):
                    if not (static(t) and t < 2):
                        act.wait_ge(gated, t - 1)
                    for n in range(2):
                        act.wait_ge(hidden, t * 2 + (n + 1))
                        for m in range(4):
                            last = nc.scalar.activation(h_t[:, u, n * 4 + m], ph[u * 2 + n][:, m], ACT.Gelu,
                                                        bias=b1[:, n * 4 + m:n * 4 + m + 1])
                        last.then_inc(active, 1)
                pairs(act, TILES, body)

        @block.tensor
        def _(pe):
            def turn(t, u):
                pe.wait_ge(loaded[u], (t // 2) * 16 + 16)
                if not (static(t) and t < 2):
                    pe.wait_ge(copied, t - 1)
                for k in range(KD):
                    last = nc.tensor.transpose(pt[u][:, k], x[:, u, k * P:(k + 1) * P], ident[:])
                last.then_inc(turned, 1)

            def hide(t, u):
                pe.wait_ge(copied, t + 1)
                for n in range(2):
                    if not (static(t) and t < 2):
                        pe.wait_ge(active, t * 2 + (n - 3))
                    for m in range(n * 4, n * 4 + 4):
                        for k in range(KD):
                            last = nc.tensor.matmul(ph[u * 2 + n][:, m % 4], w1[:, k, m * P:(m + 1) * P], x_t[:, u, k],
                                                    start=k == 0, stop=k == KD - 1)
                    last.then_inc(hidden, 1)

            def gate(t, u):
                if w1 is None:
                    pe.wait_ge(copied, t + 1)
                    z = x_t
                else:
                    pe.wait_ge(active, t * 2 + 2)
                    z = h_t
                if not (static(t) and t < 2):
                    pe.wait_ge(kept, t - 1)
                for k in range(km):
                    last = nc.tensor.matmul(pg[u][:, 0:EXPERTS], z[:, u, k], wg[:, k], start=k == 0, stop=k == km - 1)
                last.then_inc(gated, 1)

            def body(t, u):
                turn(t, u)
                if w1 is not None:
                    hide(t, u)
                gate(t, u)
            pairs(pe, TILES, body)


@phase
def choose(c, name, scores, top, chunks, consts, place, expert, prob=None):
    nc = c.nc
    E = EXPERTS
    with ExitStack() as ctx:
        s = scores
        won = c.sb(ctx, name + "_won", [P, E, TILES, E], FP32)
        order = c.sb(ctx, name + "_order", [P, TILES, E], FP32)
        mask = c.sb(ctx, name + "_mask", [P, TILES, E], FP32)
        tot = c.sb(ctx, name + "_tot", [P, TILES, E], FP32)
        upto = c.sb(ctx, name + "_upto", [P, E, TILES], FP32)
        row = c.sb(ctx, name + "_row", [P, 4, TILES, E], FP32)
        unit = c.sb(ctx, name + "_unit", [P, TILES], FP32)
        n_i = c.sb(ctx, name + "_ni", [P, 2, E], I32)
        n_f = c.sb(ctx, name + "_nf", [P, 4, E], FP32)
        ge = c.sb(ctx, name + "_ge", [1, E, chunks], FP32)
        ex = c.sb(ctx, name + "_ex", [1, 2, chunks], FP32)
        pick = c.sb(ctx, name + "_pick", [P, 3, TILES], FP32)
        probs = c.sb(ctx, name + "_probs", [P, 4, TILES, E], FP32)
        pk = c.ps(ctx, name + "_pk", [P, 512])
        pn = c.ps(ctx, name + "_pn", [P, 512])
        done = c.sem(name + "_done")
        counted = c.sem(name + "_counted")
        raised = c.sem(name + "_raised")
        block = ctx.enter_context(nc.Block())

        @block.scalar
        def _(act):
            if prob is not None:
                act.wait_ge(done, 2)
                nc.scalar.activation(probs[:, 1], probs[:, 0], ACT.Exp).then_inc(raised, 1)

        @block.vector
        def _(dve):
            n = [0]

            def then(ins):
                n[0] += 1
                ins.then_inc(done, 1)
                dve.wait_ge(done, n[0])

            if prob is not None:
                then(nc.vector.tensor_reduce(pick[:, 0], s[:], AX.X, ALU.max))
                then(nc.vector.tensor_tensor(probs[:, 0], s[:], pick[:, 0].unsqueeze(2).broadcast_to([P, TILES, E]), ALU.subtract))
                dve.wait_ge(raised, 1)
                then(nc.vector.reduce_sum(pick[:, 1], probs[:, 1], AX.X))
                then(nc.vector.reciprocal(pick[:, 2], pick[:, 1]))
                then(nc.vector.tensor_tensor(probs[:, 2], probs[:, 1], pick[:, 2].unsqueeze(2).broadcast_to([P, TILES, E]), ALU.mult))
                by = probs[:, 2]
            else:
                by = s[:]
            then(nc.vector.memset(won[:], 0.0))
            for j in range(E):
                if j + 1 < E:
                    nc.vector.tensor_tensor(won[:, j, :, j + 1:E], by[:, :, j:j + 1].broadcast_to([P, TILES, E - 1 - j]),
                                            by[:, :, j + 1:E], ALU.is_ge)
                if j:
                    nc.vector.tensor_tensor(won[:, j, :, 0:j], by[:, :, j:j + 1].broadcast_to([P, TILES, j]),
                                            by[:, :, 0:j], ALU.is_gt)
            then(nc.vector.memset(unit[:], 1.0))
            then(nc.vector.reduce_sum(order[:], won[:].rearrange("p j t e -> p t e j"), AX.X))
            then(nc.vector.tensor_scalar(mask[:], order[:], float(top), None, ALU.is_lt))
            if prob is not None:
                then(nc.vector.tensor_tensor(probs[:, 3], probs[:, 2], mask[:], ALU.mult))
                then(nc.vector.reduce_sum(prob[:], probs[:, 3], AX.X))
            dve.wait_ge(counted, 1)
            then(nc.vector.tensor_copy(tot[:], pn[:, 0:TILES * E].rearrange("p (t e) -> p t e", e=E)))
            for e in range(E):
                last = nc.vector.tensor_tensor_scan(upto[:, e], unit[:], tot[:, :, e], 0.0, ALU.mult, ALU.add)
            then(last)
            then(nc.vector.tensor_scalar(n_i[:, 0], upto[:, :, TILES - 1], float(P - 1), None, ALU.add))
            then(nc.vector.tensor_scalar(n_i[:, 1], n_i[:, 0], 7, None, ALU.arith_shift_right))
            then(nc.vector.tensor_copy(n_f[:, 0], n_i[:, 1]))
            then(nc.vector.tensor_tensor_scan(n_f[:, 1], unit[:, 0:E], n_f[:, 0], 0.0, ALU.mult, ALU.add))
            then(nc.vector.tensor_tensor(n_f[:, 2], n_f[:, 1], n_f[:, 0], ALU.subtract))
            then(nc.vector.tensor_scalar(n_f[:, 3], n_f[:, 2], float(P), None, ALU.mult))
            then(nc.vector.tensor_tensor(row[:, 0], upto[:].rearrange("p e t -> p t e"), tot[:], ALU.subtract))
            then(nc.vector.tensor_tensor(row[:, 1], row[:, 0], n_f[:, 3].unsqueeze(1).broadcast_to([P, TILES, E]), ALU.add))
            then(nc.vector.tensor_tensor(row[:, 2], row[:, 1], pk[:, 0:TILES * E].rearrange("p (t e) -> p t e", e=E), ALU.add))
            then(nc.vector.tensor_tensor(row[:, 3], row[:, 2], mask[:], ALU.mult))
            then(nc.vector.tensor_reduce(won[:, 0, :, 0], row[:, 3], AX.X, ALU.max))
            if top == 1:
                then(nc.vector.tensor_copy(place[:, :, 0], won[:, 0, :, 0]))
            else:
                then(nc.vector.reduce_sum(won[:, 1, :, 0], row[:, 3], AX.X))
                nc.vector.tensor_copy(place[:, :, 1], won[:, 0, :, 0])
                then(nc.vector.tensor_tensor(place[:, :, 0], won[:, 1, :, 0], won[:, 0, :, 0], ALU.subtract))
            for e in range(E):
                last = nc.vector.tensor_scalar(ge[:, e], consts["node_ids"][0:1, 0:chunks], n_f[0:1, 2, e:e + 1], None, ALU.is_ge)
            then(last)
            then(nc.vector.reduce_sum(ex[:, 0], ge[:].rearrange("p e c -> p c e"), AX.X))
            then(nc.vector.tensor_scalar(expert[:], ex[:, 0], -1.0, None, ALU.add))

        @block.tensor
        def _(pe):
            pe.wait_ge(done, (6 if prob is not None else 1) + 3)
            m = mask[:].rearrange("p t e -> p (t e)")
            nc.tensor.matmul(pk[:, 0:TILES * E], consts["earlier"][:], m, start=True, stop=True)
            nc.tensor.matmul(pn[:, 0:TILES * E], consts["ones"][:], m, start=True, stop=True).then_inc(counted, 1)


@phase
def dispatch(c, name, xn, place, top, xs):
    nc = c.nc
    with ExitStack() as ctx:
        x = c.sb(ctx, name + "_x", [P, 2, GROUP, D], FP32)
        at = c.sb(ctx, name + "_at", [P, 2, GROUP, top], I32)
        loaded = [c.sem(f"{name}_loaded{u}") for u in range(2)]
        gone = [c.sem(f"{name}_gone{u}") for u in range(2)]
        staged = c.sem(name + "_staged")
        passed = c.sem(name + "_passed")
        block = ctx.enter_context(nc.Block())
        per = 16 * GROUP * top

        @block.sync
        def _(sp):
            def body(g, u):
                if not (static(g) and g < 2):
                    sp.wait_ge(gone[u], (g // 2) * per)
                sp.dma_start(x[:, u], tiles_view(xn)[bass.ds(g, 1)].rearrange("o p a d -> p (o a) d")).then_inc(loaded[u], 16)
            pairs(sp, GROUPS, body)

        @block.vector
        def _(dve):
            def body(g, u):
                if not (static(g) and g < 2):
                    dve.wait_ge(gone[u], (g // 2) * per)
                    dve.sem_inc(passed, 1)
                nc.vector.tensor_copy(at[:, u], place[:, bass.ds(g * GROUP, GROUP)]).then_inc(staged, 1)
            pairs(dve, GROUPS, body)

        @block.gpsimd
        def _(pool):
            def body(g, u):
                pool.wait_ge(loaded[u], (g // 2) * 16 + 16)
                pool.sem_inc(passed, 1)
                pool.wait_ge(staged, g + 1)
                pool.sem_inc(passed, 1)
                for t in range(GROUP):
                    for k in range(top):
                        pool.indirect_dma_start(
                            out=xs, out_offset=bass.IndirectOffsetOnAxis(ap=at[:, u, t, k:k + 1], axis=0),
                            in_=x[:, u, t], in_offset=None).then_inc(gone[u], 16)
            pairs(pool, GROUPS, body)
            pool.wait_ge(gone[0], per * ((GROUPS + 1) // 2))
            pool.wait_ge(gone[1], per * (GROUPS // 2))


@phase
def experts(c, name, xs, ys, chunks, expert, ident, hid, w1, b1, w2, b2, first_shared, beside=None):
    nc = c.nc
    nh = hid // 512
    kh = hid // P
    with ExitStack() as ctx:
        x = c.sb(ctx, name + "_x", [P, 2, D], FP32)
        x_t = c.sb(ctx, name + "_xt", [P, 2, KD, P], FP32)
        pre = c.sb(ctx, name + "_pre", [P, 2, hid], FP32)
        h = c.sb(ctx, name + "_h", [P, 2, hid], FP32)
        h_t = c.sb(ctx, name + "_ht", [P, 2, kh, P], FP32)
        y = c.sb(ctx, name + "_y", [P, 2, D], FP32)
        px = c.ps(ctx, name + "_px", [P, KD, P])
        ph = [c.ps(ctx, f"{name}_ph{u}", [P, 512]) for u in range(2)]
        pt = [c.ps(ctx, f"{name}_pt{u}", [P, 4, P]) for u in range(2)]
        po = [c.ps(ctx, f"{name}_po{u}", [P, 512]) for u in range(2)]
        loaded = [c.sem(f"{name}_loaded{u}") for u in range(2)]
        stored = [c.sem(f"{name}_stored{u}") for u in range(2)]
        x_turned = c.sem(name + "_x_turned")
        x_copied = c.sem(name + "_x_copied")
        up = c.sem(name + "_up")
        biased = c.sem(name + "_biased")
        active = c.sem(name + "_active")
        h_turned = c.sem(name + "_h_turned")
        h_copied = c.sem(name + "_h_copied")
        down = c.sem(name + "_down")
        out_done = c.sem(name + "_out_done")
        passed = c.sem(name + "_passed")
        block = ctx.enter_context(nc.Block())
        if beside is not None:
            beside(block)

        def stages(eng, body):
            for s in range(4):
                body(s, s % 2)
            with eng.Fori(2, chunks // 2) as i:
                body(i * 2, 0)
                body(i * 2 + 1, 1)
            for s in range(chunks, chunks + 3):
                body(s, s % 2)

        def runs(n):
            return not static(n) or 0 <= n < chunks

        def reused(n, by=2):
            return not (static(n) and n < by)

        def number(eng, n):
            return eng.value_load(expert[0:1, bass.ds(n, 1)], min_val=0, max_val=EXPERTS - 1)

        @block.sync
        def _(sp):
            def body(n, u):
                if reused(n):
                    sp.wait_ge(x_turned, n - 1)
                sp.dma_start(x[:, u], xs[bass.ds(n * P, P), :]).then_inc(loaded[u], 16)
            pairs(sp, chunks, body)

        @block.tensor
        def _(pe):
            def body(s, u):
                if runs(s):
                    pe.wait_ge(loaded[u], (s // 2) * 16 + 16)
                    if reused(s, 1):
                        pe.wait_ge(x_copied, s)
                    for k in range(KD):
                        last = nc.tensor.transpose(px[:, k], x[:, u, k * P:(k + 1) * P], ident[:])
                    last.then_inc(x_turned, 1)
                n, v = s - 1, 1 - u
                if runs(n):
                    pe.wait_ge(x_copied, n + 1)
                    e = 0 if first_shared else number(pe, n)
                    for b in range(nh):
                        q = (n * nh + b) % 2 if nh == 1 else b
                        if nh == 1:
                            q = v
                        if reused(n, 2 if nh == 1 else 1):
                            pe.wait_ge(biased, n * nh + (b - 1))
                        for k in range(KD):
                            cols = slice(b * 512, b * 512 + 512)
                            w = w1[:, 0, k, cols] if first_shared else w1[:, bass.ds(e, 1), k, cols].rearrange("p o n -> p (o n)")
                            last = nc.tensor.matmul(ph[q][:], x_t[:, v, k], w, start=k == 0, stop=k == KD - 1)
                        last.then_inc(up, 1)
                n, v = s - 2, u
                if runs(n):
                    pe.wait_ge(active, n + 1)
                    for b in range(nh):
                        q = v if nh == 1 else b
                        if reused(n, 2 if nh == 1 else 1):
                            pe.wait_ge(h_copied, n * nh + (b - 1))
                        for m in range(4):
                            last = nc.tensor.transpose(pt[q][:, m], h[:, v, (b * 4 + m) * P:(b * 4 + m + 1) * P], ident[:])
                        last.then_inc(h_turned, 1)
                n, v = s - 3, 1 - u
                if runs(n):
                    e = number(pe, n)
                    pe.wait_ge(h_copied, n * nh + nh)
                    if reused(n):
                        pe.wait_ge(out_done, n - 1)
                    for m in range(kh):
                        last = nc.tensor.matmul(po[v][:, 0:D], h_t[:, v, m],
                                                w2[:, bass.ds(e, 1), m].rearrange("p o n -> p (o n)"),
                                                start=m == 0, stop=m == kh - 1)
                    last.then_inc(down, 1)
            stages(pe, body)

        @block.scalar
        def _(act):
            def body(s, u):
                if runs(s):
                    act.wait_ge(x_turned, s + 1)
                    if reused(s):
                        act.wait_ge(up, (s - 1) * nh)
                    nc.scalar.activation(x_t[:, u], px[:], ACT.Copy).then_inc(x_copied, 1)
                n, v = s - 1, 1 - u
                if runs(n):
                    act.wait_ge(biased, n * nh + nh)
                    if reused(n):
                        act.wait_ge(h_turned, (n - 1) * nh)
                    nc.scalar.activation(h[:, v], pre[:, v], ACT.Gelu).then_inc(active, 1)
                n, v = s - 3, 1 - u
                if runs(n):
                    act.wait_ge(out_done, n + 1)
                    act.sem_inc(passed, 1)
                    act.dma_start(ys[bass.ds(n * P, P), :], y[:, v]).then_inc(stored[v], 16)
            stages(act, body)
            for v in range(2):
                act.wait_ge(stored[v], 16 * (chunks // 2))

        @block.vector
        def _(dve):
            def body(s, u):
                n, v = s - 1, 1 - u
                if runs(n):
                    e = 0 if first_shared else number(dve, n)
                    for b in range(nh):
                        q = v if nh == 1 else b
                        dve.wait_ge(up, n * nh + (b + 1))
                        if reused(n) and b == 0:
                            dve.wait_ge(active, n - 1)
                        cols = slice(b * 512, b * 512 + 512)
                        bias = b1[:, 0, cols] if first_shared else b1[:, bass.ds(e, 1), cols].rearrange("p o n -> p (o n)")
                        nc.vector.tensor_tensor(pre[:, v, cols], ph[q][:], bias, ALU.add).then_inc(biased, 1)
                n, v = s - 2, u
                if runs(n):
                    for b in range(nh):
                        q = v if nh == 1 else b
                        dve.wait_ge(h_turned, n * nh + (b + 1))
                        if reused(n) and b == 0:
                            dve.wait_ge(down, n - 1)
                        nc.vector.tensor_copy(h_t[:, v, b * 4:b * 4 + 4], pt[q][:]).then_inc(h_copied, 1)
                n, v = s - 3, 1 - u
                if runs(n):
                    e = number(dve, n)
                    dve.wait_ge(down, n + 1)
                    if reused(n):
                        dve.wait_ge(stored[v], (n // 2) * 16)
                    nc.vector.tensor_tensor(y[:, v], po[v][:, 0:D], b2[:, bass.ds(e, 1)].rearrange("p o n -> p (o n)"),
                                            ALU.add).then_inc(out_done, 1)
            stages(dve, body)


@phase
def combine(c, name, x_in, ys, place, top, x_out, prob=None):
    nc = c.nc
    with ExitStack() as ctx:
        x = c.sb(ctx, name + "_x", [P, 2, GROUP, D], FP32)
        r = c.sb(ctx, name + "_r", [P, 2, top, GROUP, D], FP32)
        z = c.sb(ctx, name + "_z", [P, 2, GROUP, D], FP32)
        w = c.sb(ctx, name + "_w", [P, 2, GROUP, D], FP32)
        at = c.sb(ctx, name + "_at", [P, 2, GROUP, top], I32)
        loaded = [c.sem(f"{name}_loaded{u}") for u in range(2)]
        got = [c.sem(f"{name}_got{u}") for u in range(2)]
        stored = [c.sem(f"{name}_stored{u}") for u in range(2)]
        staged = c.sem(name + "_staged")
        partly = c.sem(name + "_partly")
        added = c.sem(name + "_added")
        passed = c.sem(name + "_passed")
        block = ctx.enter_context(nc.Block())
        per = 16 * GROUP * top

        @block.sync
        def _(sp):
            def body(g, u):
                if not (static(g) and g < 2):
                    sp.wait_ge(added, g - 1)
                sp.dma_start(x[:, u], tiles_view(x_in)[bass.ds(g, 1)].rearrange("o p a d -> p (o a) d")).then_inc(loaded[u], 16)
            pairs(sp, GROUPS, body)

        @block.gpsimd
        def _(pool):
            def body(g, u):
                pool.wait_ge(staged, g + 1)
                pool.sem_inc(passed, 1)
                if not (static(g) and g < 2):
                    pool.wait_ge(added, g - 1)
                    pool.sem_inc(passed, 1)
                for t in range(GROUP):
                    for k in range(top):
                        pool.indirect_dma_start(
                            out=r[:, u, k, t], out_offset=None, in_=ys,
                            in_offset=bass.IndirectOffsetOnAxis(ap=at[:, u, t, k:k + 1], axis=0)).then_inc(got[u], 16)
            pairs(pool, GROUPS, body)

        @block.vector
        def _(dve):
            def body(g, u):
                if not (static(g) and g < 2):
                    dve.wait_ge(got[u], (g // 2) * per)
                    dve.sem_inc(passed, 1)
                nc.vector.tensor_copy(at[:, u], place[:, bass.ds(g * GROUP, GROUP)]).then_inc(staged, 1)
                dve.wait_ge(got[u], (g // 2) * per + per)
                if not (static(g) and g < 2):
                    dve.wait_ge(added, g - 1)
                if prob is None:
                    nc.vector.tensor_tensor(w[:, u], r[:, u, 0], r[:, u, 1], ALU.add).then_inc(partly, 1)
                else:
                    nc.vector.tensor_tensor(w[:, u], r[:, u, 0],
                                            prob[:, bass.ds(g * GROUP, GROUP)].unsqueeze(2).broadcast_to([P, GROUP, D]),
                                            ALU.mult).then_inc(partly, 1)
                dve.wait_ge(partly, g + 1)
                dve.wait_ge(loaded[u], (g // 2) * 16 + 16)
                if not (static(g) and g < 2):
                    dve.wait_ge(stored[u], (g // 2) * 16)
                nc.vector.tensor_tensor(z[:, u], w[:, u], x[:, u], ALU.add).then_inc(added, 1)
            pairs(dve, GROUPS, body)

        @block.scalar
        def _(act):
            def body(g, u):
                act.wait_ge(added, g + 1)
                act.sem_inc(passed, 1)
                act.dma_start(tiles_view(x_out)[bass.ds(g, 1)].rearrange("o p a d -> p (o a) d"), z[:, u]).then_inc(stored[u], 16)
            pairs(act, GROUPS, body)
            act.wait_ge(stored[0], 16 * ((GROUPS + 1) // 2))
            act.wait_ge(stored[1], 16 * (GROUPS // 2))


@phase
def load_all(c, name, items):
    nc = c.nc
    loaded = c.sem(name + "_loaded")
    with ExitStack() as ctx:
        block = ctx.enter_context(nc.Block())

        @block.sync
        def _(sp):
            for tile, src in items:
                sp.dma_start(tile, src).then_inc(loaded, 16)
            sp.wait_ge(loaded, 16 * len(items))


def const_arrays():
    q = np.arange(P)
    half, tile = q // 64, q % 64
    f = np.float32
    return {
        "bucket": tile[:, None].astype(f),
        "fold": (tile[:, None] == q[None, :]).astype(f),
        "before": ((tile[:, None] < tile[None, :]) | ((tile[:, None] == tile[None, :]) & (half[:, None] < half[None, :]))).astype(f),
        "lower": ((q[:, None] < q[None, :]) & (q[:, None] < 64)).astype(f),
        "diff": ((q[:, None] == q[None, :]).astype(f) - (q[:, None] == q[None, :] - 1).astype(f)),
        "steps": np.arange(STEPS, dtype=f)[None, :],
        "node_ids": np.arange(SLOTS * P, dtype=f)[None, :],
        "earlier": (q[:, None] < q[None, :]).astype(f),
        "ident": np.eye(P, dtype=f),
        "halves": (half[:, None] == np.arange(HALVES)[None, :]).astype(f),
    }


def weights_view(w):
    return w.rearrange("(k p) n -> p k n", p=P)


def row_view(b, n):
    return b.rearrange("(o n) -> o n", o=1).broadcast_to([P, n])


def all_rows(b):
    e, n = b.shape
    return b.rearrange("(o e) n -> o e n", o=1).broadcast_to([P, e, n])


def program(nc, a, out):
    with ExitStack() as ctx:
        c = Core(nc, ctx)
        rows = {k: c.dram(k, [NODES_PAD, D], FP32) for k in ("xn0", "x1", "xn1", "x2", "y2", "x3", "xn3")}
        ids_src = c.dram("ids_src", [EDGES_PAD], BF16)
        ids_dst = c.dram("ids_dst", [EDGES_PAD], BF16)
        rec0 = c.dram("rec0", [EDGES_PAD, REC0], I32)
        rec1 = c.dram("rec1", [EDGES_PAD, REC1], I32)
        dinv_row = c.dram("dinv_row", [NODES_PAD], FP32)
        xs = [c.dram(f"xs{i}", [n * P, D], FP32) for i, n in enumerate((CHUNKS0, CHUNKS1))]
        ys = [c.dram(f"ys{i}", [n * P, D], FP32) for i, n in enumerate((CHUNKS0, CHUNKS1))]

        ident = c.sb(ctx, "ident", [P, P], FP32)
        eps = c.sb(ctx, "eps", [P, 1], FP32)
        ones = c.sb(ctx, "ones", [P, P], FP32)
        halves = c.sb(ctx, "halves", [P, HALVES], FP32)
        bucket = c.sb(ctx, "bucket", [P, 1], FP32)
        earlier = c.sb(ctx, "earlier", [P, P], FP32)
        node_ids = c.sb(ctx, "node_ids", [P, SLOTS * P], FP32)
        dinv = c.sb(ctx, "dinv", [P, TILES], FP32)
        base = [c.sb(ctx, f"base{i}", [P, 1], FP32) for i in range(2)]
        tab = [c.sb(ctx, f"tab{i}", [1, 2, STEPS], I32) for i in range(2)]
        scores = c.sb(ctx, "scores", [P, TILES, EXPERTS], FP32)
        consts = {"ident": ident, "ones": ones, "halves": halves, "bucket": bucket, "earlier": earlier, "node_ids": node_ids}
        set_const = c.sem("set_const")
        filled = c.sem("filled")
        with ExitStack() as ctx_c:
            for k, n in (("fold", P), ("before", P), ("lower", P), ("diff", P), ("steps", STEPS)):
                consts[k] = c.sb(ctx_c, k, [P, n], FP32)
            widths = {"steps": STEPS, "node_ids": SLOTS * P}
            load_all(c, "const", [(consts[k][:], a[k].broadcast_to([P, widths[k]]) if k in widths else a[k])
                                  for k in ("ident", "halves", "bucket", "earlier", "node_ids", "fold", "before", "lower",
                                            "diff", "steps")])
            zeros = c.sb(ctx_c, "zeros", [P, CHUNKS0 * D // 2], FP32)
            with nc.Block() as block:
                @block.vector
                def _(dve):
                    nc.vector.memset(ones[:], 1.0).then_inc(set_const, 1)
                    nc.vector.memset(eps[:], EPS).then_inc(set_const, 1)
                    nc.vector.memset(zeros[:], 0.0).then_inc(set_const, 1)
                    dve.wait_ge(set_const, 3)

                @block.sync
                def _(sp):
                    sp.wait_ge(set_const, 3)
                    for i, n in enumerate((CHUNKS0, CHUNKS1)):
                        for j in range(2):
                            half = n * P // 2
                            sp.dma_start(xs[i][j * half:(j + 1) * half].rearrange("(p r) d -> p (r d)", p=P),
                                         zeros[:, 0:n * D // 2]).then_inc(filled, 16)
                    sp.wait_ge(filled, 64)
        posrec = c.sb(ctx, "posrec", [P, COLS, 1 + REC1], I32)
        with ExitStack() as ctx_c:
            for k, n in (("fold", P), ("before", P), ("lower", P), ("diff", P), ("steps", STEPS)):
                consts[k] = c.sb(ctx_c, k + "2", [P, n], FP32)
            load_all(c, "const2", [(consts[k][:], a[k].broadcast_to([P, STEPS]) if k == "steps" else a[k])
                                   for k in ("fold", "before", "lower", "diff", "steps")])
            tile_ids(c, a["src"], a["dst"], ids_src, ids_dst, rec0, posrec, a["src_cols"], a["dst_cols"], a["ew_cols"])
            count(c, "cd", ids_dst, consts, tab[0], base[0])
            count(c, "cs", ids_src, consts, tab[1], base[1])
            rank(c, "rk", ids_src, consts, base[1], posrec)
        scatter = RecordScatter(c, ctx, posrec, rec1)
        degrees(c, posrec, dinv, dinv_row, ident, consts)

        normalize(c, "ln0", a["x"], rows["xn0"], eps)
        with ExitStack() as ctx_g:
            agg_t = c.sb(ctx_g, "agg_t", [P, KD, SLOTS * P], FP32)
            with ExitStack() as ctx_w:
                w_edge = c.sb(ctx_w, "w_edge", [ATTR, D], FP32)
                load_all(c, "l0e", [(w_edge[:], a["L0_gnn_W_edge"])])
                aggregate_edges(c, "e0", rows["xn0"], rec0, REC0, tab[0], node_ids, agg_t, a["attr_t"], w_edge)
            with ExitStack() as ctx_w:
                w = {k: c.sb(ctx_w, k, [P, KD, D], FP32) for k in ("w_rel", "w_root", "w_res")}
                v = {k: c.sb(ctx_w, k, [P, KD], FP32) for k in ("b_rel", "gamma", "beta")}
                load_all(c, "l0d", [(w["w_rel"][:], weights_view(a["L0_gnn_W_rel"])), (w["w_root"][:], weights_view(a["L0_gnn_W_root"])),
                                    (w["w_res"][:], weights_view(a["L0_gnn_W_res"])), (v["b_rel"][:], a["L0_gnn_b_rel"]),
                                    (v["gamma"][:], a["L0_gnn_gamma"]), (v["beta"][:], a["L0_gnn_beta"])])
                with ExitStack() as ctx_t:
                    xn_t = c.sb(ctx_t, "xn_t", [P, KD, NODES_PAD], FP32)
                    read_transposed(c, "t0", rows["xn0"], xn_t, ident, beside=lambda b: scatter.part(b, "t0", 4))
                    first_dense(c, agg_t, xn_t, w["w_rel"], w["w_root"], v["b_rel"], v["gamma"], v["beta"], eps, beside=lambda b: scatter.part(b, "fd", 5))
                add_block_output(c, "o0", a["x"], agg_t, rows["xn0"], w["w_res"], ident, rows["x1"], beside=lambda b: scatter.part(b, "o0", 13))

        normalize(c, "ln1", rows["x1"], rows["xn1"], eps, beside=lambda b: scatter.part(b, "ln1", 3))
        with ExitStack() as ctx_f:
            place = c.sb(ctx_f, "place0", [P, TILES, TOP0], I32)
            expert = c.sb(ctx_f, "expert0", [1, CHUNKS0], I32)
            wg = c.sb(ctx_f, "wg0", [P, KD, EXPERTS], FP32)
            bg = c.sb(ctx_f, "bg0", [P, EXPERTS], FP32)
            load_all(c, "l0g", [(wg[:], weights_view(a["L0_ffn_Wg"])), (bg[:], row_view(a["L0_ffn_bg"], EXPERTS))])
            gate_scores(c, "g0", rows["xn1"], scores, ident, wg, bg, beside=lambda b: scatter.part(b, "g0", 6))
            choose(c, "c0", scores, TOP0, CHUNKS0, consts, place, expert)
            dispatch(c, "d0", rows["xn1"], place, TOP0, xs[0])
            with ExitStack() as ctx_w:
                w1 = c.sb(ctx_w, "w1_0", [P, EXPERTS, KD, HID0], FP32)
                b1 = c.sb(ctx_w, "b1_0", [P, EXPERTS, HID0], FP32)
                w2 = c.sb(ctx_w, "w2_0", [P, EXPERTS, HID0 // P, D], FP32)
                b2 = c.sb(ctx_w, "b2_0", [P, EXPERTS, D], FP32)
                load_all(c, "l0x", [(w1[:], a["L0_ffn_W1"].rearrange("e (k p) n -> p e k n", p=P)), (b1[:], all_rows(a["L0_ffn_b1"])),
                                    (w2[:], a["L0_ffn_W2"].rearrange("e (k p) n -> p e k n", p=P)), (b2[:], all_rows(a["L0_ffn_b2"]))])
                experts(c, "x0", xs[0], ys[0], CHUNKS0, expert, ident, HID0, w1, b1, w2, b2, False,
                        beside=lambda b: scatter.part(b, "x0", COLS))
            combine(c, "m0", rows["x1"], ys[0], place, TOP0, rows["x2"])

        normalize(c, "ln2", rows["x2"], rows["y2"], eps, dinv)
        with ExitStack() as ctx_g:
            agg_t = c.sb(ctx_g, "agg_t2", [P, KD, SLOTS * P], FP32)
            aggregate_edges(c, "e1", rows["y2"], rec1, REC1, tab[1], node_ids, agg_t)
            w = {k: c.sb(ctx_g, "s" + k, [P, KD, D], FP32) for k in ("W", "W1", "W2")}
            v = {k: c.sb(ctx_g, "s" + k, [P, KD], FP32) for k in ("b", "b1")}
            b2 = c.sb(ctx_g, "sb2", [P, D], FP32)
            with ExitStack() as ctx_t:
                y_t = c.sb(ctx_t, "y_t", [P, KD, NODES_PAD], FP32)
                dinv_b = c.sb(ctx_t, "dinv_b", [P, NODES_PAD], FP32)
                load_all(c, "l1d", [(w[k][:], weights_view(a["L1_gnn_" + k])) for k in w] + [(v[k][:], a["L1_gnn_" + k]) for k in v]
                         + [(b2[:], row_view(a["L1_gnn_b2"], D)), (dinv_b[:], row_view(dinv_row, NODES_PAD))])
                read_transposed(c, "t1", rows["y2"], y_t, ident)
                second_dense(c, agg_t, y_t, dinv_b, w["W"], v["b"], w["W1"], v["b1"])
            add_projection(c, "o1", rows["x2"], agg_t, w["W2"], b2, rows["x3"])

        normalize(c, "ln3", rows["x3"], rows["xn3"], eps)
        with ExitStack() as ctx_f:
            place = c.sb(ctx_f, "place1", [P, TILES, TOP1], I32)
            prob = c.sb(ctx_f, "prob", [P, TILES], FP32)
            expert = c.sb(ctx_f, "expert1", [1, CHUNKS1], I32)
            w1 = c.sb(ctx_f, "w1_1", [P, 1, KD, HID1], FP32)
            b1 = c.sb(ctx_f, "b1_1", [P, 1, HID1], FP32)
            b1_col = c.sb(ctx_f, "b1_col", [P, HID1 // P], FP32)
            wg = c.sb(ctx_f, "wg1", [P, HID1 // P, EXPERTS], FP32)
            bg = c.sb(ctx_f, "bg1", [P, EXPERTS], FP32)
            load_all(c, "l1g", [(wg[:], weights_view(a["L1_ffn_Wg"])), (bg[:], row_view(a["L1_ffn_bg"], EXPERTS)),
                                (w1[:, 0], weights_view(a["L1_ffn_W1"])), (b1[:, 0], row_view(a["L1_ffn_b1"], HID1)),
                                (b1_col[:], a["b1_cols"])])
            gate_scores(c, "g1", rows["xn3"], scores, ident, wg, bg, w1[:, 0], b1_col)
            choose(c, "c1", scores, TOP1, CHUNKS1, consts, place, expert, prob)
            dispatch(c, "d1", rows["xn3"], place, TOP1, xs[1])
            with ExitStack() as ctx_w:
                w2 = c.sb(ctx_w, "w2_1", [P, EXPERTS, HID1 // P, D], FP32)
                b2 = c.sb(ctx_w, "b2_1", [P, EXPERTS, D], FP32)
                load_all(c, "l1x", [(w2[:], a["L1_ffn_Wd"].rearrange("e (k p) n -> p e k n", p=P)), (b2[:], all_rows(a["L1_ffn_bd"]))])
                experts(c, "x1", xs[1], ys[1], CHUNKS1, expert, ident, HID1, w1, b1, w2, b2, True)
            combine(c, "m1", rows["x3"], ys[1], place, TOP1, out, prob)


def kernel(**inputs):
    import concourse.bacc as bacc
    from concourse.bass_utils import run_bass_kernel_spmd as run

    nc = bacc.Bacc("TRN2", target_bir_lowering=False, num_devices=1)
    arrays = {k: np.ascontiguousarray(v) for k, v in inputs.items()}
    x, src, dst = arrays.pop("x"), arrays.pop("src"), arrays.pop("dst")
    attr, ew = arrays.pop("edge_attr_64"), arrays.pop("edge_weight")
    more = EDGES_PAD - EDGES
    arrays["x"] = np.concatenate([x, np.zeros((NODES_PAD - NODES, D), x.dtype)])
    arrays["src"] = np.concatenate([src, np.full(more, NODES_PAD, src.dtype)])
    arrays["dst"] = np.concatenate([dst, np.full(more, NODES_PAD, dst.dtype)])
    arrays["attr_t"] = np.ascontiguousarray(np.concatenate([attr, np.zeros((more, ATTR), attr.dtype)]).T)
    ew = np.concatenate([ew, np.zeros(more, ew.dtype)])
    for name, v in (("src_cols", arrays["src"]), ("dst_cols", arrays["dst"]), ("ew_cols", ew)):
        arrays[name] = np.ascontiguousarray(v.reshape(COLS, P).T)
    arrays["b1_cols"] = np.ascontiguousarray(arrays["L1_ffn_b1"].reshape(HID1 // P, P).T)
    for name in ("L0_gnn_b_rel", "L0_gnn_gamma", "L0_gnn_beta", "L1_gnn_b", "L1_gnn_b1"):
        arrays[name] = np.ascontiguousarray(arrays[name].reshape(KD, P).T)
    arrays.update(const_arrays())
    aps = {k: nc.dram_tensor("in_" + k, v.shape, mybir.dt.from_np(v.dtype), kind="ExternalInput").ap()
           for k, v in arrays.items()}
    out = nc.dram_tensor("out", (NODES_PAD, D), FP32, kind="ExternalOutput").ap()
    program(nc, aps, out)
    result = run(nc, [{"in_" + k: v for k, v in arrays.items()}], core_ids=[0])
    return np.asarray(result.results[0]["out"])[:NODES]
```

```python
from contextlib import ExitStack

import numpy as np
import concourse.bass as bass
from concourse import mybir

FP32 = mybir.dt.float32
BF16 = mybir.dt.bfloat16
I32 = mybir.dt.int32
ALU = mybir.AluOpType
ACT = mybir.ActivationFunctionType
AX = mybir.AxisListType
EngineType = mybir.EngineType

P = 128
D = 256
KD = D // P
NODES = 6250
TILES = -(-NODES // P)
NODES_PAD = TILES * P
SLOTS = TILES + 1
EDGES = 106250
COLS = 832
EDGES_PAD = COLS * P
ATTR = 64
UNROLL = 16
SLOT = 4
STEPS = -(-(EDGES // P + TILES) // UNROLL) * UNROLL
EPS = 1e-5
HALVES = 2
HALF = EDGES_PAD // HALVES
RANK_BLOCKS = 16
RANK_COLS = COLS // HALVES // RANK_BLOCKS
RANK_LEN = RANK_COLS * P
GROUP = 7
GROUPS = TILES // GROUP
WIDE = NODES_PAD // 14
WIDES = 14
EXPERTS = 8
TOP0, TOP1 = 2, 1
HID0, HID1 = 512, 1024
CHUNKS0 = -(-((NODES_PAD * TOP0 + EXPERTS * (P - 1)) // P) // 2) * 2
CHUNKS1 = -(-((NODES_PAD * TOP1 + EXPERTS * (P - 1)) // P) // 2) * 2
REC0 = 2
REC1 = 4


def static(t):
    return isinstance(t, int)


def pairs(eng, n, body):
    body(0, 0)
    body(1, 1)
    if n >= 4:
        with eng.Fori(1, n // 2) as i:
            body(i * 2, 0)
            body(i * 2 + 1, 1)
    if n % 2:
        body(n - 1, 0)


def unrolled(eng, n, body):
    body(0, 0)
    with eng.Fori(1, n // UNROLL) as i:
        body(i * UNROLL, i)


class Core:

    def __init__(self, nc, ctx):
        self.nc, self.ctx, self.live = nc, ctx, []

    def sb(self, ctx, name, shape, dt):
        return ctx.enter_context(self.nc.sbuf_tensor(name, shape, dt))

    def ps(self, ctx, name, shape, dt=FP32):
        return ctx.enter_context(self.nc.psum_tensor(name, shape, dt))

    def sem(self, name):
        s = self.nc.alloc_semaphore(name=name)
        self.live.append(s)
        return s

    def clear(self, first):
        self.nc.clear_and_free_semaphores(self.live[first:])
        self.nc.all_engine_barrier()
        del self.live[first:]

    def dram(self, name, shape, dt):
        return self.nc.dram_tensor(name, shape, dt, kind="Internal").ap()


def phase(f):
    def run(c, *args, **kwargs):
        first = len(c.live)
        f(c, *args, **kwargs)
        c.clear(first)
    return run


def tiles_view(a):
    return a.rearrange("(g a p) d -> g p a d", a=GROUP, p=P)


class At:

    def __init__(self, step, u, i, n):
        self.step, self.u, self.i, self.n = step, u, i, n

    def __call__(self, lag):
        t, slot = self.step - lag, (self.u - lag) % SLOT
        if static(t):
            return (t, slot, t // SLOT) if 0 <= t < self.n else None
        return t, slot, self.i + (self.u - lag) // SLOT


def old(t, k):
    return not static(t) or t >= k


def pipeline(eng, n, depth, body):
    for s in range(2 * SLOT):
        body(At(s, s % SLOT, None, n))
    with eng.Fori(2, n // SLOT) as i:
        for u in range(SLOT):
            body(At(i * SLOT + u, u, i, n))
    for s in range(n // SLOT * SLOT, n + depth - 1):
        body(At(s, s % SLOT, None, n))


def tile_rows(a, t):
    return a[bass.ds(t * P, P), :]


@phase
def rows_pass(c, name, x_in, ys=None, place=None, top=0, prob=None, x_out=None, norm=None, beside=None):
    nc = c.nc
    with ExitStack() as ctx:
        x = c.sb(ctx, name + "_x", [P, 2, GROUP, D], FP32)
        passed = c.sem(name + "_passed")
        loaded = [c.sem(f"{name}_loaded{u}") for u in range(2)]
        if ys is not None:
            r = c.sb(ctx, name + "_r", [P, 2, top, GROUP, D], FP32)
            z = c.sb(ctx, name + "_z", [P, 2, GROUP, D], FP32)
            at = c.sb(ctx, name + "_at", [P, 2, GROUP, top], I32)
            got = [c.sem(f"{name}_got{u}") for u in range(2)]
            stored = [c.sem(f"{name}_stored{u}") for u in range(2)]
            staged = c.sem(name + "_staged")
            partly = c.sem(name + "_partly")
            added = c.sem(name + "_added")
            per = 16 * GROUP * top
        if norm is not None:
            eps, row_scale, out, turned_t, ident = norm
            y = c.sb(ctx, name + "_y", [P, 2, GROUP, D], FP32)
            st = c.sb(ctx, name + "_st", [P, 2, GROUP, 6], FP32)
            mv = c.sb(ctx, name + "_mv", [P, 2, GROUP, 2], FP32)
            sd = c.sb(ctx, name + "_sd", [P, 2, GROUP], FP32)
            rs = c.sb(ctx, name + "_rs", [P, 2, GROUP], FP32)
            pt = [c.ps(ctx, f"{name}_pt{a}", [P, KD, P]) for a in range(GROUP)]
            normed_out = [c.sem(f"{name}_normed_out{u}") for u in range(2)]
            stats = c.sem(name + "_stats")
            moments = c.sem(name + "_moments")
            root = c.sem(name + "_root")
            inverse = c.sem(name + "_inverse")
            normed = c.sem(name + "_normed")
            turned = c.sem(name + "_turned")
            copied = c.sem(name + "_copied")
            ni = 1 if row_scale is None else 2
        block = ctx.enter_context(nc.Block())
        if beside is not None:
            beside(block)

        @block.sync
        def _(sp):
            def body(g, u):
                if old(g, 2):
                    sp.wait_ge(normed if ys is None else added, g - 1)
                sp.dma_start(x[:, u], tiles_view(x_in)[bass.ds(g, 1)].rearrange("o p a d -> p (o a) d")).then_inc(loaded[u], 16)
            pairs(sp, GROUPS, body)

        if ys is not None:
            @block.gpsimd
            def _(pool):
                def body(g, u):
                    if old(g, 2):
                        pool.wait_ge(added, g - 1)
                    pool.tensor_copy(at[:, u], place[:, bass.ds(g * GROUP, GROUP)]).then_inc(staged, 1)
                    pool.wait_ge(staged, g + 1)
                    pool.sem_inc(passed, 1)
                    for t in range(GROUP):
                        for k in range(top):
                            pool.indirect_dma_start(
                                out=r[:, u, k, t], out_offset=None, in_=ys,
                                in_offset=bass.IndirectOffsetOnAxis(ap=at[:, u, t, k:k + 1], axis=0)).then_inc(got[u], 16)
                pairs(pool, GROUPS, body)

        @block.vector
        def _(dve):
            def body(g, u):
                if ys is not None:
                    dve.wait_ge(got[u], (g // 2) * per + per)
                    r0 = r[:, u, 0]
                    if prob is None:
                        nc.vector.tensor_tensor(r0, r0, r[:, u, 1], ALU.add).then_inc(partly, 1)
                    else:
                        nc.vector.tensor_tensor(r0, r0, prob[:, bass.ds(g * GROUP, GROUP)].unsqueeze(2).broadcast_to([P, GROUP, D]),
                                                ALU.mult).then_inc(partly, 1)
                    dve.wait_ge(partly, g + 1)
                    dve.wait_ge(loaded[u], (g // 2) * 16 + 16)
                    if old(g, 2):
                        dve.wait_ge(stored[u], (g // 2) * 16)
                        if norm is not None:
                            dve.wait_ge(normed, g - 1)
                    nc.vector.tensor_tensor(z[:, u], r0, x[:, u], ALU.add).then_inc(added, 1)
                    dve.wait_ge(added, g + 1)
                    rows = z
                else:
                    dve.wait_ge(loaded[u], (g // 2) * 16 + 16)
                    rows = x
                if norm is None:
                    return
                for a in range(GROUP):
                    last = nc.vector.bn_stats(st[:, u, a], rows[:, u, a])
                last.then_inc(stats, 1)
                dve.wait_ge(stats, g + 1)
                if old(g, 2):
                    dve.wait_ge(root, g - 1)
                dve.sem_inc(passed, 1)
                for a in range(GROUP):
                    last = nc.vector.bn_aggr(mv[:, u, a], st[:, u, a])
                last.then_inc(moments, 1)
                dve.wait_ge(root, g + 1)
                nc.vector.reciprocal(rs[:, u], sd[:, u]).then_inc(inverse, 1)
                dve.wait_ge(inverse, g * ni + 1)
                if row_scale is not None:
                    nc.vector.tensor_tensor(rs[:, u], rs[:, u], row_scale[:, bass.ds(g * GROUP, GROUP)],
                                            ALU.mult).then_inc(inverse, 1)
                    dve.wait_ge(inverse, g * ni + 2)
                if old(g, 2):
                    dve.wait_ge(normed_out[u], (g // 2) * 16)
                    dve.wait_ge(turned, g * GROUP - GROUP)
                for a in range(GROUP):
                    last = nc.vector.tensor_scalar(y[:, u, a], rows[:, u, a], mv[:, u, a, 0:1], rs[:, u, a:a + 1],
                                                   ALU.subtract, ALU.mult)
                last.then_inc(normed, 1)
            pairs(dve, GROUPS, body)

        @block.scalar
        def _(act):
            def put(dst, g, tile, u, sem):
                act.dma_start(tiles_view(dst)[bass.ds(g, 1)].rearrange("o p a d -> p (o a) d"), tile[:, u]).then_inc(sem[u], 16)

            def body(g, u):
                if ys is not None:
                    act.wait_ge(added, g + 1)
                    put(x_out, g, z, u, stored)
                if norm is None:
                    return
                act.wait_ge(moments, g + 1)
                if old(g, 2):
                    act.wait_ge(inverse, g * ni - ni)
                nc.scalar.activation(sd[:, u], mv[:, u, :, 1], ACT.Sqrt, bias=eps[:, 0:1]).then_inc(root, 1)
                act.wait_ge(normed, g + 1)
                put(out, g, y, u, normed_out)
                for a in range(GROUP):
                    act.wait_ge(turned, g * GROUP + (a + 1))
                    act.sem_inc(passed, 1)
                    nc.scalar.activation(turned_t[:, :, bass.ds((g * GROUP + a) * P, P)], pt[a][:], ACT.Copy).then_inc(copied, 1)
            pairs(act, GROUPS, body)
            for u in range(2):
                n = 16 * ((GROUPS + 1 - u) // 2)
                if ys is not None:
                    act.wait_ge(stored[u], n)
                if norm is not None:
                    act.wait_ge(normed_out[u], n)

        if norm is not None:
            @block.tensor
            def _(pe):
                def body(g, u):
                    pe.wait_ge(normed, g + 1)
                    for a in range(GROUP):
                        if old(g, 1):
                            pe.wait_ge(copied, g * GROUP + (a + 1 - GROUP))
                        for k in range(KD):
                            last = nc.tensor.transpose(pt[a][:, k], y[:, u, a, k * P:(k + 1) * P], ident[:])
                        last.then_inc(turned, 1)
                pairs(pe, GROUPS, body)


@phase
def finish_graph(c, name, x_in, z_t, w, ident, mv, x_out, xn_t=None, scale=None, shift=None, b_row=None, beside=None):
    nc = c.nc
    first = xn_t is not None
    with ExitStack() as ctx:
        x = c.sb(ctx, name + "_x", [P, SLOT, D], FP32)
        za = c.sb(ctx, name + "_za", [P, SLOT, KD, P], FP32)
        zb = c.sb(ctx, name + "_zb", [P, SLOT, KD, P], FP32)
        y = c.sb(ctx, name + "_y", [P, SLOT, D], FP32)
        st = c.sb(ctx, name + "_st", [P, TILES, 6], FP32)
        pr = [c.ps(ctx, f"{name}_pr{u}", [P, KD, P]) for u in range(2)]
        po = [c.ps(ctx, f"{name}_po{u}", [P, KD, P]) for u in range(2)]
        loaded = [c.sem(f"{name}_loaded{u}") for u in range(SLOT)]
        stored = [c.sem(f"{name}_stored{u}") for u in range(SLOT)]
        staged = c.sem(name + "_staged")
        residual = c.sem(name + "_residual")
        ready = c.sem(name + "_ready")
        multiplied = c.sem(name + "_multiplied")
        added = c.sem(name + "_added")
        stats = c.sem(name + "_stats")
        passed = c.sem(name + "_passed")
        block = ctx.enter_context(nc.Block())
        if beside is not None:
            beside(block)

        @block.sync
        def _(sp):
            def body(at):
                if now := at(0):
                    t, v, i = now
                    if old(t, SLOT):
                        sp.wait_ge(added, t - (SLOT - 1))
                    sp.dma_start(x[:, v], tile_rows(x_in, t)).then_inc(loaded[v], 16)
            pipeline(sp, TILES, 1, body)

        @block.scalar
        def _(act):
            def body(at):
                if now := at(0):
                    t, v, i = now
                    if old(t, SLOT):
                        act.wait_ge(ready if first else multiplied, t - (SLOT - 1))
                        act.sem_inc(passed, 1)
                    z = z_t[:, :, bass.ds(t * P, P)]
                    if first:
                        for m in range(KD):
                            last = nc.scalar.activation(za[:, v, m], z[:, m], ACT.Identity, bias=shift[:, m:m + 1],
                                                        scale=scale[:, m:m + 1])
                        last.then_inc(staged, 1)
                    else:
                        nc.scalar.activation(za[:, v], z, ACT.Copy).then_inc(staged, 1)
                if now := at(4):
                    t, v, i = now
                    act.wait_ge(added, t + 1)
                    act.sem_inc(passed, 1)
                    act.dma_start(tile_rows(x_out, t), y[:, v]).then_inc(stored[v], 16)
            pipeline(act, TILES, 5, body)
            for v in range(SLOT):
                act.wait_ge(stored[v], 16 * ((TILES + SLOT - 1 - v) // SLOT))

        @block.tensor
        def _(pe):
            def body(at):
                if first and (now := at(0)):
                    t, v, i = now
                    if old(t, 2):
                        pe.wait_ge(ready, t - 1)
                    for m in range(KD):
                        for k in range(KD):
                            last = nc.tensor.matmul(pr[v % 2][:, m], w[:, k, m * P:(m + 1) * P], xn_t[:, k, bass.ds(t * P, P)],
                                                    start=k == 0, stop=k == KD - 1)
                    last.then_inc(residual, 1)
                if now := at(2):
                    t, v, i = now
                    pe.wait_ge(ready, t + 1)
                    if not first:
                        pe.wait_ge(staged, t + 1)
                    if old(t, 2):
                        pe.wait_ge(added, t - 1)
                    for k in range(KD):
                        if first:
                            last = nc.tensor.transpose(po[v % 2][:, k], zb[:, v, k], ident[:])
                        else:
                            last = nc.tensor.matmul(po[v % 2][:].rearrange("p k n -> p (k n)"), za[:, v, k], w[:, k],
                                                    start=k == 0, stop=k == KD - 1)
                    last.then_inc(multiplied, 1)
            pipeline(pe, TILES, 3, body)

        @block.vector
        def _(dve):
            def body(at):
                if now := at(1):
                    t, v, i = now
                    if first:
                        dve.wait_ge(staged, t + 1)
                        dve.wait_ge(residual, t + 1)
                        if old(t, SLOT):
                            dve.wait_ge(multiplied, t - (SLOT - 1))
                        nc.vector.tensor_tensor(zb[:, v], za[:, v], pr[v % 2][:], ALU.add).then_inc(ready, 1)
                    else:
                        dve.wait_ge(loaded[v], i * 16 + 16)
                        if old(t, SLOT):
                            dve.wait_ge(added, t - (SLOT - 1))
                        nc.vector.tensor_tensor(zb[:, v].rearrange("p k n -> p (k n)"), x[:, v], b_row[:], ALU.add).then_inc(ready, 1)
                if now := at(3):
                    t, v, i = now
                    dve.wait_ge(loaded[v], i * 16 + 16)
                    dve.wait_ge(ready, t + 1)
                    dve.wait_ge(multiplied, t + 1)
                    if old(t, SLOT):
                        dve.wait_ge(stored[v], i * 16)
                        dve.wait_ge(stats, t - (SLOT - 1))
                    a = x[:, v] if first else zb[:, v].rearrange("p k n -> p (k n)")
                    nc.vector.tensor_tensor(y[:, v], a, po[v % 2][:].rearrange("p k n -> p (k n)"), ALU.add).then_inc(added, 1)
                if now := at(4):
                    t, v, i = now
                    dve.wait_ge(added, t + 1)
                    dve.sem_inc(passed, 1)
                    nc.vector.bn_stats(st[:, bass.ds(t, 1)].rearrange("p o s -> p (o s)"), y[:, v]).then_inc(stats, 1)
            pipeline(dve, TILES, 5, body)
            dve.wait_ge(stats, TILES)
            for t in range(TILES):
                nc.vector.bn_aggr(mv[:, t], st[:, t])


@phase
def gate_pass(c, name, x_in, mv, eps, xn, scores, ident, wg, bg_row, w1=None, b1=None, beside=None):
    nc = c.nc
    hidden_layer = w1 is not None
    km = HID1 // P if hidden_layer else KD
    with ExitStack() as ctx:
        x = c.sb(ctx, name + "_x", [P, SLOT, D], FP32)
        y = c.sb(ctx, name + "_y", [P, SLOT, D], FP32)
        x_t = c.sb(ctx, name + "_xt", [P, SLOT, KD, P], FP32)
        sd = c.sb(ctx, name + "_sd", [P, TILES], FP32)
        rs = c.sb(ctx, name + "_rs", [P, TILES], FP32)
        pt = [c.ps(ctx, f"{name}_pt{u}", [P, KD, P]) for u in range(2)]
        pg = [c.ps(ctx, f"{name}_pg{u}", [P, 512]) for u in range(2)]
        if hidden_layer:
            h_t = c.sb(ctx, name + "_ht", [P, SLOT, km, P], FP32)
            ph = [c.ps(ctx, f"{name}_ph{n}", [P, 4, P]) for n in range(4)]
            hidden = c.sem(name + "_hidden")
            active = c.sem(name + "_active")
        loaded = [c.sem(f"{name}_loaded{u}") for u in range(SLOT)]
        stored = [c.sem(f"{name}_stored{u}") for u in range(SLOT)]
        root = c.sem(name + "_root")
        inverse = c.sem(name + "_inverse")
        normed = c.sem(name + "_normed")
        turned = c.sem(name + "_turned")
        copied = c.sem(name + "_copied")
        gated = c.sem(name + "_gated")
        kept = c.sem(name + "_kept")
        passed = c.sem(name + "_passed")
        block = ctx.enter_context(nc.Block())
        if beside is not None:
            beside(block)

        @block.sync
        def _(sp):
            def body(at):
                if now := at(0):
                    t, v, i = now
                    if old(t, SLOT):
                        sp.wait_ge(normed, t - (SLOT - 1))
                    sp.dma_start(x[:, v], tile_rows(x_in, t)).then_inc(loaded[v], 16)
                if now := at(2):
                    t, v, i = now
                    sp.wait_ge(normed, t + 1)
                    sp.dma_start(tile_rows(xn, t), y[:, v]).then_inc(stored[v], 16)
            pipeline(sp, TILES, 3, body)
            for v in range(SLOT):
                sp.wait_ge(stored[v], 16 * ((TILES + SLOT - 1 - v) // SLOT))

        @block.vector
        def _(dve):
            dve.wait_ge(root, 1)
            nc.vector.reciprocal(rs[:], sd[:]).then_inc(inverse, 1)
            dve.wait_ge(inverse, 1)

            def body(at):
                if now := at(1):
                    t, v, i = now
                    dve.wait_ge(loaded[v], i * 16 + 16)
                    if old(t, SLOT):
                        dve.wait_ge(stored[v], i * 16)
                        dve.wait_ge(turned, t - (SLOT - 1))
                    nc.vector.tensor_scalar(y[:, v], x[:, v], mv[:, bass.ds(t, 1), 0], rs[:, bass.ds(t, 1)],
                                            ALU.subtract, ALU.mult).then_inc(normed, 1)
                if now := at(2):
                    t, v, i = now
                    dve.wait_ge(turned, t + 1)
                    if old(t, SLOT):
                        dve.wait_ge(hidden, t * 2 - (SLOT * 2 - 2)) if hidden_layer else dve.wait_ge(gated, t - (SLOT - 1))
                        dve.sem_inc(passed, 1)
                    nc.vector.tensor_copy(x_t[:, v], pt[v % 2][:]).then_inc(copied, 1)
                if now := at(4):
                    t, v, i = now
                    dve.wait_ge(gated, t + 1)
                    nc.vector.tensor_tensor(scores[:, bass.ds(t, 1)].rearrange("p o e -> p (o e)"), pg[v % 2][:, 0:EXPERTS],
                                            bg_row[:], ALU.add).then_inc(kept, 1)
            pipeline(dve, TILES, 5, body)

        @block.scalar
        def _(act):
            nc.scalar.activation(sd[:], mv[:, :, 1], ACT.Sqrt, bias=eps[:, 0:1]).then_inc(root, 1)
            if hidden_layer:
                def body(at):
                    if now := at(3):
                        t, v, i = now
                        if old(t, SLOT):
                            act.wait_ge(gated, t - (SLOT - 1))
                        for n in range(2):
                            act.wait_ge(hidden, t * 2 + (n + 1))
                            for m in range(4):
                                last = nc.scalar.activation(h_t[:, v, n * 4 + m], ph[v % 2 * 2 + n][:, m], ACT.Gelu,
                                                            bias=b1[:, n * 4 + m:n * 4 + m + 1])
                            last.then_inc(active, 1)
                pipeline(act, TILES, 4, body)

        @block.tensor
        def _(pe):
            def body(at):
                if now := at(2):
                    t, v, i = now
                    pe.wait_ge(normed, t + 1)
                    if old(t, 2):
                        pe.wait_ge(copied, t - 1)
                    for k in range(KD):
                        last = nc.tensor.transpose(pt[v % 2][:, k], y[:, v, k * P:(k + 1) * P], ident[:])
                    last.then_inc(turned, 1)
                if hidden_layer and (now := at(3)):
                    t, v, i = now
                    pe.wait_ge(copied, t + 1)
                    for n in range(2):
                        if old(t, 2):
                            pe.wait_ge(active, t * 2 + (n - 3))
                        for m in range(n * 4, n * 4 + 4):
                            for k in range(KD):
                                last = nc.tensor.matmul(ph[v % 2 * 2 + n][:, m % 4], w1[:, k, m * P:(m + 1) * P],
                                                        x_t[:, v, k], start=k == 0, stop=k == KD - 1)
                        last.then_inc(hidden, 1)
                if now := at(4):
                    t, v, i = now
                    if hidden_layer:
                        pe.wait_ge(active, t * 2 + 2)
                    else:
                        pe.wait_ge(copied, t + 1)
                    z = h_t if hidden_layer else x_t
                    if old(t, 2):
                        pe.wait_ge(kept, t - 1)
                    for k in range(km):
                        last = nc.tensor.matmul(pg[v % 2][:, 0:EXPERTS], z[:, v, k], wg[:, k], start=k == 0, stop=k == km - 1)
                    last.then_inc(gated, 1)
            pipeline(pe, TILES, 5, body)


class Prefetch:

    def __init__(self, c, name, items):
        self.items, self.sem = items, c.nc.alloc_semaphore(name=name + "_fetched")

    def start(self, block):
        @block.sync
        def _(sp):
            for tile, src in self.items:
                sp.dma_start(tile, src).then_inc(self.sem, 16)

    def finish(self, block):
        @block.scalar
        def _(act):
            act.wait_ge(self.sem, 16 * len(self.items))


@phase
def tile_ids(c, src_flat, dst_flat, ids_src, ids_dst, rec0, posrec, src_cols, dst_cols, ew_cols, beside):
    nc = c.nc
    with ExitStack() as ctx:
        s_i = c.sb(ctx, "ids_s", [P, COLS], I32)
        d_i = c.sb(ctx, "ids_d", [P, COLS], I32)
        t_i = c.sb(ctx, "ids_t", [P, 2, COLS], I32)
        t_b = c.sb(ctx, "ids_b", [P, 2, COLS], BF16)
        r0 = c.sb(ctx, "ids_r0", [P, COLS, REC0], I32)
        sc = c.sb(ctx, "ids_sc", [P, COLS], I32)
        dc = c.sb(ctx, "ids_dc", [P, COLS], I32)
        ec = c.sb(ctx, "ids_ec", [P, COLS], FP32)
        loaded = c.sem("ids_loaded")
        loaded_cols = c.sem("ids_loaded_cols")
        shifted = c.sem("ids_shifted")
        made = c.sem("ids_made")
        stored = c.sem("ids_stored")
        block = ctx.enter_context(nc.Block())

        @block.sync
        def _(sp):
            sp.dma_start(s_i[:], src_flat.rearrange("(p j) -> p j", p=P)).then_inc(loaded, 16)
            sp.dma_start(d_i[:], dst_flat.rearrange("(p j) -> p j", p=P)).then_inc(loaded, 16)
            sp.dma_start(sc[:], src_cols).then_inc(loaded_cols, 16)
            sp.dma_start(dc[:], dst_cols).then_inc(loaded_cols, 16)
            sp.dma_start(ec[:], ew_cols).then_inc(loaded_cols, 16)
            sp.wait_ge(made, 1)
            sp.dma_start(ids_src.rearrange("(p j) -> p j", p=P), t_b[:, 0]).then_inc(stored, 16)
            sp.dma_start(ids_dst.rearrange("(p j) -> p j", p=P), t_b[:, 1]).then_inc(stored, 16)
            sp.wait_ge(made, 2)
            sp.dma_start(rec0.rearrange("(p j) w -> p (j w)", p=P), r0[:].rearrange("p j w -> p (j w)")).then_inc(stored, 16)
            sp.wait_ge(stored, 48)

        beside(block)

        @block.vector
        def _(dve):
            dve.wait_ge(loaded, 32)
            nc.vector.tensor_scalar(t_i[:, 0], s_i[:], 7, None, ALU.arith_shift_right)
            nc.vector.tensor_scalar(t_i[:, 1], d_i[:], 7, None, ALU.arith_shift_right).then_inc(shifted, 1)
            dve.wait_ge(shifted, 1)
            nc.vector.tensor_copy(t_b[:], t_i[:]).then_inc(made, 1)
            nc.vector.tensor_scalar(r0[:, :, 0], s_i[:], NODES_PAD - 1, None, ALU.min)
            nc.vector.tensor_copy(r0[:, :, 1].bitcast(FP32), d_i[:]).then_inc(made, 1)
            dve.wait_ge(loaded_cols, 48)
            nc.vector.tensor_copy(posrec[:, :, 1].bitcast(FP32), sc[:])
            nc.vector.tensor_scalar(posrec[:, :, 2], dc[:], NODES_PAD - 1, None, ALU.min)
            nc.vector.tensor_copy(posrec[:, :, 3], ec[:].bitcast(I32))
            nc.vector.memset(posrec[:, :, 4], 0)


@phase
def count(c, name, ids, consts, tab, base):
    nc = c.nc
    with ExitStack() as ctx:
        ids_b = c.sb(ctx, name + "_ids", [P, 2, RANK_LEN], BF16)
        hit = c.sb(ctx, name + "_hit", [P, 2, RANK_LEN], BF16)
        part = c.sb(ctx, name + "_part", [P, RANK_BLOCKS], FP32)
        cnt = c.sb(ctx, name + "_cnt", [P, 1], FP32)
        small = c.sb(ctx, name + "_small", [P, 8], FP32)
        small_i = c.sb(ctx, name + "_small_i", [P, 2], I32)
        ge = c.sb(ctx, name + "_ge", [P, STEPS], FP32)
        rows = c.sb(ctx, name + "_rows", [1, 2, STEPS], FP32)
        pm = c.ps(ctx, name + "_pm", [P, 512])
        pt = [c.ps(ctx, f"{name}_pt{i}", [1, 512]) for i in range(4)]
        loaded = [c.sem(f"{name}_loaded{u}") for u in range(2)]
        counted = c.sem(name + "_counted")
        small_done = c.sem(name + "_small_done")
        product = c.sem(name + "_product")
        table = c.sem(name + "_table")
        passed = c.sem(name + "_passed")
        bucket, fold, before, lower, diff, ones, steps = (consts[k] for k in (
            "bucket", "fold", "before", "lower", "diff", "ones", "steps"))
        ids_h = ids.rearrange("(h n) -> h n", h=HALVES)

        block = ctx.enter_context(nc.Block())

        @block.sync
        def _(sp):
            def body(k, u):
                if not (static(k) and k < 2):
                    sp.wait_ge(counted, k - 1)
                for h in range(HALVES):
                    sp.dma_start(ids_b[h * 64:h * 64 + 64, u],
                                 ids_h[h:h + 1, bass.ds(k * RANK_LEN, RANK_LEN)].broadcast_to([64, RANK_LEN])).then_inc(loaded[u], 16)
            pairs(sp, RANK_BLOCKS, body)

        @block.vector
        def _(dve):
            def body(k, u):
                dve.wait_ge(loaded[u], (k // 2) * 32 + 32)
                if not (static(k) and k < 2):
                    dve.wait_ge(counted, k - 1)
                nc.vector.tensor_scalar(hit[:, u], ids_b[:, u], bucket[:, 0:1], 0.0, ALU.is_equal, ALU.add,
                                        accum_out=part[:, bass.ds(k, 1)]).then_inc(counted, 1)
            pairs(dve, RANK_BLOCKS, body)
            dve.wait_ge(counted, RANK_BLOCKS)
            nc.vector.reduce_sum(cnt[:], part[:], AX.X).then_inc(small_done, 1)
            dve.wait_ge(product, 1)
            nc.vector.tensor_copy(small[:, 0:2], pm[:, 0:2]).then_inc(small_done, 1)
            nc.vector.tensor_scalar(base[:], pm[:, 0:1], -1.0, None, ALU.add)
            dve.wait_ge(small_done, 2)
            nc.vector.tensor_scalar(small_i[:, 0:1], small[:, 1:2], float(P - 1), None, ALU.add).then_inc(small_done, 1)
            dve.wait_ge(small_done, 3)
            nc.vector.tensor_scalar(small_i[:, 1:2], small_i[:, 0:1], 7, None, ALU.arith_shift_right).then_inc(small_done, 1)
            dve.wait_ge(small_done, 4)
            nc.vector.tensor_copy(small[:, 2:3], small_i[:, 1:2]).then_inc(small_done, 1)
            dve.wait_ge(product, 2)
            nc.vector.tensor_copy(small[:, 3:4], pm[:, 2:3]).then_inc(small_done, 1)
            dve.wait_ge(small_done, 6)
            nc.vector.scalar_tensor_tensor(small[:, 4:5], small[:, 3:4], -float(P), small[:, 0:1],
                                           ALU.mult, ALU.add).then_inc(small_done, 1)
            nc.vector.tensor_scalar(ge[:], steps[:], small[:, 3:4], None, ALU.is_ge)
            dve.wait_ge(product, 3)
            nc.vector.tensor_copy(small[:, 5:6], pm[:, 3:4]).then_inc(small_done, 1)
            dve.wait_ge(product, 4)
            for i in range(2):
                s = slice(i * (STEPS // 2), (i + 1) * (STEPS // 2))
                nc.vector.scalar_tensor_tensor(rows[:, 0, s], steps[0:1, s], float(P), pt[i][:, 0:STEPS // 2],
                                               ALU.mult, ALU.add)
                last = nc.vector.tensor_scalar(rows[:, 1, s], pt[2 + i][:, 0:STEPS // 2], -1.0, None, ALU.add)
            last.then_inc(small_done, 1)
            dve.wait_ge(small_done, 9)
            nc.vector.tensor_scalar(tab[:, 0], rows[:, 0], float(EDGES_PAD - P), None, ALU.min)
            nc.vector.tensor_scalar(tab[:, 1], rows[:, 1], float(P), None, ALU.mult).then_inc(table, 1)

        @block.tensor
        def _(pe):
            pe.wait_ge(small_done, 1)
            nc.tensor.matmul(pm[:, 0:1], before[:], cnt[:], start=True, stop=True)
            nc.tensor.matmul(pm[:, 1:2], fold[:], cnt[:], start=True, stop=True).then_inc(product, 1)
            pe.wait_ge(small_done, 5)
            nc.tensor.matmul(pm[:, 2:3], lower[:], small[:, 2:3], start=True, stop=True).then_inc(product, 1)
            pe.wait_ge(small_done, 7)
            nc.tensor.matmul(pm[:, 3:4], diff[:], small[:, 4:5], start=True, stop=True).then_inc(product, 1)
            pe.wait_ge(small_done, 8)
            for i in range(2):
                s = slice(i * (STEPS // 2), (i + 1) * (STEPS // 2))
                nc.tensor.matmul(pt[i][:, 0:STEPS // 2], small[0:SLOTS, 5:6], ge[0:SLOTS, s], start=True, stop=True)
                last = nc.tensor.matmul(pt[2 + i][:, 0:STEPS // 2], ones[0:SLOTS, 0:1], ge[0:SLOTS, s],
                                        start=True, stop=True)
            last.then_inc(product, 1)


@phase
def rank(c, name, ids, consts, base, posrec, ident, pos_flat, beside):
    nc = c.nc
    B = 3
    cuts = [(s, min(512, RANK_LEN - s)) for s in range(0, RANK_LEN, 512)]
    rows8 = COLS // 8
    with ExitStack() as ctx:
        ids_b = c.sb(ctx, name + "_ids", [P, B, RANK_LEN], BF16)
        hit = c.sb(ctx, name + "_hit", [P, RANK_LEN], BF16)
        run = c.sb(ctx, name + "_run", [P, 2, RANK_LEN], FP32)
        place = c.sb(ctx, name + "_place", [P, 2, RANK_LEN], FP32)
        unit = c.sb(ctx, name + "_unit", [P, RANK_LEN], BF16)
        flat = c.sb(ctx, name + "_flat", [HALVES, 2, RANK_LEN], FP32)
        by_col = c.sb(ctx, name + "_by_col", [rows8, 8, P], FP32)
        pp = [c.ps(ctx, f"{name}_pp{u}", [HALVES, 512]) for u in range(4)]
        pt = [c.ps(ctx, f"{name}_pt{u}", [P, 4, P]) for u in range(2)]
        loaded = [c.sem(f"{name}_loaded{u}") for u in range(B)]
        stored = [c.sem(f"{name}_stored{u}") for u in range(2)]
        hits = c.sem(name + "_hits")
        scanned = c.sem(name + "_scanned")
        placed = c.sem(name + "_placed")
        summed = c.sem(name + "_summed")
        kept = c.sem(name + "_kept")
        unit_set = c.sem(name + "_unit_set")
        reloaded = c.sem(name + "_reloaded")
        turned = c.sem(name + "_turned")
        bucket, halves = consts["bucket"], consts["halves"]
        ids_h = ids.rearrange("(h n) -> h n", h=HALVES)
        flat_h = pos_flat.rearrange("(h n) -> h n", h=HALVES)
        nk = len(cuts)
        block = ctx.enter_context(nc.Block())

        @block.sync
        def _(sp):
            for k in range(RANK_BLOCKS):
                if k >= B:
                    sp.wait_ge(hits, k - (B - 1))
                for h in range(HALVES):
                    sp.dma_start(ids_b[h * 64:h * 64 + 64, k % B],
                                 ids_h[h:h + 1, k * RANK_LEN:(k + 1) * RANK_LEN].broadcast_to([64, RANK_LEN])).then_inc(loaded[k % B], 16)
            for u in range(2):
                sp.wait_ge(stored[u], 16 * (RANK_BLOCKS // 2))
            sp.dma_start(by_col[:], pos_flat.rearrange("(b r p) -> r b p", b=8, p=P)).then_inc(reloaded, 16)

        @block.vector
        def _(dve):
            nc.vector.memset(unit[:], 1.0).then_inc(unit_set, 1)
            dve.wait_ge(unit_set, 1)
            for k in range(RANK_BLOCKS):
                u = k % 2
                dve.wait_ge(loaded[k % B], 16 * HALVES * (k // B + 1))
                if k >= 1:
                    dve.wait_ge(placed, k)
                nc.vector.tensor_scalar(hit[:], ids_b[:, k % B], bucket[:, 0:1], None, ALU.is_equal).then_inc(hits, 1)
                dve.wait_ge(hits, k + 1)
                if k >= 1:
                    dve.wait_ge(scanned, k)
                start = base[:, 0:1] if k == 0 else run[:, 1 - u, RANK_LEN - 1:RANK_LEN]
                nc.vector.tensor_tensor_scan(run[:, u], unit[:], hit[:], start, ALU.mult, ALU.add).then_inc(scanned, 1)
                dve.wait_ge(scanned, k + 1)
                if k >= 2:
                    dve.wait_ge(summed, (k - 1) * nk)
                nc.vector.tensor_tensor(place[:, u], run[:, u], hit[:], ALU.mult).then_inc(placed, 1)
            for u in range(2):
                dve.wait_ge(turned, u + 1)
                nc.vector.tensor_copy(posrec[:, u * (COLS // 2):(u + 1) * (COLS // 2), 0].rearrange("p (b r) -> p b r", b=4),
                                      pt[u][:, :, 0:rows8])

        @block.tensor
        def _(pe):
            for k in range(RANK_BLOCKS):
                pe.wait_ge(placed, k + 1)
                for n, (s, m) in enumerate(cuts):
                    if k * nk + n >= 4:
                        pe.wait_ge(kept, k * nk + n - 3)
                    nc.tensor.matmul(pp[(k * nk + n) % 4][:, 0:m], halves[:], place[:, k % 2, s:s + m],
                                     start=True, stop=True).then_inc(summed, 1)
            pe.wait_ge(reloaded, 16)
            for u in range(2):
                for b in range(4):
                    last = nc.tensor.transpose(pt[u][:, b, 0:rows8], by_col[:, u * 4 + b], ident[0:rows8, 0:rows8])
                last.then_inc(turned, 1)

        @block.scalar
        def _(act):
            for k in range(RANK_BLOCKS):
                u = k % 2
                if k >= 2:
                    act.wait_ge(stored[u], 16 * (k // 2))
                for n, (s, m) in enumerate(cuts):
                    act.wait_ge(summed, k * nk + n + 1)
                    nc.scalar.activation(flat[:, u, s:s + m], pp[(k * nk + n) % 4][:, 0:m], ACT.Copy).then_inc(kept, 1)
                act.wait_ge(kept, (k + 1) * nk)
                act.dma_start(flat_h[:, k * RANK_LEN:(k + 1) * RANK_LEN], flat[:, u]).then_inc(stored[u], 16)
        beside(block)


@phase
def aggregate_edges(c, name, table, rec, rec_words, tab, node_ids, agg_t, attr_t=None, w_edge=None, beside=None):
    nc = c.nc
    U = UNROLL
    with ExitStack() as ctx:
        with_attr = attr_t is not None
        rb = c.sb(ctx, name + "_rec", [P, U, rec_words], I32)
        rows = c.sb(ctx, name + "_rows", [P, U, D], FP32)
        pick = c.sb(ctx, name + "_pick", [P, U, P], FP32)
        msg = rows
        if with_attr:
            at = c.sb(ctx, name + "_attr", [ATTR, U, P], FP32)
            pe_edge = [c.ps(ctx, f"{name}_pe{u}", [P, 512]) for u in range(2)]
            got_at = [c.sem(f"{name}_got_at{u}") for u in range(U)]
            edge_done = [c.sem(f"{name}_edge_done{u}") for u in range(U)]
            msg_done = [c.sem(f"{name}_msg_done{u}") for u in range(U)]
        else:
            picked = [c.sem(f"{name}_picked{u}") for u in range(U)]
        pa = [c.ps(ctx, f"{name}_pa{u}", [P, KD, P]) for u in range(2)]
        got_rec = [c.sem(f"{name}_got_rec{u}") for u in range(U)]
        got_rows = [c.sem(f"{name}_got_rows{u}") for u in range(U)]
        summed = [c.sem(f"{name}_summed{u}") for u in range(U)]
        added = [c.sem(f"{name}_added{u}") for u in range(U)]
        zeroed = c.sem(name + "_zeroed")
        passed = c.sem(name + "_passed")
        block = ctx.enter_context(nc.Block())
        if beside is not None:
            beside(block)

        def wait_steps_before(eng, sem, u, i, back):
            if u >= back:
                eng.wait_ge(sem[u - back], i + 1)
            elif not static(i):
                eng.wait_ge(sem[u - back + U], i * 1)

        def numbers(engine, row, s0, top):
            return nc.values_load_multi_w_load_instructions(
                tab[0:1, row, bass.ds(s0, 4)], engines=(engine,), min_val=0, max_val=top,
                skip_runtime_bounds_check_because="the table is clamped to this range when it is made")[1]

        @block.sync
        def _(sp):
            def body(s0, i):
                for u in range(U):
                    if u % 4 == 0:
                        start = numbers(EngineType.SP, 0, s0 + u, EDGES_PAD - P)
                    wait_steps_before(sp, summed, u, i, U)
                    sp.dma_start(rb[:, u], rec[bass.ds(start[u % 4], P), :]).then_inc(got_rec[u], 16)
            unrolled(sp, STEPS, body)

        if with_attr:
            @block.scalar
            def _(act):
                def body(s0, i):
                    for u in range(U):
                        if u % 4 == 0:
                            start = numbers(EngineType.Activation, 0, s0 + u, EDGES_PAD - P)
                        wait_steps_before(act, summed, u, i, U)
                        act.dma_start(at[:, u], attr_t[:, bass.ds(start[u % 4], P)]).then_inc(got_at[u], 16)
                unrolled(act, STEPS, body)

        @block.gpsimd
        def _(pool):
            row_word = 0 if with_attr else 1

            def body(s0, i):
                for u in range(U):
                    wait_steps_before(pool, summed, u, i, U)
                    if not static(i):
                        pool.sem_inc(passed, 1)
                    pool.wait_ge(got_rec[u], i * 16 + 16)
                    pool.sem_inc(passed, 1)
                    pool.indirect_dma_start(
                        out=rows[:, u], out_offset=None, in_=table,
                        in_offset=bass.IndirectOffsetOnAxis(ap=rb[:, u, row_word:row_word + 1], axis=0),
                    ).then_inc(got_rows[u], 16)
            unrolled(pool, STEPS, body)

        @block.vector
        def _(dve):
            nc.vector.memset(agg_t[:] if with_attr else agg_t[:, :, NODES_PAD:], 0.0).then_inc(zeroed, 1)
            dve.wait_ge(zeroed, 1)

            def front(u, i, shift):
                dve.wait_ge(got_rec[u], i * 16 + 16)
                wait_steps_before(dve, summed, u, i, U)
                if with_attr:
                    nc.vector.tensor_scalar(pick[:, u], node_ids[:, bass.ds(shift, P)], rb[:, u, 1:2].bitcast(FP32),
                                            None, ALU.is_equal)
                    dve.wait_ge(got_rows[u], i * 16 + 16)
                    dve.wait_ge(edge_done[u], i + 1)
                    nc.vector.tensor_tensor(msg[:, u], rows[:, u], pe_edge[u % 2][:, 0:D], ALU.mult).then_inc(msg_done[u], 1)
                else:
                    nc.vector.tensor_scalar(pick[:, u], node_ids[:, bass.ds(shift, P)], rb[:, u, 0:1].bitcast(FP32),
                                            rb[:, u, 2:3].bitcast(FP32), ALU.is_equal, ALU.mult).then_inc(picked[u], 1)

            def back(u, i, shift):
                dve.wait_ge(summed[u], i + 1)
                wait_steps_before(dve, added, u, i, 1)
                at_tile = agg_t[:, :, bass.ds(shift, P)]
                nc.vector.tensor_tensor(at_tile, at_tile, pa[u % 2][:], ALU.add).then_inc(added[u], 1)

            def body(s0, i):
                shifts = []
                for u in range(U):
                    if u % 4 == 0:
                        shifts += numbers(EngineType.DVE, 1, s0 + u, TILES * P)
                    front(u, i, shifts[u])
                    if u:
                        back(u - 1, i, shifts[u - 1])
                back(U - 1, i, shifts[-1])
            unrolled(dve, STEPS, body)

        @block.tensor
        def _(pe):
            def edge(u, i):
                pe.wait_ge(got_at[u], i * 16 + 16)
                wait_steps_before(pe, msg_done, u, i, 2)
                nc.tensor.matmul(pe_edge[u % 2][:, 0:D], at[:, u], w_edge[:], start=True, stop=True).then_inc(edge_done[u], 1)

            def add_up(u, i):
                if with_attr:
                    pe.wait_ge(msg_done[u], i + 1)
                else:
                    pe.wait_ge(got_rows[u], i * 16 + 16)
                    pe.wait_ge(picked[u], i + 1)
                wait_steps_before(pe, added, u, i, 2)
                for k in range(KD):
                    last = nc.tensor.matmul(pa[u % 2][:, k], msg[:, u, k * P:(k + 1) * P], pick[:, u],
                                            start=True, stop=True)
                last.then_inc(summed[u], 1)

            def body(s0, i):
                for u in range(U):
                    if with_attr:
                        edge(u, i)
                        if u:
                            add_up(u - 1, i)
                    else:
                        add_up(u, i)
                if with_attr:
                    add_up(U - 1, i)
            unrolled(pe, STEPS, body)


@phase
def first_dense(c, agg_t, xn_t, w_rel, w_root, b_rel, gamma, beta, eps, scale, shift, beside=None):
    nc = c.nc
    with ExitStack() as ctx:
        ph = [[c.ps(ctx, f"fd_ph{u}{m}", [P, 512]) for m in range(KD)] for u in range(2)]
        st = c.sb(ctx, "fd_st", [P, KD, WIDES, 6], FP32)
        mv = c.sb(ctx, "fd_mv", [P, KD, 2], FP32)
        sd = c.sb(ctx, "fd_sd", [P, KD], FP32)
        rs = c.sb(ctx, "fd_rs", [P, KD], FP32)
        tmp = c.sb(ctx, "fd_tmp", [P, KD], FP32)
        multiplied = c.sem("fd_multiplied")
        relued = c.sem("fd_relued")
        passed = c.sem("fd_passed")
        stats = c.sem("fd_stats")
        small = c.sem("fd_small")
        root = c.sem("fd_root")
        block = ctx.enter_context(nc.Block())
        if beside is not None:
            beside(block)

        @block.tensor
        def _(pe):
            def body(g, u):
                if not (static(g) and g < 2):
                    pe.wait_ge(relued, g * 2 - 2)
                for m in range(KD):
                    steps = [(w, x, k) for w, x in ((w_rel, agg_t), (w_root, xn_t)) for k in range(KD)]
                    for n, (w, x, k) in enumerate(steps):
                        last = nc.tensor.matmul(ph[u][m][:, 0:WIDE], w[:, k, m * P:(m + 1) * P],
                                                x[:, k, bass.ds(g * WIDE, WIDE)], start=n == 0, stop=n == len(steps) - 1)
                last.then_inc(multiplied, 1)
            pairs(pe, WIDES, body)

        @block.scalar
        def _(act):
            def body(g, u):
                act.wait_ge(multiplied, g + 1)
                act.sem_inc(passed, 1)
                for m in range(KD):
                    nc.scalar.activation(agg_t[:, m, bass.ds(g * WIDE, WIDE)], ph[u][m][:, 0:WIDE], ACT.Relu,
                                         bias=b_rel[:, m:m + 1]).then_inc(relued, 1)
            pairs(act, WIDES, body)
            act.wait_ge(small, 1)
            nc.scalar.activation(sd[:], mv[:, :, 1], ACT.Sqrt, bias=eps[:, 0:1]).then_inc(root, 1)

        @block.vector
        def _(dve):
            for g in range(WIDES):
                n = min(WIDE, NODES - g * WIDE)
                dve.wait_ge(relued, g * 2 + 2)
                for m in range(KD):
                    last = nc.vector.bn_stats(st[:, m, g], agg_t[:, m, g * WIDE:g * WIDE + n])
            last.then_inc(stats, 1)
            dve.wait_ge(stats, 1)
            for m in range(KD):
                last = nc.vector.bn_aggr(mv[:, m], st[:, m].rearrange("p g s -> p (g s)"))
            last.then_inc(small, 1)
            dve.wait_ge(root, 1)
            nc.vector.reciprocal(rs[:], sd[:]).then_inc(small, 1)
            dve.wait_ge(small, 2)
            nc.vector.tensor_tensor(scale[:], rs[:], gamma[:], ALU.mult).then_inc(small, 1)
            dve.wait_ge(small, 3)
            nc.vector.tensor_tensor(tmp[:], mv[:, :, 0], scale[:], ALU.mult).then_inc(small, 1)
            dve.wait_ge(small, 4)
            nc.vector.tensor_tensor(shift[:], beta[:], tmp[:], ALU.subtract)


class RecordScatter:

    def __init__(self, c, ctx, posrec, rec1):
        self.c, self.posrec, self.rec1 = c, posrec, rec1
        self.stage = c.sb(ctx, "sr_stage", [P, 2, UNROLL, 1 + REC1], I32)
        self.at = 0

    def part(self, block, name, groups):
        c, stage, first = self.c, self.stage, self.at
        groups = min(groups, COLS // UNROLL - first)
        if groups < 1:
            return
        self.at += groups
        staged = c.sem(name + "_sr_staged")
        gone = [c.sem(f"{name}_sr_gone{u}") for u in range(2)]
        passed = c.sem(name + "_sr_passed")

        @block.gpsimd
        def _(pool):
            def body(g, u):
                if not (static(g) and g < 2):
                    pool.wait_ge(gone[u], (g // 2) * (16 * UNROLL))
                    pool.sem_inc(passed, 1)
                pool.tensor_copy(stage[:, u], self.posrec[:, bass.ds((g + first) * UNROLL, UNROLL)]).then_inc(staged, 1)
                pool.wait_ge(staged, g + 1)
                pool.sem_inc(passed, 1)
                for j in range(UNROLL):
                    pool.indirect_dma_start(
                        out=self.rec1, out_offset=bass.IndirectOffsetOnAxis(ap=stage[:, u, j, 0:1], axis=0),
                        in_=stage[:, u, j, 1:1 + REC1], in_offset=None,
                    ).then_inc(gone[u], 16)
            if groups == 1:
                body(0, 0)
            else:
                pairs(pool, groups, body)
                pool.wait_ge(gone[1], 16 * UNROLL * (groups // 2))
            pool.wait_ge(gone[0], 16 * UNROLL * ((groups + 1) // 2))


@phase
def degrees(c, posrec, dinv, dinv_row, ident, consts, beside):
    nc = c.nc
    with ExitStack() as ctx:
        hi_ids = c.sb(ctx, "dg_hi_ids", [P, TILES], FP32)
        lo_ids = c.sb(ctx, "dg_lo_ids", [P, P], FP32)
        s_i = c.sb(ctx, "dg_si", [P, COLS], I32)
        hl_i = c.sb(ctx, "dg_hli", [P, 2, COLS], I32)
        hl = c.sb(ctx, "dg_hl", [P, 2, COLS], FP32)
        lo = c.sb(ctx, "dg_lo", [P, 2, UNROLL, P], FP32)
        hi = c.sb(ctx, "dg_hi", [P, 2, UNROLL, TILES], FP32)
        hw = c.sb(ctx, "dg_hw", [P, 2, UNROLL, TILES], FP32)
        deg = c.sb(ctx, "dg_deg", [TILES, 2, P], FP32)
        sd = c.sb(ctx, "dg_sd", [TILES, P], FP32)
        pos = c.sb(ctx, "dg_pos", [TILES, P], FP32)
        inv = c.sb(ctx, "dg_inv", [TILES, P], FP32)
        by_tile = c.sb(ctx, "dg_by_tile", [TILES, P], FP32)
        pd = c.ps(ctx, "dg_pd", [P, 512])
        pt = c.ps(ctx, "dg_pt", [P, 512])
        ids_set = c.sem("dg_ids_set")
        split = c.sem("dg_split")
        made = c.sem("dg_made")
        weighted = c.sem("dg_weighted")
        multiplied = c.sem("dg_multiplied")
        small = c.sem("dg_small")
        root = c.sem("dg_root")
        stored = c.sem("dg_stored")
        block = ctx.enter_context(nc.Block())
        beside(block)
        ew = posrec[:, :, 3].bitcast(FP32)

        @block.vector
        def _(dve):
            nc.vector.tensor_copy(s_i[:], posrec[:, :, 1].bitcast(FP32)).then_inc(split, 1)
            nc.vector.tensor_copy(lo_ids[:], consts["node_ids"][:, 0:P])
            nc.vector.tensor_copy(hi_ids[:], consts["node_ids"][:, 0:TILES])
            dve.wait_ge(split, 1)
            nc.vector.tensor_scalar(hl_i[:, 0], s_i[:], 7, None, ALU.arith_shift_right)
            nc.vector.tensor_scalar(hl_i[:, 1], s_i[:], P - 1, None, ALU.bitwise_and).then_inc(split, 1)
            dve.wait_ge(split, 2)
            nc.vector.tensor_copy(hl[:], hl_i[:]).then_inc(split, 1)
            dve.wait_ge(split, 3)

            def body(g, u):
                if not (static(g) and g < 2):
                    dve.wait_ge(multiplied, g - 1)
                j = bass.ds(g * UNROLL, UNROLL)
                nc.vector.tensor_tensor(lo[:, u], lo_ids[:].unsqueeze(1).broadcast_to([P, UNROLL, P]),
                                        hl[:, 1, j].unsqueeze(2).broadcast_to([P, UNROLL, P]), ALU.is_equal)
                nc.vector.tensor_tensor(hi[:, u], hi_ids[:].unsqueeze(1).broadcast_to([P, UNROLL, TILES]),
                                        hl[:, 0, j].unsqueeze(2).broadcast_to([P, UNROLL, TILES]), ALU.is_equal).then_inc(made, 1)
                dve.wait_ge(made, g + 1)
                nc.vector.tensor_tensor(hw[:, u], hi[:, u], ew[:, j].unsqueeze(2).broadcast_to([P, UNROLL, TILES]),
                                        ALU.mult).then_inc(weighted, 1)
            pairs(dve, COLS // UNROLL, body)
            dve.wait_ge(multiplied, COLS // UNROLL)
            nc.vector.tensor_scalar(deg[:, 0], pd[0:TILES, 0:P], 1.0, None, ALU.add).then_inc(small, 1)
            dve.wait_ge(small, 1)
            nc.vector.tensor_scalar(deg[:, 1], deg[:, 0], 1e-30, None, ALU.max).then_inc(small, 1)
            nc.vector.tensor_scalar(pos[:], deg[:, 0], 0.0, None, ALU.is_gt)
            dve.wait_ge(root, 1)
            nc.vector.reciprocal(inv[:], sd[:]).then_inc(small, 1)
            dve.wait_ge(small, 3)
            nc.vector.tensor_tensor(by_tile[:], inv[:], pos[:], ALU.mult).then_inc(small, 1)
            dve.wait_ge(multiplied, COLS // UNROLL + 1)
            nc.vector.tensor_copy(dinv[:], pt[:, 0:TILES])

        @block.scalar
        def _(act):
            act.wait_ge(small, 2)
            nc.scalar.activation(sd[:], deg[:, 1], ACT.Sqrt).then_inc(root, 1)
            act.wait_ge(small, 4)
            act.dma_start(dinv_row.rearrange("(t p) -> t p", p=P), by_tile[:]).then_inc(stored, 16)
            act.wait_ge(stored, 16)

        @block.tensor
        def _(pe):
            def body(g, u):
                pe.wait_ge(weighted, g + 1)
                for j in range(UNROLL):
                    last = nc.tensor.matmul(pd[0:TILES, 0:P], hw[:, u, j], lo[:, u, j],
                                            start=static(g) and g == 0 and j == 0, stop=False, skip_group_check=True)
                last.then_inc(multiplied, 1)
            pairs(pe, COLS // UNROLL, body)
            pe.wait_ge(small, 4)
            nc.tensor.transpose(pt[:, 0:TILES], by_tile[:], ident[0:TILES, 0:TILES]).then_inc(multiplied, 1)


@phase
def second_dense(c, agg_t, dinv_b, w, b, w1, b1):
    nc = c.nc
    with ExitStack() as ctx:
        ph = [[c.ps(ctx, f"sd_ph{s}{m}", [P, 512]) for m in range(KD)] for s in range(2)]
        h7 = c.sb(ctx, "sd_h7", [P, KD, WIDE], FP32)
        scaled = c.sem("sd_scaled")
        first = c.sem("sd_first")
        second = c.sem("sd_second")
        h7_done = c.sem("sd_h7_done")
        out_done = c.sem("sd_out_done")
        passed = c.sem("sd_passed")
        block = ctx.enter_context(nc.Block())

        @block.vector
        def _(dve):
            def body(g, u):
                n = bass.ds(g * WIDE, WIDE)
                nc.vector.tensor_tensor(agg_t[:, :, n], agg_t[:, :, n],
                                        dinv_b[:, n].unsqueeze(1).broadcast_to([P, KD, WIDE]), ALU.mult).then_inc(scaled, 1)
            pairs(dve, WIDES, body)

        @block.tensor
        def _(pe):
            def body(g, u):
                pe.wait_ge(scaled, g + 1)
                if not (static(g) and g < 1):
                    pe.wait_ge(h7_done, g * 2)
                for m in range(KD):
                    for k in range(KD):
                        last = nc.tensor.matmul(ph[0][m][:, 0:WIDE], w[:, k, m * P:(m + 1) * P],
                                                agg_t[:, k, bass.ds(g * WIDE, WIDE)], start=k == 0, stop=k == KD - 1)
                last.then_inc(first, 1)
                pe.wait_ge(h7_done, g * 2 + 2)
                if not (static(g) and g < 1):
                    pe.wait_ge(out_done, g * 2)
                for m in range(KD):
                    for k in range(KD):
                        last = nc.tensor.matmul(ph[1][m][:, 0:WIDE], w1[:, k, m * P:(m + 1) * P], h7[:, k],
                                                start=k == 0, stop=k == KD - 1)
                last.then_inc(second, 1)
            pairs(pe, WIDES, body)

        @block.scalar
        def _(act):
            def body(g, u):
                act.wait_ge(first, g + 1)
                if not (static(g) and g < 1):
                    act.wait_ge(second, g)
                for m in range(KD):
                    nc.scalar.activation(h7[:, m], ph[0][m][:, 0:WIDE], ACT.Identity, bias=b[:, m:m + 1]).then_inc(h7_done, 1)
                act.wait_ge(second, g + 1)
                act.sem_inc(passed, 1)
                for m in range(KD):
                    nc.scalar.activation(agg_t[:, m, bass.ds(g * WIDE, WIDE)], ph[1][m][:, 0:WIDE], ACT.Relu,
                                         bias=b1[:, m:m + 1]).then_inc(out_done, 1)
            pairs(act, WIDES, body)


@phase
def choose(c, name, scores, top, chunks, consts, place, expert, prob=None, beside=None):
    nc = c.nc
    E = EXPERTS
    with ExitStack() as ctx:
        s = scores
        won = c.sb(ctx, name + "_won", [P, E, TILES, E], FP32)
        order = c.sb(ctx, name + "_order", [P, TILES, E], FP32)
        mask = c.sb(ctx, name + "_mask", [P, TILES, E], FP32)
        tot = c.sb(ctx, name + "_tot", [P, TILES, E], FP32)
        upto = c.sb(ctx, name + "_upto", [P, E, TILES], FP32)
        row = c.sb(ctx, name + "_row", [P, 4, TILES, E], FP32)
        unit = c.sb(ctx, name + "_unit", [P, TILES], FP32)
        n_i = c.sb(ctx, name + "_ni", [P, 2, E], I32)
        n_f = c.sb(ctx, name + "_nf", [P, 4, E], FP32)
        ge = c.sb(ctx, name + "_ge", [1, E, chunks], FP32)
        ex = c.sb(ctx, name + "_ex", [1, 2, chunks], FP32)
        pick = c.sb(ctx, name + "_pick", [P, 3, TILES], FP32)
        probs = c.sb(ctx, name + "_probs", [P, 4, TILES, E], FP32)
        pk = c.ps(ctx, name + "_pk", [P, 512])
        pn = c.ps(ctx, name + "_pn", [P, 512])
        done = c.sem(name + "_done")
        counted = c.sem(name + "_counted")
        raised = c.sem(name + "_raised")
        block = ctx.enter_context(nc.Block())
        if beside is not None:
            beside(block)

        @block.scalar
        def _(act):
            if prob is not None:
                act.wait_ge(done, 2)
                nc.scalar.activation(probs[:, 1], probs[:, 0], ACT.Exp).then_inc(raised, 1)

        @block.vector
        def _(dve):
            n = [0]

            def then(ins):
                n[0] += 1
                ins.then_inc(done, 1)
                dve.wait_ge(done, n[0])

            if prob is not None:
                then(nc.vector.tensor_reduce(pick[:, 0], s[:], AX.X, ALU.max))
                then(nc.vector.tensor_tensor(probs[:, 0], s[:], pick[:, 0].unsqueeze(2).broadcast_to([P, TILES, E]), ALU.subtract))
                dve.wait_ge(raised, 1)
                then(nc.vector.reduce_sum(pick[:, 1], probs[:, 1], AX.X))
                then(nc.vector.reciprocal(pick[:, 2], pick[:, 1]))
                then(nc.vector.tensor_tensor(probs[:, 2], probs[:, 1], pick[:, 2].unsqueeze(2).broadcast_to([P, TILES, E]), ALU.mult))
                by = probs[:, 2]
            else:
                by = s[:]
            then(nc.vector.memset(won[:], 0.0))
            for j in range(E):
                if j + 1 < E:
                    nc.vector.tensor_tensor(won[:, j, :, j + 1:E], by[:, :, j:j + 1].broadcast_to([P, TILES, E - 1 - j]),
                                            by[:, :, j + 1:E], ALU.is_ge)
                if j:
                    nc.vector.tensor_tensor(won[:, j, :, 0:j], by[:, :, j:j + 1].broadcast_to([P, TILES, j]),
                                            by[:, :, 0:j], ALU.is_gt)
            then(nc.vector.memset(unit[:], 1.0))
            then(nc.vector.reduce_sum(order[:], won[:].rearrange("p j t e -> p t e j"), AX.X))
            then(nc.vector.tensor_scalar(mask[:], order[:], float(top), None, ALU.is_lt))
            if prob is not None:
                then(nc.vector.tensor_tensor(probs[:, 3], probs[:, 2], mask[:], ALU.mult))
                then(nc.vector.reduce_sum(prob[:], probs[:, 3], AX.X))
            dve.wait_ge(counted, 1)
            then(nc.vector.tensor_copy(tot[:], pn[:, 0:TILES * E].rearrange("p (t e) -> p t e", e=E)))
            for e in range(E):
                last = nc.vector.tensor_tensor_scan(upto[:, e], unit[:], tot[:, :, e], 0.0, ALU.mult, ALU.add)
            then(last)
            then(nc.vector.tensor_scalar(n_i[:, 0], upto[:, :, TILES - 1], float(P - 1), None, ALU.add))
            then(nc.vector.tensor_scalar(n_i[:, 1], n_i[:, 0], 7, None, ALU.arith_shift_right))
            then(nc.vector.tensor_copy(n_f[:, 0], n_i[:, 1]))
            then(nc.vector.tensor_tensor_scan(n_f[:, 1], unit[:, 0:E], n_f[:, 0], 0.0, ALU.mult, ALU.add))
            then(nc.vector.tensor_tensor(n_f[:, 2], n_f[:, 1], n_f[:, 0], ALU.subtract))
            then(nc.vector.tensor_scalar(n_f[:, 3], n_f[:, 2], float(P), None, ALU.mult))
            then(nc.vector.tensor_tensor(row[:, 0], upto[:].rearrange("p e t -> p t e"), tot[:], ALU.subtract))
            then(nc.vector.tensor_tensor(row[:, 1], row[:, 0], n_f[:, 3].unsqueeze(1).broadcast_to([P, TILES, E]), ALU.add))
            then(nc.vector.tensor_tensor(row[:, 2], row[:, 1], pk[:, 0:TILES * E].rearrange("p (t e) -> p t e", e=E), ALU.add))
            then(nc.vector.tensor_tensor(row[:, 3], row[:, 2], mask[:], ALU.mult))
            then(nc.vector.tensor_reduce(won[:, 0, :, 0], row[:, 3], AX.X, ALU.max))
            if top == 1:
                then(nc.vector.tensor_copy(place[:, :, 0], won[:, 0, :, 0]))
            else:
                then(nc.vector.reduce_sum(won[:, 1, :, 0], row[:, 3], AX.X))
                nc.vector.tensor_copy(place[:, :, 1], won[:, 0, :, 0])
                then(nc.vector.tensor_tensor(place[:, :, 0], won[:, 1, :, 0], won[:, 0, :, 0], ALU.subtract))
            for e in range(E):
                last = nc.vector.tensor_scalar(ge[:, e], consts["node_ids"][0:1, 0:chunks], n_f[0:1, 2, e:e + 1], None, ALU.is_ge)
            then(last)
            then(nc.vector.reduce_sum(ex[:, 0], ge[:].rearrange("p e c -> p c e"), AX.X))
            then(nc.vector.tensor_scalar(expert[:], ex[:, 0], -1.0, None, ALU.add))

        @block.tensor
        def _(pe):
            pe.wait_ge(done, (6 if prob is not None else 1) + 3)
            m = mask[:].rearrange("p t e -> p (t e)")
            nc.tensor.matmul(pk[:, 0:TILES * E], consts["earlier"][:], m, start=True, stop=True)
            nc.tensor.matmul(pn[:, 0:TILES * E], consts["ones"][:], m, start=True, stop=True).then_inc(counted, 1)


@phase
def dispatch(c, name, xn, place, top, xs, beside=None):
    nc = c.nc
    with ExitStack() as ctx:
        x = c.sb(ctx, name + "_x", [P, 2, GROUP, D], FP32)
        at = c.sb(ctx, name + "_at", [P, 2, GROUP, top], I32)
        loaded = [c.sem(f"{name}_loaded{u}") for u in range(2)]
        gone = [c.sem(f"{name}_gone{u}") for u in range(2)]
        staged = c.sem(name + "_staged")
        passed = c.sem(name + "_passed")
        block = ctx.enter_context(nc.Block())
        if beside is not None:
            beside(block)
        per = 16 * GROUP * top

        @block.sync
        def _(sp):
            def body(g, u):
                if not (static(g) and g < 2):
                    sp.wait_ge(gone[u], (g // 2) * per)
                sp.dma_start(x[:, u], tiles_view(xn)[bass.ds(g, 1)].rearrange("o p a d -> p (o a) d")).then_inc(loaded[u], 16)
            pairs(sp, GROUPS, body)

        @block.gpsimd
        def _(pool):
            def body(g, u):
                if old(g, 2):
                    pool.wait_ge(gone[u], (g // 2) * per)
                    pool.sem_inc(passed, 1)
                pool.tensor_copy(at[:, u], place[:, bass.ds(g * GROUP, GROUP)]).then_inc(staged, 1)
                pool.wait_ge(loaded[u], (g // 2) * 16 + 16)
                pool.sem_inc(passed, 1)
                pool.wait_ge(staged, g + 1)
                pool.sem_inc(passed, 1)
                for t in range(GROUP):
                    for k in range(top):
                        pool.indirect_dma_start(
                            out=xs, out_offset=bass.IndirectOffsetOnAxis(ap=at[:, u, t, k:k + 1], axis=0),
                            in_=x[:, u, t], in_offset=None).then_inc(gone[u], 16)
            pairs(pool, GROUPS, body)
            pool.wait_ge(gone[0], per * ((GROUPS + 1) // 2))
            pool.wait_ge(gone[1], per * (GROUPS // 2))


@phase
def experts(c, name, xs, ys, chunks, expert, ident, hid, w1, b1, w2, b2, beside=None):
    nc = c.nc
    nh = hid // 512
    kh = hid // P
    own = b1 is None
    with ExitStack() as ctx:
        x = c.sb(ctx, name + "_x", [P, 2, D], FP32)
        x_t = c.sb(ctx, name + "_xt", [P, 2, KD, P], FP32)
        h_t = c.sb(ctx, name + "_ht", [P, 2, kh, P], FP32)
        y = c.sb(ctx, name + "_y", [P, 2, D], FP32)
        px = [c.ps(ctx, f"{name}_px{u}", [P, KD, P]) for u in range(2)]
        ph = [[c.ps(ctx, f"{name}_ph{u}{b}", [P, 4, P]) for b in range(nh)] for u in range(2)]
        po = [c.ps(ctx, f"{name}_po{u}", [P, 512]) for u in range(2)]
        loaded = [c.sem(f"{name}_loaded{u}") for u in range(2)]
        stored = [c.sem(f"{name}_stored{u}") for u in range(2)]
        x_turned = c.sem(name + "_x_turned")
        x_copied = c.sem(name + "_x_copied")
        up = c.sem(name + "_up")
        active = c.sem(name + "_active")
        down = c.sem(name + "_down")
        out_done = c.sem(name + "_out_done")
        passed = c.sem(name + "_passed")
        if own:
            w_own = c.sb(ctx, name + "_w_own", [P, 2, KD * hid + kh], FP32)
            fetched = c.sem(name + "_fetched")
        block = ctx.enter_context(nc.Block())
        if beside is not None:
            beside(block)

        def stages(eng, body):
            for s in range(4):
                body(s, s % 2)
            with eng.Fori(2, chunks // 2) as i:
                body(i * 2, 0)
                body(i * 2 + 1, 1)
            for s in range(chunks, chunks + 2):
                body(s, s % 2)

        def runs(n):
            return not static(n) or 0 <= n < chunks

        def number(eng, n):
            return eng.value_load(expert[0:1, bass.ds(n, 1)], min_val=0, max_val=EXPERTS - 1)

        @block.sync
        def _(sp):
            def body(n, u):
                if old(n, 2):
                    sp.wait_ge(x_turned, n - 1)
                sp.dma_start(x[:, u], xs[bass.ds(n * P, P), :]).then_inc(loaded[u], 16)
            pairs(sp, chunks, body)

        @block.tensor
        def _(pe):
            def body(s, u):
                if runs(s):
                    pe.wait_ge(loaded[u], (s // 2) * 16 + 16)
                    if old(s, 2):
                        pe.wait_ge(x_copied, s - 1)
                    for k in range(KD):
                        last = nc.tensor.transpose(px[u][:, k], x[:, u, k * P:(k + 1) * P], ident[:])
                    last.then_inc(x_turned, 1)
                n, v = s - 1, 1 - u
                if runs(n):
                    pe.wait_ge(x_copied, n + 1)
                    if own:
                        pe.wait_ge(fetched, n + 1)
                    for b in range(nh):
                        if old(n, 2):
                            pe.wait_ge(active, n * nh + (b + 1 - 2 * nh))
                        for m in range(b * 4, b * 4 + 4):
                            for k in range(KD):
                                w = w_own[:, v, k * hid + m * P:k * hid + m * P + P] if own else w1[:, k, m * P:(m + 1) * P]
                                last = nc.tensor.matmul(ph[v][b][:, m % 4], w, x_t[:, v, k], start=k == 0, stop=k == KD - 1)
                        last.then_inc(up, 1)
                n, v = s - 2, u
                if runs(n):
                    e = number(pe, n)
                    if old(n, 2):
                        pe.wait_ge(out_done, n - 1)
                    for m in range(kh):
                        if m % 4 == 0:
                            pe.wait_ge(active, n * nh + (m // 4 + 1))
                        last = nc.tensor.matmul(po[v][:, 0:D], h_t[:, v, m],
                                                w2[:, bass.ds(e, 1), m].rearrange("p o n -> p (o n)"),
                                                start=m == 0, stop=m == kh - 1)
                    last.then_inc(down, 1)
            stages(pe, body)

        @block.scalar
        def _(act):
            def body(s, u):
                n, v = s - 1, 1 - u
                if runs(n):
                    for b in range(nh):
                        act.wait_ge(up, n * nh + (b + 1))
                        if old(n, 2) and b == 0:
                            act.wait_ge(down, n - 1)
                        for m in range(b * 4, b * 4 + 4):
                            bias = w_own[:, v, KD * hid + m:KD * hid + m + 1] if own else b1[:, m:m + 1]
                            last = nc.scalar.activation(h_t[:, v, m], ph[v][b][:, m % 4], ACT.Gelu, bias=bias)
                        last.then_inc(active, 1)
                n, v = s - 2, u
                if runs(n):
                    act.wait_ge(out_done, n + 1)
                    act.sem_inc(passed, 1)
                    act.dma_start(ys[bass.ds(n * P, P), :], y[:, v]).then_inc(stored[v], 16)
            stages(act, body)
            for v in range(2):
                act.wait_ge(stored[v], 16 * (chunks // 2))

        @block.vector
        def _(dve):
            def body(s, u):
                if runs(s):
                    if own:
                        e = number(dve, s)
                        if old(s, 2):
                            dve.wait_ge(active, s * nh + (nh - 2 * nh))
                            dve.sem_inc(passed, 1)
                        nc.vector.tensor_copy(w_own[:, u], w1[:, bass.ds(e, 1)].rearrange("p o n -> p (o n)")).then_inc(fetched, 1)
                    dve.wait_ge(x_turned, s + 1)
                    if old(s, 2):
                        dve.wait_ge(up, s * nh + (nh - 2 * nh))
                    nc.vector.tensor_copy(x_t[:, u], px[u][:]).then_inc(x_copied, 1)
                n, v = s - 2, u
                if runs(n):
                    e = number(dve, n)
                    dve.wait_ge(down, n + 1)
                    if old(n, 2):
                        dve.wait_ge(stored[v], (n // 2) * 16)
                    nc.vector.tensor_tensor(y[:, v], po[v][:, 0:D], b2[:, bass.ds(e, 1)].rearrange("p o n -> p (o n)"),
                                            ALU.add).then_inc(out_done, 1)
            stages(dve, body)


@phase
def load_all(c, name, items):
    nc = c.nc
    loaded = c.sem(name + "_loaded")
    with ExitStack() as ctx:
        block = ctx.enter_context(nc.Block())

        @block.sync
        def _(sp):
            for tile, src in items:
                sp.dma_start(tile, src).then_inc(loaded, 16)
            sp.wait_ge(loaded, 16 * len(items))


def const_arrays():
    q = np.arange(P)
    half, tile = q // 64, q % 64
    f = np.float32
    return {
        "bucket": tile[:, None].astype(f),
        "fold": (tile[:, None] == q[None, :]).astype(f),
        "before": ((tile[:, None] < tile[None, :]) | ((tile[:, None] == tile[None, :]) & (half[:, None] < half[None, :]))).astype(f),
        "lower": ((q[:, None] < q[None, :]) & (q[:, None] < 64)).astype(f),
        "diff": ((q[:, None] == q[None, :]).astype(f) - (q[:, None] == q[None, :] - 1).astype(f)),
        "steps": np.arange(STEPS, dtype=f)[None, :],
        "node_ids": np.arange(SLOTS * P, dtype=f)[None, :],
        "earlier": (q[:, None] < q[None, :]).astype(f),
        "ident": np.eye(P, dtype=f),
        "halves": (half[:, None] == np.arange(HALVES)[None, :]).astype(f),
    }


def weights_view(w):
    return w.rearrange("(k p) n -> p k n", p=P)


def row_view(b, n):
    return b.rearrange("(o n) -> o n", o=1).broadcast_to([P, n])


def all_rows(b):
    e, n = b.shape
    return b.rearrange("(o e) n -> o e n", o=1).broadcast_to([P, e, n])


def program(nc, a, out):
    with ExitStack() as ctx:
        c = Core(nc, ctx)
        rows = {k: c.dram(k, [NODES_PAD, D], FP32) for k in ("xn0", "x1", "xn1", "x2", "y2", "x3", "xn3")}
        ids_src = c.dram("ids_src", [EDGES_PAD], BF16)
        ids_dst = c.dram("ids_dst", [EDGES_PAD], BF16)
        rec0 = c.dram("rec0", [EDGES_PAD, REC0], I32)
        rec1 = c.dram("rec1", [EDGES_PAD, REC1], I32)
        dinv_row = c.dram("dinv_row", [NODES_PAD], FP32)
        pos_flat = c.dram("pos_flat", [EDGES_PAD], FP32)
        xs = [c.dram(f"xs{i}", [n * P, D], FP32) for i, n in enumerate((CHUNKS0, CHUNKS1))]
        ys = [c.dram(f"ys{i}", [n * P, D], FP32) for i, n in enumerate((CHUNKS0, CHUNKS1))]

        ident = c.sb(ctx, "ident", [P, P], FP32)
        eps = c.sb(ctx, "eps", [P, 1], FP32)
        ones = c.sb(ctx, "ones", [P, P], FP32)
        halves = c.sb(ctx, "halves", [P, HALVES], FP32)
        bucket = c.sb(ctx, "bucket", [P, 1], FP32)
        earlier = c.sb(ctx, "earlier", [P, P], FP32)
        node_ids = c.sb(ctx, "node_ids", [P, SLOTS * P], FP32)
        dinv = c.sb(ctx, "dinv", [P, TILES], FP32)
        base = [c.sb(ctx, f"base{i}", [P, 1], FP32) for i in range(2)]
        tab = [c.sb(ctx, f"tab{i}", [1, 2, STEPS], I32) for i in range(2)]
        scores = c.sb(ctx, "scores", [P, TILES, EXPERTS], FP32)
        mv = c.sb(ctx, "mv", [P, TILES, 2], FP32)
        place0 = c.sb(ctx, "place0", [P, TILES, TOP0], I32)
        consts = {"ident": ident, "ones": ones, "halves": halves, "bucket": bucket, "earlier": earlier, "node_ids": node_ids}
        set_const = c.sem("set_const")
        posrec = c.sb(ctx, "posrec", [P, COLS, 1 + REC1], I32)
        with ExitStack() as ctx_c:
            for k, n in (("fold", P), ("before", P), ("lower", P), ("diff", P), ("steps", STEPS)):
                consts[k] = c.sb(ctx_c, k, [P, n], FP32)
            widths = {"steps": STEPS, "node_ids": SLOTS * P}
            load_all(c, "const", [(consts[k][:], a[k].broadcast_to([P, widths[k]]) if k in widths else a[k])
                                  for k in ("ident", "halves", "bucket", "earlier", "node_ids", "fold", "before", "lower",
                                            "diff", "steps")])
            zeros = c.sb(ctx_c, "zeros", [P, CHUNKS0 * D // 4], FP32)
            with nc.Block() as block:
                @block.vector
                def _(dve):
                    nc.vector.memset(ones[:], 1.0).then_inc(set_const, 1)
                    nc.vector.memset(eps[:], EPS).then_inc(set_const, 1)
                    nc.vector.memset(zeros[:], 0.0).then_inc(set_const, 1)
                    dve.wait_ge(set_const, 3)

            filling = Prefetch(c, "fill", [(xs[i].rearrange("(p r) d -> p (r d)", p=P)[:, j * n * D // 4:(j + 1) * n * D // 4],
                                            zeros[:, 0:n * D // 4])
                                           for i, n in enumerate((CHUNKS0, CHUNKS1)) for j in range(4)])
            tile_ids(c, a["src"], a["dst"], ids_src, ids_dst, rec0, posrec, a["src_cols"], a["dst_cols"], a["ew_cols"],
                     beside=filling.start)
            count(c, "cd", ids_dst, consts, tab[0], base[0])
            count(c, "cs", ids_src, consts, tab[1], base[1])
            rank(c, "rk", ids_src, consts, base[1], posrec, ident, pos_flat, beside=filling.finish)
        scatter = RecordScatter(c, ctx, posrec, rec1)
        degrees(c, posrec, dinv, dinv_row, ident, consts, beside=lambda b: scatter.part(b, "dg", 13))

        with ExitStack() as ctx_g:
            agg_t = c.sb(ctx_g, "agg_t", [P, KD, SLOTS * P], FP32)
            xn_t = c.sb(ctx_g, "xn_t", [P, KD, NODES_PAD], FP32)
            rows_pass(c, "ln0", a["x"], norm=(eps, None, rows["xn0"], xn_t, ident), beside=lambda b: scatter.part(b, "ln0", 3))
            with ExitStack() as ctx_w:
                w_edge = c.sb(ctx_w, "w_edge", [ATTR, D], FP32)
                load_all(c, "l0e", [(w_edge[:], a["L0_gnn_W_edge"])])
                aggregate_edges(c, "e0", rows["xn0"], rec0, REC0, tab[0], node_ids, agg_t, a["attr_t"], w_edge)
            w = {k: c.sb(ctx_g, k, [P, KD, D], FP32) for k in ("w_rel", "w_root", "w_res")}
            v = {k: c.sb(ctx_g, k, [P, KD], FP32) for k in ("b_rel", "gamma", "beta")}
            scale = c.sb(ctx_g, "bn_scale", [P, KD], FP32)
            shift = c.sb(ctx_g, "bn_shift", [P, KD], FP32)
            load_all(c, "l0d", [(w["w_rel"][:], weights_view(a["L0_gnn_W_rel"])), (w["w_root"][:], weights_view(a["L0_gnn_W_root"])),
                                (w["w_res"][:], weights_view(a["L0_gnn_W_res"])), (v["b_rel"][:], a["L0_gnn_b_rel"]),
                                (v["gamma"][:], a["L0_gnn_gamma"]), (v["beta"][:], a["L0_gnn_beta"])])
            first_dense(c, agg_t, xn_t, w["w_rel"], w["w_root"], v["b_rel"], v["gamma"], v["beta"], eps, scale, shift,
                        beside=lambda b: scatter.part(b, "fd", 5))
            finish_graph(c, "o0", a["x"], agg_t, w["w_res"], ident, mv, rows["x1"], xn_t, scale, shift,
                         beside=lambda b: scatter.part(b, "o0", 7))

        with ExitStack() as ctx_f:
            place = place0
            expert = c.sb(ctx_f, "expert0", [1, CHUNKS0], I32)
            wg = c.sb(ctx_f, "wg0", [P, KD, EXPERTS], FP32)
            bg = c.sb(ctx_f, "bg0", [P, EXPERTS], FP32)
            load_all(c, "l0g", [(wg[:], weights_view(a["L0_ffn_Wg"])), (bg[:], row_view(a["L0_ffn_bg"], EXPERTS))])
            gate_pass(c, "g0", rows["x1"], mv, eps, rows["xn1"], scores, ident, wg, bg,
                      beside=lambda b: scatter.part(b, "g0", 4))
            w1 = c.sb(ctx_f, "w1_0", [P, EXPERTS, KD * HID0 + HID0 // P], FP32)
            w2 = c.sb(ctx_f, "w2_0", [P, EXPERTS, HID0 // P, D], FP32)
            b2 = c.sb(ctx_f, "b2_0", [P, EXPERTS, D], FP32)
            fetch = Prefetch(c, "l0x", [(w1[:, :, k * HID0:(k + 1) * HID0], a["L0_ffn_W1"].rearrange("e (k p) n -> k p e n", p=P)[k]) for k in range(KD)]
                             + [(w1[:, :, KD * HID0:], a["b1_experts"]),
                                        (w2[:], a["L0_ffn_W2"].rearrange("e (k p) n -> p e k n", p=P)), (b2[:], all_rows(a["L0_ffn_b2"]))])

            def while_choosing(block):
                fetch.start(block)
                scatter.part(block, "c0", 2)
            choose(c, "c0", scores, TOP0, CHUNKS0, consts, place, expert, beside=while_choosing)
            dispatch(c, "d0", rows["xn1"], place, TOP0, xs[0], beside=fetch.finish)
            experts(c, "x0", xs[0], ys[0], CHUNKS0, expert, ident, HID0, w1, None, w2, b2,
                    beside=lambda b: scatter.part(b, "x0", COLS))
        with ExitStack() as ctx_g:
            agg_t = c.sb(ctx_g, "agg_t2", [P, KD, SLOTS * P], FP32)
            rows_pass(c, "m0", rows["x1"], ys[0], place0, TOP0, x_out=rows["x2"], norm=(eps, dinv, rows["y2"], agg_t, ident))
            w = {k: c.sb(ctx_g, "s" + k, [P, KD, D], FP32) for k in ("W", "W1", "W2")}
            v = {k: c.sb(ctx_g, "s" + k, [P, KD], FP32) for k in ("b", "b1")}
            b2 = c.sb(ctx_g, "sb2", [P, D], FP32)
            dinv_b = c.sb(ctx_g, "dinv_b", [P, NODES_PAD], FP32)
            fetch = Prefetch(c, "l1d", [(w[k][:], weights_view(a["L1_gnn_" + k])) for k in w] + [(v[k][:], a["L1_gnn_" + k]) for k in v]
                             + [(b2[:], row_view(a["L1_gnn_b2"], D)), (dinv_b[:], row_view(dinv_row, NODES_PAD))])

            def while_adding(block):
                fetch.start(block)
                fetch.finish(block)
            aggregate_edges(c, "e1", rows["y2"], rec1, REC1, tab[1], node_ids, agg_t, beside=while_adding)
            second_dense(c, agg_t, dinv_b, w["W"], v["b"], w["W1"], v["b1"])
            finish_graph(c, "o1", rows["x2"], agg_t, w["W2"], ident, mv, rows["x3"], b_row=b2)

        with ExitStack() as ctx_f:
            place = c.sb(ctx_f, "place1", [P, TILES, TOP1], I32)
            prob = c.sb(ctx_f, "prob", [P, TILES], FP32)
            expert = c.sb(ctx_f, "expert1", [1, CHUNKS1], I32)
            w1 = c.sb(ctx_f, "w1_1", [P, KD, HID1], FP32)
            b1 = c.sb(ctx_f, "b1_1", [P, HID1 // P], FP32)
            wg = c.sb(ctx_f, "wg1", [P, HID1 // P, EXPERTS], FP32)
            bg = c.sb(ctx_f, "bg1", [P, EXPERTS], FP32)
            w2 = c.sb(ctx_f, "w2_1", [P, EXPERTS, HID1 // P, D], FP32)
            b2 = c.sb(ctx_f, "b2_1", [P, EXPERTS, D], FP32)
            load_all(c, "l1g", [(wg[:], weights_view(a["L1_ffn_Wg"])), (bg[:], row_view(a["L1_ffn_bg"], EXPERTS)),
                                (w1[:], weights_view(a["L1_ffn_W1"])), (b1[:], a["b1_cols"])])
            gate_pass(c, "g1", rows["x3"], mv, eps, rows["xn3"], scores, ident, wg, bg, w1, b1)
            fetch = Prefetch(c, "l1x", [(w2[:], a["L1_ffn_Wd"].rearrange("e (k p) n -> p e k n", p=P)), (b2[:], all_rows(a["L1_ffn_bd"]))])
            choose(c, "c1", scores, TOP1, CHUNKS1, consts, place, expert, prob, beside=fetch.start)
            dispatch(c, "d1", rows["xn3"], place, TOP1, xs[1], beside=fetch.finish)
            experts(c, "x1", xs[1], ys[1], CHUNKS1, expert, ident, HID1, w1, b1, w2, b2)
            rows_pass(c, "m1", rows["x3"], ys[1], place, TOP1, prob, out)


def kernel(**inputs):
    import concourse.bacc as bacc
    from concourse.bass_utils import run_bass_kernel_spmd as run

    nc = bacc.Bacc("TRN2", target_bir_lowering=False, num_devices=1)
    arrays = {k: np.ascontiguousarray(v) for k, v in inputs.items()}
    x, src, dst = arrays.pop("x"), arrays.pop("src"), arrays.pop("dst")
    attr, ew = arrays.pop("edge_attr_64"), arrays.pop("edge_weight")
    more = EDGES_PAD - EDGES
    arrays["x"] = np.concatenate([x, np.zeros((NODES_PAD - NODES, D), x.dtype)])
    arrays["src"] = np.concatenate([src, np.full(more, NODES_PAD, src.dtype)])
    arrays["dst"] = np.concatenate([dst, np.full(more, NODES_PAD, dst.dtype)])
    arrays["attr_t"] = np.ascontiguousarray(np.concatenate([attr, np.zeros((more, ATTR), attr.dtype)]).T)
    ew = np.concatenate([ew, np.zeros(more, ew.dtype)])
    for name, v in (("src_cols", arrays["src"]), ("dst_cols", arrays["dst"]), ("ew_cols", ew)):
        arrays[name] = np.ascontiguousarray(v.reshape(COLS, P).T)
    arrays["b1_cols"] = np.ascontiguousarray(arrays["L1_ffn_b1"].reshape(HID1 // P, P).T)
    arrays["b1_experts"] = np.ascontiguousarray(arrays["L0_ffn_b1"].reshape(EXPERTS, HID0 // P, P).transpose(2, 0, 1))
    for name in ("L0_gnn_b_rel", "L0_gnn_gamma", "L0_gnn_beta", "L1_gnn_b", "L1_gnn_b1"):
        arrays[name] = np.ascontiguousarray(arrays[name].reshape(KD, P).T)
    arrays.update(const_arrays())
    aps = {k: nc.dram_tensor("in_" + k, v.shape, mybir.dt.from_np(v.dtype), kind="ExternalInput").ap()
           for k, v in arrays.items()}
    out = nc.dram_tensor("out", (NODES_PAD, D), FP32, kind="ExternalOutput").ap()
    program(nc, aps, out)
    result = run(nc, [{"in_" + k: v for k, v in arrays.items()}], core_ids=[0])
    return np.asarray(result.results[0]["out"])[:NODES]
```

```python
from contextlib import ExitStack

import numpy as np
import concourse.bass as bass
from concourse import mybir

FP32 = mybir.dt.float32
BF16 = mybir.dt.bfloat16
I32 = mybir.dt.int32
ALU = mybir.AluOpType
ACT = mybir.ActivationFunctionType
AX = mybir.AxisListType
EngineType = mybir.EngineType

P = 128
D = 256
KD = D // P
NODES = 6250
TILES = -(-NODES // P)
NODES_PAD = TILES * P
SLOTS = TILES + 1
EDGES = 106250
COLS = 832
EDGES_PAD = COLS * P
ATTR = 64
UNROLL = 16
SLOT = 4
STEPS = -(-(EDGES // P + TILES) // UNROLL) * UNROLL
EPS = 1e-5
HALVES = 2
HALF = EDGES_PAD // HALVES
RANK_BLOCKS = 16
RANK_COLS = COLS // HALVES // RANK_BLOCKS
RANK_LEN = RANK_COLS * P
GROUP = 7
GROUPS = TILES // GROUP
WIDE = NODES_PAD // 14
WIDES = 14
EXPERTS = 8
TOP0, TOP1 = 2, 1
HID0, HID1 = 512, 1024
CHUNKS0 = -(-((NODES_PAD * TOP0 + EXPERTS * (P - 1)) // P) // 2) * 2
CHUNKS1 = -(-((NODES_PAD * TOP1 + EXPERTS * (P - 1)) // P) // 2) * 2
REC0 = 2
REC1 = 4


def static(t):
    return isinstance(t, int)


def pairs(eng, n, body):
    body(0, 0)
    body(1, 1)
    if n >= 4:
        with eng.Fori(1, n // 2) as i:
            body(i * 2, 0)
            body(i * 2 + 1, 1)
    if n % 2:
        body(n - 1, 0)


def unrolled(eng, n, body):
    body(0, 0)
    with eng.Fori(1, n // UNROLL) as i:
        body(i * UNROLL, i)


class Core:

    def __init__(self, nc, ctx):
        self.nc, self.ctx, self.live = nc, ctx, []

    def sb(self, ctx, name, shape, dt):
        return ctx.enter_context(self.nc.sbuf_tensor(name, shape, dt))

    def ps(self, ctx, name, shape, dt=FP32):
        return ctx.enter_context(self.nc.psum_tensor(name, shape, dt))

    def sem(self, name):
        s = self.nc.alloc_semaphore(name=name)
        self.live.append(s)
        return s

    def clear(self, first):
        self.nc.clear_and_free_semaphores(self.live[first:])
        self.nc.all_engine_barrier()
        del self.live[first:]

    def dram(self, name, shape, dt):
        return self.nc.dram_tensor(name, shape, dt, kind="Internal").ap()


def phase(f):
    def run(c, *args, **kwargs):
        first = len(c.live)
        f(c, *args, **kwargs)
        c.clear(first)
    return run


def tiles_view(a):
    return a.rearrange("(g a p) d -> g p a d", a=GROUP, p=P)


class At:

    def __init__(self, step, u, i, n):
        self.step, self.u, self.i, self.n = step, u, i, n

    def __call__(self, lag):
        t, slot = self.step - lag, (self.u - lag) % SLOT
        if static(t):
            return (t, slot, t // SLOT) if 0 <= t < self.n else None
        return t, slot, self.i + (self.u - lag) // SLOT


def old(t, k):
    return not static(t) or t >= k


def pipeline(eng, n, depth, body):
    for s in range(2 * SLOT):
        body(At(s, s % SLOT, None, n))
    with eng.Fori(2, n // SLOT) as i:
        for u in range(SLOT):
            body(At(i * SLOT + u, u, i, n))
    for s in range(n // SLOT * SLOT, n + depth - 1):
        body(At(s, s % SLOT, None, n))


def tile_rows(a, t):
    return a[bass.ds(t * P, P), :]


@phase
def rows_pass(c, name, x_in, ys=None, place=None, top=0, prob=None, x_out=None, norm=None, beside=None):
    nc = c.nc
    with ExitStack() as ctx:
        x = c.sb(ctx, name + "_x", [P, 2, GROUP, D], FP32)
        passed = c.sem(name + "_passed")
        loaded = [c.sem(f"{name}_loaded{u}") for u in range(2)]
        if ys is not None:
            r = c.sb(ctx, name + "_r", [P, 2, top, GROUP, D], FP32)
            z = c.sb(ctx, name + "_z", [P, 2, GROUP, D], FP32)
            at = c.sb(ctx, name + "_at", [P, 2, GROUP, top], I32)
            got = [c.sem(f"{name}_got{u}") for u in range(2)]
            stored = [c.sem(f"{name}_stored{u}") for u in range(2)]
            staged = c.sem(name + "_staged")
            partly = c.sem(name + "_partly")
            added = c.sem(name + "_added")
            per = 16 * GROUP * top
        if norm is not None:
            eps, row_scale, out, turned_t, ident = norm
            y = c.sb(ctx, name + "_y", [P, 2, GROUP, D], FP32)
            st = c.sb(ctx, name + "_st", [P, 2, GROUP, 6], FP32)
            mv = c.sb(ctx, name + "_mv", [P, 2, GROUP, 2], FP32)
            sd = c.sb(ctx, name + "_sd", [P, 2, GROUP], FP32)
            rs = c.sb(ctx, name + "_rs", [P, 2, GROUP], FP32)
            pt = [c.ps(ctx, f"{name}_pt{a}", [P, KD, P]) for a in range(GROUP)]
            normed_out = [c.sem(f"{name}_normed_out{u}") for u in range(2)]
            stats = c.sem(name + "_stats")
            moments = c.sem(name + "_moments")
            root = c.sem(name + "_root")
            inverse = c.sem(name + "_inverse")
            normed = c.sem(name + "_normed")
            turned = c.sem(name + "_turned")
            copied = c.sem(name + "_copied")
            ni = 1 if row_scale is None else 2
        block = ctx.enter_context(nc.Block())
        if beside is not None:
            beside(block)

        @block.sync
        def _(sp):
            def body(g, u):
                if old(g, 2):
                    sp.wait_ge(normed if ys is None else added, g - 1)
                sp.dma_start(x[:, u], tiles_view(x_in)[bass.ds(g, 1)].rearrange("o p a d -> p (o a) d")).then_inc(loaded[u], 16)
            pairs(sp, GROUPS, body)

        if ys is not None:
            @block.gpsimd
            def _(pool):
                def body(g, u):
                    if old(g, 2):
                        pool.wait_ge(added, g - 1)
                    pool.tensor_copy(at[:, u], place[:, bass.ds(g * GROUP, GROUP)]).then_inc(staged, 1)
                    pool.wait_ge(staged, g + 1)
                    pool.sem_inc(passed, 1)
                    for t in range(GROUP):
                        for k in range(top):
                            pool.indirect_dma_start(
                                out=r[:, u, k, t], out_offset=None, in_=ys,
                                in_offset=bass.IndirectOffsetOnAxis(ap=at[:, u, t, k:k + 1], axis=0)).then_inc(got[u], 16)
                pairs(pool, GROUPS, body)

        @block.vector
        def _(dve):
            def body(g, u):
                if ys is not None:
                    dve.wait_ge(got[u], (g // 2) * per + per)
                    r0 = r[:, u, 0]
                    if prob is None:
                        nc.vector.tensor_tensor(r0, r0, r[:, u, 1], ALU.add).then_inc(partly, 1)
                    else:
                        nc.vector.tensor_tensor(r0, r0, prob[:, bass.ds(g * GROUP, GROUP)].unsqueeze(2).broadcast_to([P, GROUP, D]),
                                                ALU.mult).then_inc(partly, 1)
                    dve.wait_ge(partly, g + 1)
                    dve.wait_ge(loaded[u], (g // 2) * 16 + 16)
                    if old(g, 2):
                        dve.wait_ge(stored[u], (g // 2) * 16)
                        if norm is not None:
                            dve.wait_ge(normed, g - 1)
                    nc.vector.tensor_tensor(z[:, u], r0, x[:, u], ALU.add).then_inc(added, 1)
                    dve.wait_ge(added, g + 1)
                    rows = z
                else:
                    dve.wait_ge(loaded[u], (g // 2) * 16 + 16)
                    rows = x
                if norm is None:
                    return
                for a in range(GROUP):
                    last = nc.vector.bn_stats(st[:, u, a], rows[:, u, a])
                last.then_inc(stats, 1)
                dve.wait_ge(stats, g + 1)
                if old(g, 2):
                    dve.wait_ge(root, g - 1)
                dve.sem_inc(passed, 1)
                for a in range(GROUP):
                    last = nc.vector.bn_aggr(mv[:, u, a], st[:, u, a])
                last.then_inc(moments, 1)
                dve.wait_ge(root, g + 1)
                nc.vector.reciprocal(rs[:, u], sd[:, u]).then_inc(inverse, 1)
                dve.wait_ge(inverse, g * ni + 1)
                if row_scale is not None:
                    nc.vector.tensor_tensor(rs[:, u], rs[:, u], row_scale[:, bass.ds(g * GROUP, GROUP)],
                                            ALU.mult).then_inc(inverse, 1)
                    dve.wait_ge(inverse, g * ni + 2)
                if old(g, 2):
                    dve.wait_ge(normed_out[u], (g // 2) * 16)
                    dve.wait_ge(turned, g * GROUP - GROUP)
                for a in range(GROUP):
                    last = nc.vector.tensor_scalar(y[:, u, a], rows[:, u, a], mv[:, u, a, 0:1], rs[:, u, a:a + 1],
                                                   ALU.subtract, ALU.mult)
                last.then_inc(normed, 1)
            pairs(dve, GROUPS, body)

        @block.scalar
        def _(act):
            def put(dst, g, tile, u, sem):
                act.dma_start(tiles_view(dst)[bass.ds(g, 1)].rearrange("o p a d -> p (o a) d"), tile[:, u]).then_inc(sem[u], 16)

            def body(g, u):
                if ys is not None:
                    act.wait_ge(added, g + 1)
                    put(x_out, g, z, u, stored)
                if norm is None:
                    return
                act.wait_ge(moments, g + 1)
                if old(g, 2):
                    act.wait_ge(inverse, g * ni - ni)
                nc.scalar.activation(sd[:, u], mv[:, u, :, 1], ACT.Sqrt, bias=eps[:, 0:1]).then_inc(root, 1)
                act.wait_ge(normed, g + 1)
                put(out, g, y, u, normed_out)
                for a in range(GROUP):
                    act.wait_ge(turned, g * GROUP + (a + 1))
                    act.sem_inc(passed, 1)
                    nc.scalar.activation(turned_t[:, :, bass.ds((g * GROUP + a) * P, P)], pt[a][:], ACT.Copy).then_inc(copied, 1)
            pairs(act, GROUPS, body)
            for u in range(2):
                n = 16 * ((GROUPS + 1 - u) // 2)
                if ys is not None:
                    act.wait_ge(stored[u], n)
                if norm is not None:
                    act.wait_ge(normed_out[u], n)

        if norm is not None:
            @block.tensor
            def _(pe):
                def body(g, u):
                    pe.wait_ge(normed, g + 1)
                    for a in range(GROUP):
                        if old(g, 1):
                            pe.wait_ge(copied, g * GROUP + (a + 1 - GROUP))
                        for k in range(KD):
                            last = nc.tensor.transpose(pt[a][:, k], y[:, u, a, k * P:(k + 1) * P], ident[:])
                        last.then_inc(turned, 1)
                pairs(pe, GROUPS, body)


@phase
def finish_graph(c, name, x_in, h_t, scale, shift, xn_t, w_res, ident, mv, x_out, beside=None):
    nc = c.nc
    with ExitStack() as ctx:
        x = c.sb(ctx, name + "_x", [P, SLOT, D], FP32)
        za = c.sb(ctx, name + "_za", [P, SLOT, KD, P], FP32)
        zb = c.sb(ctx, name + "_zb", [P, SLOT, KD, P], FP32)
        y = c.sb(ctx, name + "_y", [P, SLOT, D], FP32)
        st = c.sb(ctx, name + "_st", [P, TILES, 6], FP32)
        pr = [c.ps(ctx, f"{name}_pr{u}", [P, KD, P]) for u in range(2)]
        po = [c.ps(ctx, f"{name}_po{u}", [P, KD, P]) for u in range(2)]
        loaded = [c.sem(f"{name}_loaded{u}") for u in range(SLOT)]
        stored = [c.sem(f"{name}_stored{u}") for u in range(SLOT)]
        scaled = c.sem(name + "_scaled")
        residual = c.sem(name + "_residual")
        summed = c.sem(name + "_summed")
        turned = c.sem(name + "_turned")
        added = c.sem(name + "_added")
        stats = c.sem(name + "_stats")
        passed = c.sem(name + "_passed")
        block = ctx.enter_context(nc.Block())
        if beside is not None:
            beside(block)

        @block.sync
        def _(sp):
            def body(at):
                if now := at(0):
                    t, v, i = now
                    if old(t, SLOT):
                        sp.wait_ge(added, t - (SLOT - 1))
                    sp.dma_start(x[:, v], tile_rows(x_in, t)).then_inc(loaded[v], 16)
            pipeline(sp, TILES, 1, body)

        @block.scalar
        def _(act):
            def body(at):
                if now := at(0):
                    t, v, i = now
                    if old(t, SLOT):
                        act.wait_ge(summed, t - (SLOT - 1))
                        act.sem_inc(passed, 1)
                    for m in range(KD):
                        last = nc.scalar.activation(za[:, v, m], h_t[:, m, bass.ds(t * P, P)], ACT.Identity,
                                                    bias=shift[:, m:m + 1], scale=scale[:, m:m + 1])
                    last.then_inc(scaled, 1)
                if now := at(4):
                    t, v, i = now
                    act.wait_ge(added, t + 1)
                    act.sem_inc(passed, 1)
                    act.dma_start(tile_rows(x_out, t), y[:, v]).then_inc(stored[v], 16)
            pipeline(act, TILES, 5, body)
            for v in range(SLOT):
                act.wait_ge(stored[v], 16 * ((TILES + SLOT - 1 - v) // SLOT))

        @block.tensor
        def _(pe):
            def body(at):
                if now := at(0):
                    t, v, i = now
                    if old(t, 2):
                        pe.wait_ge(summed, t - 1)
                    for m in range(KD):
                        for k in range(KD):
                            last = nc.tensor.matmul(pr[v % 2][:, m], w_res[:, k, m * P:(m + 1) * P], xn_t[:, k, bass.ds(t * P, P)],
                                                    start=k == 0, stop=k == KD - 1)
                    last.then_inc(residual, 1)
                if now := at(2):
                    t, v, i = now
                    pe.wait_ge(summed, t + 1)
                    if old(t, 2):
                        pe.wait_ge(added, t - 1)
                    for k in range(KD):
                        last = nc.tensor.transpose(po[v % 2][:, k], zb[:, v, k], ident[:])
                    last.then_inc(turned, 1)
            pipeline(pe, TILES, 3, body)

        @block.vector
        def _(dve):
            def body(at):
                if now := at(1):
                    t, v, i = now
                    dve.wait_ge(scaled, t + 1)
                    dve.wait_ge(residual, t + 1)
                    if old(t, SLOT):
                        dve.wait_ge(turned, t - (SLOT - 1))
                    nc.vector.tensor_tensor(zb[:, v], za[:, v], pr[v % 2][:], ALU.add).then_inc(summed, 1)
                if now := at(3):
                    t, v, i = now
                    dve.wait_ge(loaded[v], i * 16 + 16)
                    dve.wait_ge(turned, t + 1)
                    if old(t, SLOT):
                        dve.wait_ge(stored[v], i * 16)
                        dve.wait_ge(stats, t - (SLOT - 1))
                    nc.vector.tensor_tensor(y[:, v], x[:, v], po[v % 2][:].rearrange("p k n -> p (k n)"), ALU.add).then_inc(added, 1)
                if now := at(4):
                    t, v, i = now
                    dve.wait_ge(added, t + 1)
                    dve.sem_inc(passed, 1)
                    nc.vector.bn_stats(st[:, bass.ds(t, 1)].rearrange("p o s -> p (o s)"), y[:, v]).then_inc(stats, 1)
            pipeline(dve, TILES, 5, body)
            dve.wait_ge(stats, TILES)
            for t in range(TILES):
                nc.vector.bn_aggr(mv[:, t], st[:, t])


@phase
def second_graph(c, name, x_in, agg_t, dinv_b, w, b, w1, b1, w2, b2_row, mv, x_out):
    nc = c.nc
    with ExitStack() as ctx:
        x = c.sb(ctx, name + "_x", [P, SLOT, D], FP32)
        xb = c.sb(ctx, name + "_xb", [P, SLOT, D], FP32)
        z = c.sb(ctx, name + "_z", [P, SLOT, KD, P], FP32)
        h7 = c.sb(ctx, name + "_h7", [P, SLOT, KD, P], FP32)
        h = c.sb(ctx, name + "_h", [P, SLOT, KD, P], FP32)
        y = c.sb(ctx, name + "_y", [P, SLOT, D], FP32)
        st = c.sb(ctx, name + "_st", [P, TILES, 6], FP32)
        pa = [c.ps(ctx, f"{name}_pa{u}", [P, KD, P]) for u in range(2)]
        pb = [c.ps(ctx, f"{name}_pb{u}", [P, KD, P]) for u in range(2)]
        po = [c.ps(ctx, f"{name}_po{u}", [P, 512]) for u in range(2)]
        loaded = [c.sem(f"{name}_loaded{u}") for u in range(SLOT)]
        stored = [c.sem(f"{name}_stored{u}") for u in range(SLOT)]
        scaled = c.sem(name + "_scaled")
        first = c.sem(name + "_first")
        h7_done = c.sem(name + "_h7_done")
        second = c.sem(name + "_second")
        relued = c.sem(name + "_relued")
        third = c.sem(name + "_third")
        biased = c.sem(name + "_biased")
        added = c.sem(name + "_added")
        stats = c.sem(name + "_stats")
        passed = c.sem(name + "_passed")
        block = ctx.enter_context(nc.Block())

        @block.sync
        def _(sp):
            def body(at):
                if now := at(0):
                    t, v, i = now
                    if old(t, SLOT):
                        sp.wait_ge(biased, t - (SLOT - 1))
                    sp.dma_start(x[:, v], tile_rows(x_in, t)).then_inc(loaded[v], 16)
                if now := at(5):
                    t, v, i = now
                    sp.wait_ge(added, t + 1)
                    sp.dma_start(tile_rows(x_out, t), y[:, v]).then_inc(stored[v], 16)
            pipeline(sp, TILES, 6, body)
            for v in range(SLOT):
                sp.wait_ge(stored[v], 16 * ((TILES + SLOT - 1 - v) // SLOT))

        @block.vector
        def _(dve):
            def body(at):
                if now := at(0):
                    t, v, i = now
                    if old(t, SLOT):
                        dve.wait_ge(first, t - (SLOT - 1))
                    n = bass.ds(t * P, P)
                    nc.vector.tensor_tensor(z[:, v], agg_t[:, :, n], dinv_b[:, n].unsqueeze(1).broadcast_to([P, KD, P]),
                                            ALU.mult).then_inc(scaled, 1)
                if now := at(3):
                    t, v, i = now
                    dve.wait_ge(loaded[v], i * 16 + 16)
                    if old(t, SLOT):
                        dve.wait_ge(added, t - (SLOT - 1))
                    nc.vector.tensor_tensor(xb[:, v], x[:, v], b2_row[:], ALU.add).then_inc(biased, 1)
                if now := at(4):
                    t, v, i = now
                    dve.wait_ge(biased, t + 1)
                    dve.wait_ge(third, t + 1)
                    if old(t, SLOT):
                        dve.wait_ge(stored[v], i * 16)
                        dve.wait_ge(stats, t - (SLOT - 1))
                    nc.vector.tensor_tensor(y[:, v], xb[:, v], po[v % 2][:, 0:D], ALU.add).then_inc(added, 1)
                if now := at(5):
                    t, v, i = now
                    dve.wait_ge(added, t + 1)
                    dve.sem_inc(passed, 1)
                    nc.vector.bn_stats(st[:, bass.ds(t, 1)].rearrange("p o s -> p (o s)"), y[:, v]).then_inc(stats, 1)
            pipeline(dve, TILES, 6, body)
            dve.wait_ge(stats, TILES)
            for t in range(TILES):
                nc.vector.bn_aggr(mv[:, t], st[:, t])

        @block.scalar
        def _(act):
            def body(at):
                if now := at(1):
                    t, v, i = now
                    act.wait_ge(first, t + 1)
                    if old(t, SLOT):
                        act.wait_ge(second, t - (SLOT - 1))
                    for m in range(KD):
                        last = nc.scalar.activation(h7[:, v, m], pa[v % 2][:, m], ACT.Identity, bias=b[:, m:m + 1])
                    last.then_inc(h7_done, 1)
                if now := at(2):
                    t, v, i = now
                    act.wait_ge(second, t + 1)
                    if old(t, SLOT):
                        act.wait_ge(third, t - (SLOT - 1))
                    for m in range(KD):
                        last = nc.scalar.activation(h[:, v, m], pb[v % 2][:, m], ACT.Relu, bias=b1[:, m:m + 1])
                    last.then_inc(relued, 1)
            pipeline(act, TILES, 3, body)

        @block.tensor
        def _(pe):
            def product(p, w_, x_, v):
                for m in range(KD):
                    for k in range(KD):
                        last = nc.tensor.matmul(p[v % 2][:, m], w_[:, k, m * P:(m + 1) * P], x_[:, v, k],
                                                start=k == 0, stop=k == KD - 1)
                return last

            def body(at):
                if now := at(1):
                    t, v, i = now
                    pe.wait_ge(scaled, t + 1)
                    if old(t, 2):
                        pe.wait_ge(h7_done, t - 1)
                    product(pa, w, z, v).then_inc(first, 1)
                if now := at(2):
                    t, v, i = now
                    pe.wait_ge(h7_done, t + 1)
                    if old(t, 2):
                        pe.wait_ge(relued, t - 1)
                    product(pb, w1, h7, v).then_inc(second, 1)
                if now := at(3):
                    t, v, i = now
                    pe.wait_ge(relued, t + 1)
                    if old(t, 2):
                        pe.wait_ge(added, t - 1)
                    for k in range(KD):
                        last = nc.tensor.matmul(po[v % 2][:, 0:D], h[:, v, k], w2[:, k], start=k == 0, stop=k == KD - 1)
                    last.then_inc(third, 1)
            pipeline(pe, TILES, 4, body)


@phase
def gate_pass(c, name, x_in, mv, eps, xn, scores, ident, wg, bg_row, w1=None, b1=None, beside=None):
    nc = c.nc
    hidden_layer = w1 is not None
    km = HID1 // P if hidden_layer else KD
    with ExitStack() as ctx:
        x = c.sb(ctx, name + "_x", [P, SLOT, D], FP32)
        y = c.sb(ctx, name + "_y", [P, SLOT, D], FP32)
        x_t = c.sb(ctx, name + "_xt", [P, SLOT, KD, P], FP32)
        sd = c.sb(ctx, name + "_sd", [P, TILES], FP32)
        rs = c.sb(ctx, name + "_rs", [P, TILES], FP32)
        pt = [c.ps(ctx, f"{name}_pt{u}", [P, KD, P]) for u in range(2)]
        pg = [c.ps(ctx, f"{name}_pg{u}", [P, 512]) for u in range(2)]
        if hidden_layer:
            h_t = c.sb(ctx, name + "_ht", [P, SLOT, km, P], FP32)
            ph = [c.ps(ctx, f"{name}_ph{n}", [P, 4, P]) for n in range(4)]
            hidden = c.sem(name + "_hidden")
            active = c.sem(name + "_active")
        loaded = [c.sem(f"{name}_loaded{u}") for u in range(SLOT)]
        stored = [c.sem(f"{name}_stored{u}") for u in range(SLOT)]
        root = c.sem(name + "_root")
        inverse = c.sem(name + "_inverse")
        normed = c.sem(name + "_normed")
        turned = c.sem(name + "_turned")
        copied = c.sem(name + "_copied")
        gated = c.sem(name + "_gated")
        kept = c.sem(name + "_kept")
        passed = c.sem(name + "_passed")
        block = ctx.enter_context(nc.Block())
        if beside is not None:
            beside(block)

        @block.sync
        def _(sp):
            def body(at):
                if now := at(0):
                    t, v, i = now
                    if old(t, SLOT):
                        sp.wait_ge(normed, t - (SLOT - 1))
                    sp.dma_start(x[:, v], tile_rows(x_in, t)).then_inc(loaded[v], 16)
                if now := at(2):
                    t, v, i = now
                    sp.wait_ge(normed, t + 1)
                    sp.dma_start(tile_rows(xn, t), y[:, v]).then_inc(stored[v], 16)
            pipeline(sp, TILES, 3, body)
            for v in range(SLOT):
                sp.wait_ge(stored[v], 16 * ((TILES + SLOT - 1 - v) // SLOT))

        @block.vector
        def _(dve):
            dve.wait_ge(root, 1)
            nc.vector.reciprocal(rs[:], sd[:]).then_inc(inverse, 1)
            dve.wait_ge(inverse, 1)

            def body(at):
                if now := at(1):
                    t, v, i = now
                    dve.wait_ge(loaded[v], i * 16 + 16)
                    if old(t, SLOT):
                        dve.wait_ge(stored[v], i * 16)
                        dve.wait_ge(turned, t - (SLOT - 1))
                    nc.vector.tensor_scalar(y[:, v], x[:, v], mv[:, bass.ds(t, 1), 0], rs[:, bass.ds(t, 1)],
                                            ALU.subtract, ALU.mult).then_inc(normed, 1)
                if now := at(2):
                    t, v, i = now
                    dve.wait_ge(turned, t + 1)
                    if old(t, SLOT):
                        dve.wait_ge(hidden, t * 2 - (SLOT * 2 - 2)) if hidden_layer else dve.wait_ge(gated, t - (SLOT - 1))
                        dve.sem_inc(passed, 1)
                    nc.vector.tensor_copy(x_t[:, v], pt[v % 2][:]).then_inc(copied, 1)
                if now := at(4):
                    t, v, i = now
                    dve.wait_ge(gated, t + 1)
                    nc.vector.tensor_tensor(scores[:, bass.ds(t, 1)].rearrange("p o e -> p (o e)"), pg[v % 2][:, 0:EXPERTS],
                                            bg_row[:], ALU.add).then_inc(kept, 1)
            pipeline(dve, TILES, 5, body)

        @block.scalar
        def _(act):
            nc.scalar.activation(sd[:], mv[:, :, 1], ACT.Sqrt, bias=eps[:, 0:1]).then_inc(root, 1)
            if hidden_layer:
                def body(at):
                    if now := at(3):
                        t, v, i = now
                        if old(t, SLOT):
                            act.wait_ge(gated, t - (SLOT - 1))
                        for n in range(2):
                            act.wait_ge(hidden, t * 2 + (n + 1))
                            for m in range(4):
                                last = nc.scalar.activation(h_t[:, v, n * 4 + m], ph[v % 2 * 2 + n][:, m], ACT.Gelu,
                                                            bias=b1[:, n * 4 + m:n * 4 + m + 1])
                            last.then_inc(active, 1)
                pipeline(act, TILES, 4, body)

        @block.tensor
        def _(pe):
            def body(at):
                if now := at(2):
                    t, v, i = now
                    pe.wait_ge(normed, t + 1)
                    if old(t, 2):
                        pe.wait_ge(copied, t - 1)
                    for k in range(KD):
                        last = nc.tensor.transpose(pt[v % 2][:, k], y[:, v, k * P:(k + 1) * P], ident[:])
                    last.then_inc(turned, 1)
                if hidden_layer and (now := at(3)):
                    t, v, i = now
                    pe.wait_ge(copied, t + 1)
                    for n in range(2):
                        if old(t, 2):
                            pe.wait_ge(active, t * 2 + (n - 3))
                        for m in range(n * 4, n * 4 + 4):
                            for k in range(KD):
                                last = nc.tensor.matmul(ph[v % 2 * 2 + n][:, m % 4], w1[:, k, m * P:(m + 1) * P],
                                                        x_t[:, v, k], start=k == 0, stop=k == KD - 1)
                        last.then_inc(hidden, 1)
                if now := at(4):
                    t, v, i = now
                    if hidden_layer:
                        pe.wait_ge(active, t * 2 + 2)
                    else:
                        pe.wait_ge(copied, t + 1)
                    z = h_t if hidden_layer else x_t
                    if old(t, 2):
                        pe.wait_ge(kept, t - 1)
                    for k in range(km):
                        last = nc.tensor.matmul(pg[v % 2][:, 0:EXPERTS], z[:, v, k], wg[:, k], start=k == 0, stop=k == km - 1)
                    last.then_inc(gated, 1)
            pipeline(pe, TILES, 5, body)


class Prefetch:

    def __init__(self, c, name, items, after=None):
        self.items, self.sem, self.after = items, c.nc.alloc_semaphore(name=name + "_fetched"), after

    def start(self, block):
        @block.sync
        def _(sp):
            if self.after is not None:
                sp.wait_ge(*self.after)
            for tile, src in self.items:
                sp.dma_start(tile, src).then_inc(self.sem, 16)

    def finish(self, block):
        @block.scalar
        def _(act):
            act.wait_ge(self.sem, 16 * len(self.items))

    def both(self, block):
        self.start(block)
        self.finish(block)


@phase
def tile_ids(c, src_flat, dst_flat, ids_src, ids_dst, rec0, posrec, src_cols, dst_cols, ew_cols):
    nc = c.nc
    with ExitStack() as ctx:
        s_i = c.sb(ctx, "ids_s", [P, COLS], I32)
        d_i = c.sb(ctx, "ids_d", [P, COLS], I32)
        t_i = c.sb(ctx, "ids_t", [P, 2, COLS], I32)
        t_b = c.sb(ctx, "ids_b", [P, 2, COLS], BF16)
        r0 = c.sb(ctx, "ids_r0", [P, COLS, REC0], I32)
        sc = c.sb(ctx, "ids_sc", [P, COLS], I32)
        dc = c.sb(ctx, "ids_dc", [P, COLS], I32)
        ec = c.sb(ctx, "ids_ec", [P, COLS], FP32)
        loaded = c.sem("ids_loaded")
        loaded_cols = c.sem("ids_loaded_cols")
        shifted = c.sem("ids_shifted")
        made = c.sem("ids_made")
        stored = c.sem("ids_stored")
        block = ctx.enter_context(nc.Block())

        @block.sync
        def _(sp):
            sp.dma_start(s_i[:], src_flat.rearrange("(p j) -> p j", p=P)).then_inc(loaded, 16)
            sp.dma_start(d_i[:], dst_flat.rearrange("(p j) -> p j", p=P)).then_inc(loaded, 16)
            sp.dma_start(sc[:], src_cols).then_inc(loaded_cols, 16)
            sp.dma_start(dc[:], dst_cols).then_inc(loaded_cols, 16)
            sp.dma_start(ec[:], ew_cols).then_inc(loaded_cols, 16)
            sp.wait_ge(made, 1)
            sp.dma_start(ids_src.rearrange("(p j) -> p j", p=P), t_b[:, 0]).then_inc(stored, 16)
            sp.dma_start(ids_dst.rearrange("(p j) -> p j", p=P), t_b[:, 1]).then_inc(stored, 16)
            sp.wait_ge(made, 2)
            sp.dma_start(rec0.rearrange("(p j) w -> p (j w)", p=P), r0[:].rearrange("p j w -> p (j w)")).then_inc(stored, 16)
            sp.wait_ge(stored, 48)


        @block.vector
        def _(dve):
            dve.wait_ge(loaded, 32)
            nc.vector.tensor_scalar(t_i[:, 0], s_i[:], 7, None, ALU.arith_shift_right)
            nc.vector.tensor_scalar(t_i[:, 1], d_i[:], 7, None, ALU.arith_shift_right).then_inc(shifted, 1)
            dve.wait_ge(shifted, 1)
            nc.vector.tensor_copy(t_b[:], t_i[:]).then_inc(made, 1)
            nc.vector.tensor_scalar(r0[:, :, 0], s_i[:], NODES_PAD - 1, None, ALU.min)
            nc.vector.tensor_copy(r0[:, :, 1].bitcast(FP32), d_i[:]).then_inc(made, 1)
            dve.wait_ge(loaded_cols, 48)
            nc.vector.tensor_copy(posrec[:, :, 1].bitcast(FP32), sc[:])
            nc.vector.tensor_scalar(posrec[:, :, 2], dc[:], NODES_PAD - 1, None, ALU.min)
            nc.vector.tensor_copy(posrec[:, :, 3], ec[:].bitcast(I32))
            nc.vector.memset(posrec[:, :, 4], 0)


@phase
def count(c, name, ids, consts, tab, base, beside=None):
    nc = c.nc
    B = 4
    with ExitStack() as ctx:
        ids_b = c.sb(ctx, name + "_ids", [P, B, RANK_LEN], BF16)
        hit = c.sb(ctx, name + "_hit", [P, 2, RANK_LEN], BF16)
        part = c.sb(ctx, name + "_part", [P, RANK_BLOCKS], FP32)
        cnt = c.sb(ctx, name + "_cnt", [P, 1], FP32)
        small = c.sb(ctx, name + "_small", [P, 8], FP32)
        small_i = c.sb(ctx, name + "_small_i", [P, 2], I32)
        ge = c.sb(ctx, name + "_ge", [P, STEPS], FP32)
        rows = c.sb(ctx, name + "_rows", [1, 2, STEPS], FP32)
        pm = c.ps(ctx, name + "_pm", [P, 512])
        pt = [c.ps(ctx, f"{name}_pt{i}", [1, 512]) for i in range(4)]
        loaded = [c.sem(f"{name}_loaded{u}") for u in range(B)]
        counted = c.sem(name + "_counted")
        small_done = c.sem(name + "_small_done")
        product = c.sem(name + "_product")
        table = c.sem(name + "_table")
        passed = c.sem(name + "_passed")
        bucket, fold, before, lower, diff, ones, steps = (consts[k] for k in (
            "bucket", "fold", "before", "lower", "diff", "ones", "steps"))
        ids_h = ids.rearrange("(h n) -> h n", h=HALVES)

        block = ctx.enter_context(nc.Block())
        if beside is not None:
            beside(block)

        @block.sync
        def _(sp):
            for k in range(RANK_BLOCKS):
                if k >= B:
                    sp.wait_ge(counted, k - (B - 1))
                for h in range(HALVES):
                    sp.dma_start(ids_b[h * 64:h * 64 + 64, k % B],
                                 ids_h[h:h + 1, k * RANK_LEN:(k + 1) * RANK_LEN].broadcast_to([64, RANK_LEN])).then_inc(loaded[k % B], 16)

        @block.vector
        def _(dve):
            for k in range(RANK_BLOCKS):
                dve.wait_ge(loaded[k % B], 16 * HALVES * (k // B + 1))
                if k >= 2:
                    dve.wait_ge(counted, k - 1)
                nc.vector.tensor_scalar(hit[:, k % 2], ids_b[:, k % B], bucket[:, 0:1], 0.0, ALU.is_equal, ALU.add,
                                        accum_out=part[:, k:k + 1]).then_inc(counted, 1)
            dve.wait_ge(counted, RANK_BLOCKS)
            nc.vector.reduce_sum(cnt[:], part[:], AX.X).then_inc(small_done, 1)
            dve.wait_ge(product, 1)
            nc.vector.tensor_copy(small[:, 0:2], pm[:, 0:2]).then_inc(small_done, 1)
            nc.vector.tensor_scalar(base[:], pm[:, 0:1], -1.0, None, ALU.add)
            dve.wait_ge(small_done, 2)
            nc.vector.tensor_scalar(small_i[:, 0:1], small[:, 1:2], float(P - 1), None, ALU.add).then_inc(small_done, 1)
            dve.wait_ge(small_done, 3)
            nc.vector.tensor_scalar(small_i[:, 1:2], small_i[:, 0:1], 7, None, ALU.arith_shift_right).then_inc(small_done, 1)
            dve.wait_ge(small_done, 4)
            nc.vector.tensor_copy(small[:, 2:3], small_i[:, 1:2]).then_inc(small_done, 1)
            dve.wait_ge(product, 2)
            nc.vector.tensor_copy(small[:, 3:4], pm[:, 2:3]).then_inc(small_done, 1)
            dve.wait_ge(small_done, 6)
            nc.vector.scalar_tensor_tensor(small[:, 4:5], small[:, 3:4], -float(P), small[:, 0:1],
                                           ALU.mult, ALU.add).then_inc(small_done, 1)
            nc.vector.tensor_scalar(ge[:], steps[:], small[:, 3:4], None, ALU.is_ge)
            dve.wait_ge(product, 3)
            nc.vector.tensor_copy(small[:, 5:6], pm[:, 3:4]).then_inc(small_done, 1)
            dve.wait_ge(product, 4)
            for i in range(2):
                s = slice(i * (STEPS // 2), (i + 1) * (STEPS // 2))
                nc.vector.scalar_tensor_tensor(rows[:, 0, s], steps[0:1, s], float(P), pt[i][:, 0:STEPS // 2],
                                               ALU.mult, ALU.add)
                last = nc.vector.tensor_scalar(rows[:, 1, s], pt[2 + i][:, 0:STEPS // 2], -1.0, None, ALU.add)
            last.then_inc(small_done, 1)
            dve.wait_ge(small_done, 9)
            nc.vector.tensor_scalar(tab[:, 0], rows[:, 0], float(EDGES_PAD - P), None, ALU.min)
            nc.vector.tensor_scalar(tab[:, 1], rows[:, 1], float(P), None, ALU.mult).then_inc(table, 1)

        @block.tensor
        def _(pe):
            pe.wait_ge(small_done, 1)
            nc.tensor.matmul(pm[:, 0:1], before[:], cnt[:], start=True, stop=True)
            nc.tensor.matmul(pm[:, 1:2], fold[:], cnt[:], start=True, stop=True).then_inc(product, 1)
            pe.wait_ge(small_done, 5)
            nc.tensor.matmul(pm[:, 2:3], lower[:], small[:, 2:3], start=True, stop=True).then_inc(product, 1)
            pe.wait_ge(small_done, 7)
            nc.tensor.matmul(pm[:, 3:4], diff[:], small[:, 4:5], start=True, stop=True).then_inc(product, 1)
            pe.wait_ge(small_done, 8)
            for i in range(2):
                s = slice(i * (STEPS // 2), (i + 1) * (STEPS // 2))
                nc.tensor.matmul(pt[i][:, 0:STEPS // 2], small[0:SLOTS, 5:6], ge[0:SLOTS, s], start=True, stop=True)
                last = nc.tensor.matmul(pt[2 + i][:, 0:STEPS // 2], ones[0:SLOTS, 0:1], ge[0:SLOTS, s],
                                        start=True, stop=True)
            last.then_inc(product, 1)


class OrderCheck:

    def __init__(self, c, ctx, dst_flat, ones, unsorted):
        self.c, self.dst_flat, self.ones, self.unsorted = c, dst_flat, ones, unsorted
        self.ids = c.sb(ctx, "oc_ids", [P, 2, COLS], I32)
        self.tile_ids = c.sb(ctx, "oc_tile_ids", [P, 2, COLS], I32)
        self.falls = c.sb(ctx, "oc_falls", [P, COLS], FP32)
        self.most = c.sb(ctx, "oc_most", [P, 1], FP32)
        self.p = c.ps(ctx, "oc_p", [1, 512])

    def beside(self, block):
        nc, ids, tile_ids, falls = self.c.nc, self.ids, self.tile_ids, self.falls
        loaded = self.c.sem("oc_loaded")
        done = self.c.sem("oc_done")
        summed = self.c.sem("oc_summed")
        behind = (P - 1) * COLS

        @block.scalar
        def _(act):
            act.dma_start(ids[:, 0], self.dst_flat.rearrange("(p j) -> p j", p=P)).then_inc(loaded, 16)
            act.dma_start(ids[0:P - 1, 1], self.dst_flat[1:1 + behind].rearrange("(p j) -> p j", j=COLS)).then_inc(loaded, 16)
            act.dma_start(ids[P - 1:P, 1, 0:COLS - 1], self.dst_flat[1 + behind:].rearrange("(o j) -> o j", o=1)).then_inc(loaded, 16)

        @block.vector
        def _(dve):
            dve.wait_ge(loaded, 48)
            nc.vector.tensor_scalar(tile_ids[:, 0], ids[:, 0], 7, None, ALU.arith_shift_right)
            nc.vector.tensor_scalar(tile_ids[0:P - 1, 1, COLS - 1:], ids[0:P - 1, 1, COLS - 1:], 7, None, ALU.arith_shift_right)
            nc.vector.tensor_scalar(tile_ids[:, 1, 0:COLS - 1], ids[:, 1, 0:COLS - 1], 7, None, ALU.arith_shift_right)
            nc.vector.memset(falls[:], 0.0).then_inc(done, 1)
            dve.wait_ge(done, 1)
            nc.vector.tensor_tensor(falls[:, 0:COLS - 1], tile_ids[:, 0, 0:COLS - 1], tile_ids[:, 1, 0:COLS - 1], ALU.is_gt)
            nc.vector.tensor_tensor(falls[0:P - 1, COLS - 1:], tile_ids[0:P - 1, 0, COLS - 1:], tile_ids[0:P - 1, 1, COLS - 1:],
                                    ALU.is_gt).then_inc(done, 1)
            dve.wait_ge(done, 2)
            nc.vector.reduce_sum(self.most[:], falls[:], AX.X).then_inc(done, 1)
            dve.wait_ge(summed, 1)
            nc.vector.tensor_copy(self.unsorted[:], self.p[:, 0:1]).then_inc(done, 1)
            dve.wait_ge(done, 4)

        @block.tensor
        def _(pe):
            pe.wait_ge(done, 3)
            nc.tensor.matmul(self.p[:, 0:1], self.most[:], self.ones[:, 0:1], start=True, stop=True).then_inc(summed, 1)


@phase
def aggregate_any_order(c, name, table, rec, unsorted, node_ids, agg_t, attr_t, w_edge):
    nc = c.nc
    with ExitStack() as ctx:
        rb = c.sb(ctx, name + "_rec", [P, REC0], I32)
        at = c.sb(ctx, name + "_attr", [ATTR, P], FP32)
        rows = c.sb(ctx, name + "_rows", [P, D], FP32)
        msg = c.sb(ctx, name + "_msg", [P, D], FP32)
        pick = c.sb(ctx, name + "_pick", [P, GROUP, P], FP32)
        pe_edge = c.ps(ctx, name + "_pe", [P, 512])
        pa = [c.ps(ctx, f"{name}_pa{n}", [P, 2, KD, P]) for n in range((GROUP + 1) // 2)]
        got_rec = c.sem(name + "_got_rec")
        got_at = c.sem(name + "_got_at")
        got_rows = c.sem(name + "_got_rows")
        edge_done = c.sem(name + "_edge_done")
        msg_done = c.sem(name + "_msg_done")
        picked = c.sem(name + "_picked")
        summed = c.sem(name + "_summed")
        added = c.sem(name + "_added")
        passed = c.sem(name + "_passed")
        block = ctx.enter_context(nc.Block())

        def general(engine, eng, body):
            flag = nc.values_load_multi_w_load_instructions(
                unsorted[0:1, 0:1], engines=(engine,), min_val=0, max_val=EDGES_PAD,
                skip_runtime_bounds_check_because="it is a count of edges")[1][0]
            with eng.If(flag):
                if engine == EngineType.DVE:
                    nc.vector.memset(agg_t[:], 0.0).then_inc(added, 1)
                    eng.wait_ge(added, 1)
                with eng.Fori(0, COLS) as n:
                    body(n)

        @block.sync
        def _(sp):
            def body(n):
                sp.wait_ge(added, n * GROUPS + 1)
                sp.dma_start(rb[:], rec[bass.ds(n * P, P), :]).then_inc(got_rec, 16)
                sp.dma_start(at[:], attr_t[:, bass.ds(n * P, P)]).then_inc(got_at, 16)
            general(EngineType.SP, sp, body)

        @block.gpsimd
        def _(pool):
            def body(n):
                pool.wait_ge(got_rec, n * 16 + 16)
                pool.sem_inc(passed, 1)
                pool.indirect_dma_start(out=rows[:], out_offset=None, in_=table,
                                        in_offset=bass.IndirectOffsetOnAxis(ap=rb[:, 0:1], axis=0)).then_inc(got_rows, 16)
            general(EngineType.Pool, pool, body)

        @block.vector
        def _(dve):
            def body(n):
                dve.wait_ge(got_rec, n * 16 + 16)
                dve.wait_ge(got_rows, n * 16 + 16)
                dve.wait_ge(edge_done, n + 1)
                nc.vector.tensor_tensor(msg[:], rows[:], pe_edge[:, 0:D], ALU.mult).then_inc(msg_done, 1)
                for g in range(GROUPS):
                    for a in range(GROUP):
                        t = g * GROUP + a
                        last = nc.vector.tensor_scalar(pick[:, a], node_ids[:, t * P:(t + 1) * P], rb[:, 1:2].bitcast(FP32), None,
                                                       ALU.is_equal)
                    last.then_inc(picked, 1)
                    dve.wait_ge(summed, n * GROUPS + (g + 1))
                    for a in range(GROUP):
                        t = g * GROUP + a
                        at_tile = agg_t[:, :, t * P:(t + 1) * P]
                        last = nc.vector.tensor_tensor(at_tile, at_tile, pa[a // 2][:, a % 2], ALU.add)
                    last.then_inc(added, 1)
                    dve.wait_ge(added, n * GROUPS + (g + 2))
            general(EngineType.DVE, dve, body)

        @block.tensor
        def _(pe):
            def body(n):
                pe.wait_ge(got_at, n * 16 + 16)
                nc.tensor.matmul(pe_edge[:, 0:D], at[:], w_edge[:], start=True, stop=True).then_inc(edge_done, 1)
                pe.wait_ge(msg_done, n + 1)
                for g in range(GROUPS):
                    pe.wait_ge(picked, n * GROUPS + (g + 1))
                    for a in range(GROUP):
                        for k in range(KD):
                            last = nc.tensor.matmul(pa[a // 2][:, a % 2, k], msg[:, k * P:(k + 1) * P], pick[:, a],
                                                    start=True, stop=True)
                    last.then_inc(summed, 1)
            general(EngineType.PE, pe, body)


@phase
def rank(c, name, ids, consts, base, posrec, ident, pos_flat):
    nc = c.nc
    B = 3
    cuts = [(s, min(512, RANK_LEN - s)) for s in range(0, RANK_LEN, 512)]
    rows8 = COLS // 8
    with ExitStack() as ctx:
        ids_b = c.sb(ctx, name + "_ids", [P, B, RANK_LEN], BF16)
        hit = c.sb(ctx, name + "_hit", [P, RANK_LEN], BF16)
        run = c.sb(ctx, name + "_run", [P, 2, RANK_LEN], FP32)
        place = c.sb(ctx, name + "_place", [P, 2, RANK_LEN], FP32)
        unit = c.sb(ctx, name + "_unit", [P, RANK_LEN], BF16)
        flat = c.sb(ctx, name + "_flat", [HALVES, 2, RANK_LEN], FP32)
        by_col = c.sb(ctx, name + "_by_col", [rows8, 8, P], FP32)
        pp = [c.ps(ctx, f"{name}_pp{u}", [HALVES, 512]) for u in range(4)]
        pt = [c.ps(ctx, f"{name}_pt{u}", [P, 4, P]) for u in range(2)]
        loaded = [c.sem(f"{name}_loaded{u}") for u in range(B)]
        stored = [c.sem(f"{name}_stored{u}") for u in range(2)]
        hits = c.sem(name + "_hits")
        scanned = c.sem(name + "_scanned")
        placed = c.sem(name + "_placed")
        summed = c.sem(name + "_summed")
        kept = c.sem(name + "_kept")
        unit_set = c.sem(name + "_unit_set")
        reloaded = c.sem(name + "_reloaded")
        turned = c.sem(name + "_turned")
        bucket, halves = consts["bucket"], consts["halves"]
        ids_h = ids.rearrange("(h n) -> h n", h=HALVES)
        flat_h = pos_flat.rearrange("(h n) -> h n", h=HALVES)
        nk = len(cuts)
        block = ctx.enter_context(nc.Block())

        @block.sync
        def _(sp):
            for k in range(RANK_BLOCKS):
                if k >= B:
                    sp.wait_ge(hits, k - (B - 1))
                for h in range(HALVES):
                    sp.dma_start(ids_b[h * 64:h * 64 + 64, k % B],
                                 ids_h[h:h + 1, k * RANK_LEN:(k + 1) * RANK_LEN].broadcast_to([64, RANK_LEN])).then_inc(loaded[k % B], 16)
            for u in range(2):
                sp.wait_ge(stored[u], 16 * (RANK_BLOCKS // 2))
            sp.dma_start(by_col[:], pos_flat.rearrange("(b r p) -> r b p", b=8, p=P)).then_inc(reloaded, 16)

        @block.vector
        def _(dve):
            nc.vector.memset(unit[:], 1.0).then_inc(unit_set, 1)
            dve.wait_ge(unit_set, 1)
            for k in range(RANK_BLOCKS):
                u = k % 2
                dve.wait_ge(loaded[k % B], 16 * HALVES * (k // B + 1))
                if k >= 1:
                    dve.wait_ge(placed, k)
                nc.vector.tensor_scalar(hit[:], ids_b[:, k % B], bucket[:, 0:1], None, ALU.is_equal).then_inc(hits, 1)
                dve.wait_ge(hits, k + 1)
                if k >= 1:
                    dve.wait_ge(scanned, k)
                start = base[:, 0:1] if k == 0 else run[:, 1 - u, RANK_LEN - 1:RANK_LEN]
                nc.vector.tensor_tensor_scan(run[:, u], unit[:], hit[:], start, ALU.mult, ALU.add).then_inc(scanned, 1)
                dve.wait_ge(scanned, k + 1)
                if k >= 2:
                    dve.wait_ge(summed, (k - 1) * nk)
                nc.vector.tensor_tensor(place[:, u], run[:, u], hit[:], ALU.mult).then_inc(placed, 1)
            for u in range(2):
                dve.wait_ge(turned, u + 1)
                nc.vector.tensor_copy(posrec[:, u * (COLS // 2):(u + 1) * (COLS // 2), 0].rearrange("p (b r) -> p b r", b=4),
                                      pt[u][:, :, 0:rows8])

        @block.tensor
        def _(pe):
            for k in range(RANK_BLOCKS):
                pe.wait_ge(placed, k + 1)
                for n, (s, m) in enumerate(cuts):
                    if k * nk + n >= 4:
                        pe.wait_ge(kept, k * nk + n - 3)
                    nc.tensor.matmul(pp[(k * nk + n) % 4][:, 0:m], halves[:], place[:, k % 2, s:s + m],
                                     start=True, stop=True).then_inc(summed, 1)
            pe.wait_ge(reloaded, 16)
            for u in range(2):
                for b in range(4):
                    last = nc.tensor.transpose(pt[u][:, b, 0:rows8], by_col[:, u * 4 + b], ident[0:rows8, 0:rows8])
                last.then_inc(turned, 1)

        @block.scalar
        def _(act):
            for k in range(RANK_BLOCKS):
                u = k % 2
                if k >= 2:
                    act.wait_ge(stored[u], 16 * (k // 2))
                for n, (s, m) in enumerate(cuts):
                    act.wait_ge(summed, k * nk + n + 1)
                    nc.scalar.activation(flat[:, u, s:s + m], pp[(k * nk + n) % 4][:, 0:m], ACT.Copy).then_inc(kept, 1)
                act.wait_ge(kept, (k + 1) * nk)
                act.dma_start(flat_h[:, k * RANK_LEN:(k + 1) * RANK_LEN], flat[:, u]).then_inc(stored[u], 16)


@phase
def aggregate_edges(c, name, table, rec, rec_words, tab, node_ids, agg_t, attr_t=None, w_edge=None, beside=None):
    nc = c.nc
    U = UNROLL
    with ExitStack() as ctx:
        with_attr = attr_t is not None
        rb = c.sb(ctx, name + "_rec", [P, U, rec_words], I32)
        rows = c.sb(ctx, name + "_rows", [P, U, D], FP32)
        pick = c.sb(ctx, name + "_pick", [P, U, P], FP32)
        msg = rows
        if with_attr:
            at = c.sb(ctx, name + "_attr", [ATTR, U, P], FP32)
            pe_edge = [c.ps(ctx, f"{name}_pe{u}", [P, 512]) for u in range(2)]
            got_at = [c.sem(f"{name}_got_at{u}") for u in range(U)]
            edge_done = [c.sem(f"{name}_edge_done{u}") for u in range(U)]
            msg_done = [c.sem(f"{name}_msg_done{u}") for u in range(U)]
        else:
            picked = [c.sem(f"{name}_picked{u}") for u in range(U)]
        pa = [c.ps(ctx, f"{name}_pa{u}", [P, KD, P]) for u in range(2)]
        got_rec = [c.sem(f"{name}_got_rec{u}") for u in range(U)]
        got_rows = [c.sem(f"{name}_got_rows{u}") for u in range(U)]
        summed = [c.sem(f"{name}_summed{u}") for u in range(U)]
        added = [c.sem(f"{name}_added{u}") for u in range(U)]
        zeroed = c.sem(name + "_zeroed")
        passed = c.sem(name + "_passed")
        block = ctx.enter_context(nc.Block())
        if beside is not None:
            beside(block)

        def wait_steps_before(eng, sem, u, i, back):
            if u >= back:
                eng.wait_ge(sem[u - back], i + 1)
            elif not static(i):
                eng.wait_ge(sem[u - back + U], i * 1)

        def numbers(engine, row, s0, top):
            return nc.values_load_multi_w_load_instructions(
                tab[0:1, row, bass.ds(s0, 4)], engines=(engine,), min_val=0, max_val=top,
                skip_runtime_bounds_check_because="the table is clamped to this range when it is made")[1]

        @block.sync
        def _(sp):
            def body(s0, i):
                for u in range(U):
                    if u % 4 == 0:
                        start = numbers(EngineType.SP, 0, s0 + u, EDGES_PAD - P)
                    wait_steps_before(sp, summed, u, i, U)
                    sp.dma_start(rb[:, u], rec[bass.ds(start[u % 4], P), :]).then_inc(got_rec[u], 16)
            unrolled(sp, STEPS, body)

        if with_attr:
            @block.scalar
            def _(act):
                def body(s0, i):
                    for u in range(U):
                        if u % 4 == 0:
                            start = numbers(EngineType.Activation, 0, s0 + u, EDGES_PAD - P)
                        wait_steps_before(act, summed, u, i, U)
                        act.dma_start(at[:, u], attr_t[:, bass.ds(start[u % 4], P)]).then_inc(got_at[u], 16)
                unrolled(act, STEPS, body)

        @block.gpsimd
        def _(pool):
            row_word = 0 if with_attr else 1

            def body(s0, i):
                for u in range(U):
                    wait_steps_before(pool, summed, u, i, U)
                    if not static(i):
                        pool.sem_inc(passed, 1)
                    pool.wait_ge(got_rec[u], i * 16 + 16)
                    pool.sem_inc(passed, 1)
                    pool.indirect_dma_start(
                        out=rows[:, u], out_offset=None, in_=table,
                        in_offset=bass.IndirectOffsetOnAxis(ap=rb[:, u, row_word:row_word + 1], axis=0),
                    ).then_inc(got_rows[u], 16)
            unrolled(pool, STEPS, body)

        @block.vector
        def _(dve):
            nc.vector.memset(agg_t[:] if with_attr else agg_t[:, :, NODES_PAD:], 0.0).then_inc(zeroed, 1)
            dve.wait_ge(zeroed, 1)

            def front(u, i, shift):
                dve.wait_ge(got_rec[u], i * 16 + 16)
                wait_steps_before(dve, summed, u, i, U)
                if with_attr:
                    nc.vector.tensor_scalar(pick[:, u], node_ids[:, bass.ds(shift, P)], rb[:, u, 1:2].bitcast(FP32),
                                            None, ALU.is_equal)
                    dve.wait_ge(got_rows[u], i * 16 + 16)
                    dve.wait_ge(edge_done[u], i + 1)
                    nc.vector.tensor_tensor(msg[:, u], rows[:, u], pe_edge[u % 2][:, 0:D], ALU.mult).then_inc(msg_done[u], 1)
                else:
                    nc.vector.tensor_scalar(pick[:, u], node_ids[:, bass.ds(shift, P)], rb[:, u, 0:1].bitcast(FP32),
                                            rb[:, u, 2:3].bitcast(FP32), ALU.is_equal, ALU.mult).then_inc(picked[u], 1)

            def back(u, i, shift):
                dve.wait_ge(summed[u], i + 1)
                wait_steps_before(dve, added, u, i, 1)
                at_tile = agg_t[:, :, bass.ds(shift, P)]
                nc.vector.tensor_tensor(at_tile, at_tile, pa[u % 2][:], ALU.add).then_inc(added[u], 1)

            def body(s0, i):
                shifts = []
                for u in range(U):
                    if u % 4 == 0:
                        shifts += numbers(EngineType.DVE, 1, s0 + u, TILES * P)
                    front(u, i, shifts[u])
                    if u:
                        back(u - 1, i, shifts[u - 1])
                back(U - 1, i, shifts[-1])
            unrolled(dve, STEPS, body)

        @block.tensor
        def _(pe):
            def edge(u, i):
                pe.wait_ge(got_at[u], i * 16 + 16)
                wait_steps_before(pe, msg_done, u, i, 2)
                nc.tensor.matmul(pe_edge[u % 2][:, 0:D], at[:, u], w_edge[:], start=True, stop=True).then_inc(edge_done[u], 1)

            def add_up(u, i):
                if with_attr:
                    pe.wait_ge(msg_done[u], i + 1)
                else:
                    pe.wait_ge(got_rows[u], i * 16 + 16)
                    pe.wait_ge(picked[u], i + 1)
                wait_steps_before(pe, added, u, i, 2)
                for k in range(KD):
                    last = nc.tensor.matmul(pa[u % 2][:, k], msg[:, u, k * P:(k + 1) * P], pick[:, u],
                                            start=True, stop=True)
                last.then_inc(summed[u], 1)

            def body(s0, i):
                for u in range(U):
                    if with_attr:
                        edge(u, i)
                        if u:
                            add_up(u - 1, i)
                    else:
                        add_up(u, i)
                if with_attr:
                    add_up(U - 1, i)
            unrolled(pe, STEPS, body)


@phase
def first_dense(c, agg_t, xn_t, w_rel, w_root, b_rel, gamma, beta, eps, scale, shift, beside=None):
    nc = c.nc
    with ExitStack() as ctx:
        ph = [[c.ps(ctx, f"fd_ph{u}{m}", [P, 512]) for m in range(KD)] for u in range(2)]
        st = c.sb(ctx, "fd_st", [P, KD, WIDES, 6], FP32)
        mv = c.sb(ctx, "fd_mv", [P, KD, 2], FP32)
        sd = c.sb(ctx, "fd_sd", [P, KD], FP32)
        rs = c.sb(ctx, "fd_rs", [P, KD], FP32)
        tmp = c.sb(ctx, "fd_tmp", [P, KD], FP32)
        multiplied = c.sem("fd_multiplied")
        relued = c.sem("fd_relued")
        passed = c.sem("fd_passed")
        stats = c.sem("fd_stats")
        small = c.sem("fd_small")
        root = c.sem("fd_root")
        block = ctx.enter_context(nc.Block())
        if beside is not None:
            beside(block)

        @block.tensor
        def _(pe):
            def body(g, u):
                if not (static(g) and g < 2):
                    pe.wait_ge(relued, g * 2 - 2)
                for m in range(KD):
                    steps = [(w, x, k) for w, x in ((w_rel, agg_t), (w_root, xn_t)) for k in range(KD)]
                    for n, (w, x, k) in enumerate(steps):
                        last = nc.tensor.matmul(ph[u][m][:, 0:WIDE], w[:, k, m * P:(m + 1) * P],
                                                x[:, k, bass.ds(g * WIDE, WIDE)], start=n == 0, stop=n == len(steps) - 1)
                last.then_inc(multiplied, 1)
            pairs(pe, WIDES, body)

        @block.scalar
        def _(act):
            def body(g, u):
                act.wait_ge(multiplied, g + 1)
                act.sem_inc(passed, 1)
                for m in range(KD):
                    nc.scalar.activation(agg_t[:, m, bass.ds(g * WIDE, WIDE)], ph[u][m][:, 0:WIDE], ACT.Relu,
                                         bias=b_rel[:, m:m + 1]).then_inc(relued, 1)
            pairs(act, WIDES, body)
            act.wait_ge(small, 1)
            nc.scalar.activation(sd[:], mv[:, :, 1], ACT.Sqrt, bias=eps[:, 0:1]).then_inc(root, 1)

        @block.vector
        def _(dve):
            for g in range(WIDES):
                n = min(WIDE, NODES - g * WIDE)
                dve.wait_ge(relued, g * 2 + 2)
                for m in range(KD):
                    last = nc.vector.bn_stats(st[:, m, g], agg_t[:, m, g * WIDE:g * WIDE + n])
            last.then_inc(stats, 1)
            dve.wait_ge(stats, 1)
            for m in range(KD):
                last = nc.vector.bn_aggr(mv[:, m], st[:, m].rearrange("p g s -> p (g s)"))
            last.then_inc(small, 1)
            dve.wait_ge(root, 1)
            nc.vector.reciprocal(rs[:], sd[:]).then_inc(small, 1)
            dve.wait_ge(small, 2)
            nc.vector.tensor_tensor(scale[:], rs[:], gamma[:], ALU.mult).then_inc(small, 1)
            dve.wait_ge(small, 3)
            nc.vector.tensor_tensor(tmp[:], mv[:, :, 0], scale[:], ALU.mult).then_inc(small, 1)
            dve.wait_ge(small, 4)
            nc.vector.tensor_tensor(shift[:], beta[:], tmp[:], ALU.subtract)


class RecordScatter:

    def __init__(self, c, ctx, posrec, rec1):
        self.c, self.posrec, self.rec1 = c, posrec, rec1
        self.stage = c.sb(ctx, "sr_stage", [P, 2, UNROLL, 1 + REC1], I32)
        self.at = 0

    def part(self, block, name, groups):
        c, stage, first = self.c, self.stage, self.at
        groups = min(groups, COLS // UNROLL - first)
        if groups < 1:
            return
        self.at += groups
        staged = c.sem(name + "_sr_staged")
        gone = [c.sem(f"{name}_sr_gone{u}") for u in range(2)]
        passed = c.sem(name + "_sr_passed")

        @block.gpsimd
        def _(pool):
            def body(g, u):
                if not (static(g) and g < 2):
                    pool.wait_ge(gone[u], (g // 2) * (16 * UNROLL))
                    pool.sem_inc(passed, 1)
                pool.tensor_copy(stage[:, u], self.posrec[:, bass.ds((g + first) * UNROLL, UNROLL)]).then_inc(staged, 1)
                pool.wait_ge(staged, g + 1)
                pool.sem_inc(passed, 1)
                for j in range(UNROLL):
                    pool.indirect_dma_start(
                        out=self.rec1, out_offset=bass.IndirectOffsetOnAxis(ap=stage[:, u, j, 0:1], axis=0),
                        in_=stage[:, u, j, 1:1 + REC1], in_offset=None,
                    ).then_inc(gone[u], 16)
            if groups == 1:
                body(0, 0)
            else:
                pairs(pool, groups, body)
                pool.wait_ge(gone[1], 16 * UNROLL * (groups // 2))
            pool.wait_ge(gone[0], 16 * UNROLL * ((groups + 1) // 2))


@phase
def degrees(c, posrec, dinv, dinv_row, ident, consts, beside):
    nc = c.nc
    with ExitStack() as ctx:
        hi_ids = c.sb(ctx, "dg_hi_ids", [P, TILES], FP32)
        lo_ids = c.sb(ctx, "dg_lo_ids", [P, P], FP32)
        s_i = c.sb(ctx, "dg_si", [P, COLS], I32)
        hl_i = c.sb(ctx, "dg_hli", [P, 2, COLS], I32)
        hl = c.sb(ctx, "dg_hl", [P, 2, COLS], FP32)
        lo = c.sb(ctx, "dg_lo", [P, 2, UNROLL, P], FP32)
        hi = c.sb(ctx, "dg_hi", [P, 2, UNROLL, TILES], FP32)
        hw = c.sb(ctx, "dg_hw", [P, 2, UNROLL, TILES], FP32)
        deg = c.sb(ctx, "dg_deg", [TILES, 2, P], FP32)
        sd = c.sb(ctx, "dg_sd", [TILES, P], FP32)
        pos = c.sb(ctx, "dg_pos", [TILES, P], FP32)
        inv = c.sb(ctx, "dg_inv", [TILES, P], FP32)
        by_tile = c.sb(ctx, "dg_by_tile", [TILES, P], FP32)
        pd = c.ps(ctx, "dg_pd", [P, 512])
        pt = c.ps(ctx, "dg_pt", [P, 512])
        ids_set = c.sem("dg_ids_set")
        split = c.sem("dg_split")
        made = c.sem("dg_made")
        weighted = c.sem("dg_weighted")
        multiplied = c.sem("dg_multiplied")
        small = c.sem("dg_small")
        root = c.sem("dg_root")
        stored = c.sem("dg_stored")
        block = ctx.enter_context(nc.Block())
        beside(block)
        ew = posrec[:, :, 3].bitcast(FP32)

        @block.vector
        def _(dve):
            nc.vector.tensor_copy(s_i[:], posrec[:, :, 1].bitcast(FP32)).then_inc(split, 1)
            nc.vector.tensor_copy(lo_ids[:], consts["node_ids"][:, 0:P])
            nc.vector.tensor_copy(hi_ids[:], consts["node_ids"][:, 0:TILES])
            dve.wait_ge(split, 1)
            nc.vector.tensor_scalar(hl_i[:, 0], s_i[:], 7, None, ALU.arith_shift_right)
            nc.vector.tensor_scalar(hl_i[:, 1], s_i[:], P - 1, None, ALU.bitwise_and).then_inc(split, 1)
            dve.wait_ge(split, 2)
            nc.vector.tensor_copy(hl[:], hl_i[:]).then_inc(split, 1)
            dve.wait_ge(split, 3)

            def body(g, u):
                if not (static(g) and g < 2):
                    dve.wait_ge(multiplied, g - 1)
                j = bass.ds(g * UNROLL, UNROLL)
                nc.vector.tensor_tensor(lo[:, u], lo_ids[:].unsqueeze(1).broadcast_to([P, UNROLL, P]),
                                        hl[:, 1, j].unsqueeze(2).broadcast_to([P, UNROLL, P]), ALU.is_equal)
                nc.vector.tensor_tensor(hi[:, u], hi_ids[:].unsqueeze(1).broadcast_to([P, UNROLL, TILES]),
                                        hl[:, 0, j].unsqueeze(2).broadcast_to([P, UNROLL, TILES]), ALU.is_equal).then_inc(made, 1)
                dve.wait_ge(made, g + 1)
                nc.vector.tensor_tensor(hw[:, u], hi[:, u], ew[:, j].unsqueeze(2).broadcast_to([P, UNROLL, TILES]),
                                        ALU.mult).then_inc(weighted, 1)
            pairs(dve, COLS // UNROLL, body)
            dve.wait_ge(multiplied, COLS // UNROLL)
            nc.vector.tensor_scalar(deg[:, 0], pd[0:TILES, 0:P], 1.0, None, ALU.add).then_inc(small, 1)
            dve.wait_ge(small, 1)
            nc.vector.tensor_scalar(deg[:, 1], deg[:, 0], 1e-30, None, ALU.max).then_inc(small, 1)
            nc.vector.tensor_scalar(pos[:], deg[:, 0], 0.0, None, ALU.is_gt)
            dve.wait_ge(root, 1)
            nc.vector.reciprocal(inv[:], sd[:]).then_inc(small, 1)
            dve.wait_ge(small, 3)
            nc.vector.tensor_tensor(by_tile[:], inv[:], pos[:], ALU.mult).then_inc(small, 1)
            dve.wait_ge(multiplied, COLS // UNROLL + 1)
            nc.vector.tensor_copy(dinv[:], pt[:, 0:TILES])

        @block.scalar
        def _(act):
            act.wait_ge(small, 2)
            nc.scalar.activation(sd[:], deg[:, 1], ACT.Sqrt).then_inc(root, 1)
            act.wait_ge(small, 4)
            act.dma_start(dinv_row.rearrange("(t p) -> t p", p=P), by_tile[:]).then_inc(stored, 16)
            act.wait_ge(stored, 16)

        @block.tensor
        def _(pe):
            def body(g, u):
                pe.wait_ge(weighted, g + 1)
                for j in range(UNROLL):
                    last = nc.tensor.matmul(pd[0:TILES, 0:P], hw[:, u, j], lo[:, u, j],
                                            start=static(g) and g == 0 and j == 0, stop=False, skip_group_check=True)
                last.then_inc(multiplied, 1)
            pairs(pe, COLS // UNROLL, body)
            pe.wait_ge(small, 4)
            nc.tensor.transpose(pt[:, 0:TILES], by_tile[:], ident[0:TILES, 0:TILES]).then_inc(multiplied, 1)


@phase
def choose(c, name, scores, top, chunks, consts, place, expert, prob=None, beside=None):
    nc = c.nc
    E = EXPERTS
    with ExitStack() as ctx:
        s = scores
        won = c.sb(ctx, name + "_won", [P, E, TILES, E], FP32)
        order = c.sb(ctx, name + "_order", [P, TILES, E], FP32)
        mask = c.sb(ctx, name + "_mask", [P, TILES, E], FP32)
        tot = c.sb(ctx, name + "_tot", [P, TILES, E], FP32)
        upto = c.sb(ctx, name + "_upto", [P, E, TILES], FP32)
        row = c.sb(ctx, name + "_row", [P, 4, TILES, E], FP32)
        unit = c.sb(ctx, name + "_unit", [P, TILES], FP32)
        n_i = c.sb(ctx, name + "_ni", [P, 2, E], I32)
        n_f = c.sb(ctx, name + "_nf", [P, 4, E], FP32)
        ge = c.sb(ctx, name + "_ge", [1, E, chunks], FP32)
        ex = c.sb(ctx, name + "_ex", [1, 2, chunks], FP32)
        pick = c.sb(ctx, name + "_pick", [P, 3, TILES], FP32)
        probs = c.sb(ctx, name + "_probs", [P, 4, TILES, E], FP32)
        pk = c.ps(ctx, name + "_pk", [P, 512])
        pn = c.ps(ctx, name + "_pn", [P, 512])
        done = c.sem(name + "_done")
        counted = c.sem(name + "_counted")
        raised = c.sem(name + "_raised")
        block = ctx.enter_context(nc.Block())
        if beside is not None:
            beside(block)

        @block.scalar
        def _(act):
            if prob is not None:
                act.wait_ge(done, 2)
                nc.scalar.activation(probs[:, 1], probs[:, 0], ACT.Exp).then_inc(raised, 1)

        @block.vector
        def _(dve):
            n = [0]

            def then(ins):
                n[0] += 1
                ins.then_inc(done, 1)
                dve.wait_ge(done, n[0])

            if prob is not None:
                then(nc.vector.tensor_reduce(pick[:, 0], s[:], AX.X, ALU.max))
                then(nc.vector.tensor_tensor(probs[:, 0], s[:], pick[:, 0].unsqueeze(2).broadcast_to([P, TILES, E]), ALU.subtract))
                dve.wait_ge(raised, 1)
                then(nc.vector.reduce_sum(pick[:, 1], probs[:, 1], AX.X))
                then(nc.vector.reciprocal(pick[:, 2], pick[:, 1]))
                then(nc.vector.tensor_tensor(probs[:, 2], probs[:, 1], pick[:, 2].unsqueeze(2).broadcast_to([P, TILES, E]), ALU.mult))
                by = probs[:, 2]
            else:
                by = s[:]
            then(nc.vector.memset(won[:], 0.0))
            for j in range(E):
                if j + 1 < E:
                    nc.vector.tensor_tensor(won[:, j, :, j + 1:E], by[:, :, j:j + 1].broadcast_to([P, TILES, E - 1 - j]),
                                            by[:, :, j + 1:E], ALU.is_ge)
                if j:
                    nc.vector.tensor_tensor(won[:, j, :, 0:j], by[:, :, j:j + 1].broadcast_to([P, TILES, j]),
                                            by[:, :, 0:j], ALU.is_gt)
            then(nc.vector.memset(unit[:], 1.0))
            then(nc.vector.reduce_sum(order[:], won[:].rearrange("p j t e -> p t e j"), AX.X))
            then(nc.vector.tensor_scalar(mask[:], order[:], float(top), None, ALU.is_lt))
            if prob is not None:
                then(nc.vector.tensor_tensor(probs[:, 3], probs[:, 2], mask[:], ALU.mult))
                then(nc.vector.reduce_sum(prob[:], probs[:, 3], AX.X))
            dve.wait_ge(counted, 1)
            then(nc.vector.tensor_copy(tot[:], pn[:, 0:TILES * E].rearrange("p (t e) -> p t e", e=E)))
            for e in range(E):
                last = nc.vector.tensor_tensor_scan(upto[:, e], unit[:], tot[:, :, e], 0.0, ALU.mult, ALU.add)
            then(last)
            then(nc.vector.tensor_scalar(n_i[:, 0], upto[:, :, TILES - 1], float(P - 1), None, ALU.add))
            then(nc.vector.tensor_scalar(n_i[:, 1], n_i[:, 0], 7, None, ALU.arith_shift_right))
            then(nc.vector.tensor_copy(n_f[:, 0], n_i[:, 1]))
            then(nc.vector.tensor_tensor_scan(n_f[:, 1], unit[:, 0:E], n_f[:, 0], 0.0, ALU.mult, ALU.add))
            then(nc.vector.tensor_tensor(n_f[:, 2], n_f[:, 1], n_f[:, 0], ALU.subtract))
            then(nc.vector.tensor_scalar(n_f[:, 3], n_f[:, 2], float(P), None, ALU.mult))
            then(nc.vector.tensor_tensor(row[:, 0], upto[:].rearrange("p e t -> p t e"), tot[:], ALU.subtract))
            then(nc.vector.tensor_tensor(row[:, 1], row[:, 0], n_f[:, 3].unsqueeze(1).broadcast_to([P, TILES, E]), ALU.add))
            then(nc.vector.tensor_tensor(row[:, 2], row[:, 1], pk[:, 0:TILES * E].rearrange("p (t e) -> p t e", e=E), ALU.add))
            then(nc.vector.tensor_tensor(row[:, 3], row[:, 2], mask[:], ALU.mult))
            then(nc.vector.tensor_reduce(won[:, 0, :, 0], row[:, 3], AX.X, ALU.max))
            if top == 1:
                then(nc.vector.tensor_copy(place[:, :, 0], won[:, 0, :, 0]))
            else:
                then(nc.vector.reduce_sum(won[:, 1, :, 0], row[:, 3], AX.X))
                nc.vector.tensor_copy(place[:, :, 1], won[:, 0, :, 0])
                then(nc.vector.tensor_tensor(place[:, :, 0], won[:, 1, :, 0], won[:, 0, :, 0], ALU.subtract))
            for e in range(E):
                last = nc.vector.tensor_scalar(ge[:, e], consts["node_ids"][0:1, 0:chunks], n_f[0:1, 2, e:e + 1], None, ALU.is_ge)
            then(last)
            then(nc.vector.reduce_sum(ex[:, 0], ge[:].rearrange("p e c -> p c e"), AX.X))
            then(nc.vector.tensor_scalar(expert[:], ex[:, 0], -1.0, None, ALU.add))

        @block.tensor
        def _(pe):
            pe.wait_ge(done, (6 if prob is not None else 1) + 3)
            m = mask[:].rearrange("p t e -> p (t e)")
            nc.tensor.matmul(pk[:, 0:TILES * E], consts["earlier"][:], m, start=True, stop=True)
            nc.tensor.matmul(pn[:, 0:TILES * E], consts["ones"][:], m, start=True, stop=True).then_inc(counted, 1)


@phase
def dispatch(c, name, xn, place, top, xs, beside=None):
    nc = c.nc
    with ExitStack() as ctx:
        x = c.sb(ctx, name + "_x", [P, 2, GROUP, D], FP32)
        at = c.sb(ctx, name + "_at", [P, 2, GROUP, top], I32)
        loaded = [c.sem(f"{name}_loaded{u}") for u in range(2)]
        gone = [c.sem(f"{name}_gone{u}") for u in range(2)]
        staged = c.sem(name + "_staged")
        passed = c.sem(name + "_passed")
        block = ctx.enter_context(nc.Block())
        if beside is not None:
            beside(block)
        per = 16 * GROUP * top

        @block.sync
        def _(sp):
            def body(g, u):
                if not (static(g) and g < 2):
                    sp.wait_ge(gone[u], (g // 2) * per)
                sp.dma_start(x[:, u], tiles_view(xn)[bass.ds(g, 1)].rearrange("o p a d -> p (o a) d")).then_inc(loaded[u], 16)
            pairs(sp, GROUPS, body)

        @block.gpsimd
        def _(pool):
            def body(g, u):
                if old(g, 2):
                    pool.wait_ge(gone[u], (g // 2) * per)
                    pool.sem_inc(passed, 1)
                pool.tensor_copy(at[:, u], place[:, bass.ds(g * GROUP, GROUP)]).then_inc(staged, 1)
                pool.wait_ge(loaded[u], (g // 2) * 16 + 16)
                pool.sem_inc(passed, 1)
                pool.wait_ge(staged, g + 1)
                pool.sem_inc(passed, 1)
                for t in range(GROUP):
                    for k in range(top):
                        pool.indirect_dma_start(
                            out=xs, out_offset=bass.IndirectOffsetOnAxis(ap=at[:, u, t, k:k + 1], axis=0),
                            in_=x[:, u, t], in_offset=None).then_inc(gone[u], 16)
            pairs(pool, GROUPS, body)
            pool.wait_ge(gone[0], per * ((GROUPS + 1) // 2))
            pool.wait_ge(gone[1], per * (GROUPS // 2))


@phase
def experts(c, name, xs, ys, chunks, expert, ident, hid, w1, b1, w2, b2, beside=None):
    nc = c.nc
    nh = hid // 512
    kh = hid // P
    own = b1 is None
    with ExitStack() as ctx:
        x = c.sb(ctx, name + "_x", [P, 2, D], FP32)
        x_t = c.sb(ctx, name + "_xt", [P, 2, KD, P], FP32)
        h_t = c.sb(ctx, name + "_ht", [P, 2, kh, P], FP32)
        y = c.sb(ctx, name + "_y", [P, 2, D], FP32)
        px = [c.ps(ctx, f"{name}_px{u}", [P, KD, P]) for u in range(2)]
        ph = [[c.ps(ctx, f"{name}_ph{u}{b}", [P, 4, P]) for b in range(nh)] for u in range(2)]
        po = [c.ps(ctx, f"{name}_po{u}", [P, 512]) for u in range(2)]
        loaded = [c.sem(f"{name}_loaded{u}") for u in range(2)]
        stored = [c.sem(f"{name}_stored{u}") for u in range(2)]
        x_turned = c.sem(name + "_x_turned")
        x_copied = c.sem(name + "_x_copied")
        up = c.sem(name + "_up")
        active = c.sem(name + "_active")
        down = c.sem(name + "_down")
        out_done = c.sem(name + "_out_done")
        passed = c.sem(name + "_passed")
        if own:
            w_own = c.sb(ctx, name + "_w_own", [P, 2, KD * hid + kh], FP32)
            fetched = c.sem(name + "_fetched")
        block = ctx.enter_context(nc.Block())
        if beside is not None:
            beside(block)

        def stages(eng, body):
            for s in range(4):
                body(s, s % 2)
            with eng.Fori(2, chunks // 2) as i:
                body(i * 2, 0)
                body(i * 2 + 1, 1)
            for s in range(chunks, chunks + 2):
                body(s, s % 2)

        def runs(n):
            return not static(n) or 0 <= n < chunks

        def number(eng, n):
            return eng.value_load(expert[0:1, bass.ds(n, 1)], min_val=0, max_val=EXPERTS - 1)

        @block.sync
        def _(sp):
            def body(n, u):
                if old(n, 2):
                    sp.wait_ge(x_turned, n - 1)
                sp.dma_start(x[:, u], xs[bass.ds(n * P, P), :]).then_inc(loaded[u], 16)
            pairs(sp, chunks, body)

        @block.tensor
        def _(pe):
            def body(s, u):
                if runs(s):
                    pe.wait_ge(loaded[u], (s // 2) * 16 + 16)
                    if old(s, 2):
                        pe.wait_ge(x_copied, s - 1)
                    for k in range(KD):
                        last = nc.tensor.transpose(px[u][:, k], x[:, u, k * P:(k + 1) * P], ident[:])
                    last.then_inc(x_turned, 1)
                n, v = s - 1, 1 - u
                if runs(n):
                    pe.wait_ge(x_copied, n + 1)
                    if own:
                        pe.wait_ge(fetched, n + 1)
                    for b in range(nh):
                        if old(n, 2):
                            pe.wait_ge(active, n * nh + (b + 1 - 2 * nh))
                        for m in range(b * 4, b * 4 + 4):
                            for k in range(KD):
                                w = w_own[:, v, k * hid + m * P:k * hid + m * P + P] if own else w1[:, k, m * P:(m + 1) * P]
                                last = nc.tensor.matmul(ph[v][b][:, m % 4], w, x_t[:, v, k], start=k == 0, stop=k == KD - 1)
                        last.then_inc(up, 1)
                n, v = s - 2, u
                if runs(n):
                    e = number(pe, n)
                    if old(n, 2):
                        pe.wait_ge(out_done, n - 1)
                    for m in range(kh):
                        if m % 4 == 0:
                            pe.wait_ge(active, n * nh + (m // 4 + 1))
                        last = nc.tensor.matmul(po[v][:, 0:D], h_t[:, v, m],
                                                w2[:, bass.ds(e, 1), m].rearrange("p o n -> p (o n)"),
                                                start=m == 0, stop=m == kh - 1)
                    last.then_inc(down, 1)
            stages(pe, body)

        @block.scalar
        def _(act):
            def body(s, u):
                n, v = s - 1, 1 - u
                if runs(n):
                    for b in range(nh):
                        act.wait_ge(up, n * nh + (b + 1))
                        if old(n, 2) and b == 0:
                            act.wait_ge(down, n - 1)
                        for m in range(b * 4, b * 4 + 4):
                            bias = w_own[:, v, KD * hid + m:KD * hid + m + 1] if own else b1[:, m:m + 1]
                            last = nc.scalar.activation(h_t[:, v, m], ph[v][b][:, m % 4], ACT.Gelu, bias=bias)
                        last.then_inc(active, 1)
                n, v = s - 2, u
                if runs(n):
                    act.wait_ge(out_done, n + 1)
                    act.sem_inc(passed, 1)
                    act.dma_start(ys[bass.ds(n * P, P), :], y[:, v]).then_inc(stored[v], 16)
            stages(act, body)
            for v in range(2):
                act.wait_ge(stored[v], 16 * (chunks // 2))

        @block.vector
        def _(dve):
            def body(s, u):
                if runs(s):
                    if own:
                        e = number(dve, s)
                        if old(s, 2):
                            dve.wait_ge(active, s * nh + (nh - 2 * nh))
                            dve.sem_inc(passed, 1)
                        nc.vector.tensor_copy(w_own[:, u], w1[:, bass.ds(e, 1)].rearrange("p o n -> p (o n)")).then_inc(fetched, 1)
                    dve.wait_ge(x_turned, s + 1)
                    if old(s, 2):
                        dve.wait_ge(up, s * nh + (nh - 2 * nh))
                    nc.vector.tensor_copy(x_t[:, u], px[u][:]).then_inc(x_copied, 1)
                n, v = s - 2, u
                if runs(n):
                    e = number(dve, n)
                    dve.wait_ge(down, n + 1)
                    if old(n, 2):
                        dve.wait_ge(stored[v], (n // 2) * 16)
                    nc.vector.tensor_tensor(y[:, v], po[v][:, 0:D], b2[:, bass.ds(e, 1)].rearrange("p o n -> p (o n)"),
                                            ALU.add).then_inc(out_done, 1)
            stages(dve, body)


@phase
def load_all(c, name, items):
    nc = c.nc
    loaded = c.sem(name + "_loaded")
    with ExitStack() as ctx:
        block = ctx.enter_context(nc.Block())

        @block.sync
        def _(sp):
            for tile, src in items:
                sp.dma_start(tile, src).then_inc(loaded, 16)
            sp.wait_ge(loaded, 16 * len(items))


def const_arrays():
    q = np.arange(P)
    half, tile = q // 64, q % 64
    f = np.float32
    return {
        "bucket": tile[:, None].astype(f),
        "fold": (tile[:, None] == q[None, :]).astype(f),
        "before": ((tile[:, None] < tile[None, :]) | ((tile[:, None] == tile[None, :]) & (half[:, None] < half[None, :]))).astype(f),
        "lower": ((q[:, None] < q[None, :]) & (q[:, None] < 64)).astype(f),
        "diff": ((q[:, None] == q[None, :]).astype(f) - (q[:, None] == q[None, :] - 1).astype(f)),
        "steps": np.arange(STEPS, dtype=f)[None, :],
        "node_ids": np.arange(SLOTS * P, dtype=f)[None, :],
        "earlier": (q[:, None] < q[None, :]).astype(f),
        "ident": np.eye(P, dtype=f),
        "halves": (half[:, None] == np.arange(HALVES)[None, :]).astype(f),
    }


def weights_view(w):
    return w.rearrange("(k p) n -> p k n", p=P)


def row_view(b, n):
    return b.rearrange("(o n) -> o n", o=1).broadcast_to([P, n])


def all_rows(b):
    e, n = b.shape
    return b.rearrange("(o e) n -> o e n", o=1).broadcast_to([P, e, n])


def program(nc, a, out):
    with ExitStack() as ctx:
        c = Core(nc, ctx)
        rows = {k: c.dram(k, [NODES_PAD, D], FP32) for k in ("xn0", "x1", "xn1", "x2", "y2", "x3", "xn3")}
        ids_src = c.dram("ids_src", [EDGES_PAD], BF16)
        ids_dst = c.dram("ids_dst", [EDGES_PAD], BF16)
        rec0 = c.dram("rec0", [EDGES_PAD, REC0], I32)
        rec1 = c.dram("rec1", [EDGES_PAD, REC1], I32)
        dinv_row = c.dram("dinv_row", [NODES_PAD], FP32)
        pos_flat = c.dram("pos_flat", [EDGES_PAD], FP32)
        xs = [c.dram(f"xs{i}", [n * P, D], FP32) for i, n in enumerate((CHUNKS0, CHUNKS1))]
        ys = [c.dram(f"ys{i}", [n * P, D], FP32) for i, n in enumerate((CHUNKS0, CHUNKS1))]

        ident = c.sb(ctx, "ident", [P, P], FP32)
        eps = c.sb(ctx, "eps", [P, 1], FP32)
        ones = c.sb(ctx, "ones", [P, P], FP32)
        halves = c.sb(ctx, "halves", [P, HALVES], FP32)
        bucket = c.sb(ctx, "bucket", [P, 1], FP32)
        earlier = c.sb(ctx, "earlier", [P, P], FP32)
        node_ids = c.sb(ctx, "node_ids", [P, SLOTS * P], FP32)
        dinv = c.sb(ctx, "dinv", [P, TILES], FP32)
        base = [c.sb(ctx, f"base{i}", [P, 1], FP32) for i in range(2)]
        tab = [c.sb(ctx, f"tab{i}", [1, 2, STEPS], I32) for i in range(2)]
        unsorted = c.sb(ctx, "unsorted", [1, 1], I32)
        scores = c.sb(ctx, "scores", [P, TILES, EXPERTS], FP32)
        mv = c.sb(ctx, "mv", [P, TILES, 2], FP32)
        w_edge = c.sb(ctx, "w_edge", [ATTR, D], FP32)
        wg0 = c.sb(ctx, "wg0", [P, KD, EXPERTS], FP32)
        bg0 = c.sb(ctx, "bg0", [P, EXPERTS], FP32)
        place0 = c.sb(ctx, "place0", [P, TILES, TOP0], I32)
        consts = {"ident": ident, "ones": ones, "halves": halves, "bucket": bucket, "earlier": earlier, "node_ids": node_ids}
        set_const = c.sem("set_const")
        posrec = c.sb(ctx, "posrec", [P, COLS, 1 + REC1], I32)
        with ExitStack() as ctx_c:
            for k, n in (("fold", P), ("before", P), ("lower", P), ("diff", P), ("steps", STEPS)):
                consts[k] = c.sb(ctx_c, k, [P, n], FP32)
            widths = {"steps": STEPS, "node_ids": SLOTS * P}
            names = ("ident", "halves", "bucket", "earlier", "node_ids", "fold", "before", "lower", "diff", "steps")
            load_all(c, "const", [(w_edge[:], a["L0_gnn_W_edge"])]
                     + [(consts[k][:], a[k].broadcast_to([P, widths[k]]) if k in widths else a[k]) for k in names])
            with nc.Block() as block:
                @block.vector
                def _(dve):
                    nc.vector.memset(ones[:], 1.0).then_inc(set_const, 1)
                    nc.vector.memset(eps[:], EPS).then_inc(set_const, 1)
                    dve.wait_ge(set_const, 2)

            tile_ids(c, a["src"], a["dst"], ids_src, ids_dst, rec0, posrec, a["src_cols"], a["dst_cols"], a["ew_cols"])
            with ExitStack() as ctx_o:
                check = OrderCheck(c, ctx_o, a["dst"], ones, unsorted)
                count(c, "cd", ids_dst, consts, tab[0], base[0], beside=check.beside)
            count(c, "cs", ids_src, consts, tab[1], base[1])
            rank(c, "rk", ids_src, consts, base[1], posrec, ident, pos_flat)
        scatter = RecordScatter(c, ctx, posrec, rec1)
        with ExitStack() as ctx_z:
            zeros = c.sb(ctx_z, "zeros", [P, CHUNKS0 * D // 4], FP32)
            zeroed = c.nc.alloc_semaphore(name="fill_zeroed")
            filling = Prefetch(c, "fill", [(xs[i].rearrange("(p r) d -> p (r d)", p=P)[:, j * n * D // 4:(j + 1) * n * D // 4],
                                            zeros[:, 0:n * D // 4])
                                           for i, n in enumerate((CHUNKS0, CHUNKS1)) for j in range(4)], after=(zeroed, 1))

            def while_counting(block):
                @block.gpsimd
                def _(pool):
                    pool.memset(zeros[:], 0.0).then_inc(zeroed, 1)
                filling.both(block)
                scatter.part(block, "dg", 12)
            degrees(c, posrec, dinv, dinv_row, ident, consts, beside=while_counting)

        with ExitStack() as ctx_g:
            agg_t = c.sb(ctx_g, "agg_t", [P, KD, SLOTS * P], FP32)
            xn_t = c.sb(ctx_g, "xn_t", [P, KD, NODES_PAD], FP32)
            rows_pass(c, "ln0", a["x"], norm=(eps, None, rows["xn0"], xn_t, ident), beside=lambda b: scatter.part(b, "ln0", 3))
            w = {k: c.sb(ctx_g, k, [P, KD, D], FP32) for k in ("w_rel", "w_root", "w_res")}
            v = {k: c.sb(ctx_g, k, [P, KD], FP32) for k in ("b_rel", "gamma", "beta")}
            scale = c.sb(ctx_g, "bn_scale", [P, KD], FP32)
            shift = c.sb(ctx_g, "bn_shift", [P, KD], FP32)
            fetch = Prefetch(c, "l0d", [(w[k][:], weights_view(a["L0_gnn_W" + k[1:]])) for k in w]
                             + [(v[k][:], a["L0_gnn_" + k]) for k in v]
                             + [(wg0[:], weights_view(a["L0_ffn_Wg"])), (bg0[:], row_view(a["L0_ffn_bg"], EXPERTS))])
            aggregate_edges(c, "e0", rows["xn0"], rec0, REC0, tab[0], node_ids, agg_t, a["attr_t"], w_edge, beside=fetch.both)
            aggregate_any_order(c, "eu", rows["xn0"], rec0, unsorted, node_ids, agg_t, a["attr_t"], w_edge)
            first_dense(c, agg_t, xn_t, w["w_rel"], w["w_root"], v["b_rel"], v["gamma"], v["beta"], eps, scale, shift,
                        beside=lambda b: scatter.part(b, "fd", 5))
            finish_graph(c, "o0", a["x"], agg_t, scale, shift, xn_t, w["w_res"], ident, mv, rows["x1"],
                         beside=lambda b: scatter.part(b, "o0", 5))

        with ExitStack() as ctx_f:
            expert = c.sb(ctx_f, "expert0", [1, CHUNKS0], I32)
            gate_pass(c, "g0", rows["x1"], mv, eps, rows["xn1"], scores, ident, wg0, bg0,
                      beside=lambda b: scatter.part(b, "g0", 3))
            w1 = c.sb(ctx_f, "w1_0", [P, EXPERTS, KD * HID0 + HID0 // P], FP32)
            w2 = c.sb(ctx_f, "w2_0", [P, EXPERTS, HID0 // P, D], FP32)
            b2 = c.sb(ctx_f, "b2_0", [P, EXPERTS, D], FP32)
            w1_by_k = a["L0_ffn_W1"].rearrange("e (k p) n -> k p e n", p=P)
            fetch = Prefetch(c, "l0x", [(w1[:, :, k * HID0:(k + 1) * HID0], w1_by_k[k]) for k in range(KD)]
                             + [(w1[:, :, KD * HID0:], a["b1_experts"]),
                                (w2[:], a["L0_ffn_W2"].rearrange("e (k p) n -> p e k n", p=P)), (b2[:], all_rows(a["L0_ffn_b2"]))])

            def while_choosing(block):
                fetch.start(block)
                scatter.part(block, "c0", 1)
            choose(c, "c0", scores, TOP0, CHUNKS0, consts, place0, expert, beside=while_choosing)
            dispatch(c, "d0", rows["xn1"], place0, TOP0, xs[0], beside=fetch.finish)
            experts(c, "x0", xs[0], ys[0], CHUNKS0, expert, ident, HID0, w1, None, w2, b2,
                    beside=lambda b: scatter.part(b, "x0", COLS))
        w1 = c.sb(ctx, "w1_1", [P, KD, HID1], FP32)
        b1 = c.sb(ctx, "b1_1", [P, HID1 // P], FP32)
        wg = c.sb(ctx, "wg1", [P, HID1 // P, EXPERTS], FP32)
        bg = c.sb(ctx, "bg1", [P, EXPERTS], FP32)
        with ExitStack() as ctx_g:
            agg_t = c.sb(ctx_g, "agg_t2", [P, KD, SLOTS * P], FP32)
            rows_pass(c, "m0", rows["x1"], ys[0], place0, TOP0, x_out=rows["x2"], norm=(eps, dinv, rows["y2"], agg_t, ident))
            w = {k: c.sb(ctx_g, "s" + k, [P, KD, D], FP32) for k in ("W", "W1", "W2")}
            v = {k: c.sb(ctx_g, "s" + k, [P, KD], FP32) for k in ("b", "b1")}
            b2 = c.sb(ctx_g, "sb2", [P, D], FP32)
            dinv_b = c.sb(ctx_g, "dinv_b", [P, NODES_PAD], FP32)
            fetch = Prefetch(c, "l1d", [(w[k][:], weights_view(a["L1_gnn_" + k])) for k in w] + [(v[k][:], a["L1_gnn_" + k]) for k in v]
                             + [(b2[:], row_view(a["L1_gnn_b2"], D)), (dinv_b[:], row_view(dinv_row, NODES_PAD)),
                                (wg[:], weights_view(a["L1_ffn_Wg"])), (bg[:], row_view(a["L1_ffn_bg"], EXPERTS)),
                                (w1[:], weights_view(a["L1_ffn_W1"])), (b1[:], a["b1_cols"])])
            aggregate_edges(c, "e1", rows["y2"], rec1, REC1, tab[1], node_ids, agg_t, beside=fetch.both)
            second_graph(c, "o1", rows["x2"], agg_t, dinv_b, w["W"], v["b"], w["W1"], v["b1"], w["W2"], b2, mv, rows["x3"])

        with ExitStack() as ctx_f:
            place = c.sb(ctx_f, "place1", [P, TILES, TOP1], I32)
            prob = c.sb(ctx_f, "prob", [P, TILES], FP32)
            expert = c.sb(ctx_f, "expert1", [1, CHUNKS1], I32)
            w2 = c.sb(ctx_f, "w2_1", [P, EXPERTS, HID1 // P, D], FP32)
            b2 = c.sb(ctx_f, "b2_1", [P, EXPERTS, D], FP32)
            gate_pass(c, "g1", rows["x3"], mv, eps, rows["xn3"], scores, ident, wg, bg, w1, b1)
            fetch = Prefetch(c, "l1x", [(w2[:], a["L1_ffn_Wd"].rearrange("e (k p) n -> p e k n", p=P)), (b2[:], all_rows(a["L1_ffn_bd"]))])
            choose(c, "c1", scores, TOP1, CHUNKS1, consts, place, expert, prob, beside=fetch.start)
            dispatch(c, "d1", rows["xn3"], place, TOP1, xs[1], beside=fetch.finish)
            experts(c, "x1", xs[1], ys[1], CHUNKS1, expert, ident, HID1, w1, b1, w2, b2)
            rows_pass(c, "m1", rows["x3"], ys[1], place, TOP1, prob, out)


def kernel(**inputs):
    import concourse.bacc as bacc
    from concourse.bass_utils import run_bass_kernel_spmd as run

    nc = bacc.Bacc("TRN2", target_bir_lowering=False, num_devices=1)
    arrays = {k: np.ascontiguousarray(v) for k, v in inputs.items()}
    x, src, dst = arrays.pop("x"), arrays.pop("src"), arrays.pop("dst")
    attr, ew = arrays.pop("edge_attr_64"), arrays.pop("edge_weight")
    more = EDGES_PAD - EDGES
    arrays["x"] = np.concatenate([x, np.zeros((NODES_PAD - NODES, D), x.dtype)])
    arrays["src"] = np.concatenate([src, np.full(more, NODES_PAD, src.dtype)])
    arrays["dst"] = np.concatenate([dst, np.full(more, NODES_PAD, dst.dtype)])
    arrays["attr_t"] = np.ascontiguousarray(np.concatenate([attr, np.zeros((more, ATTR), attr.dtype)]).T)
    ew = np.concatenate([ew, np.zeros(more, ew.dtype)])
    for name, v in (("src_cols", arrays["src"]), ("dst_cols", arrays["dst"]), ("ew_cols", ew)):
        arrays[name] = np.ascontiguousarray(v.reshape(COLS, P).T)
    arrays["b1_cols"] = np.ascontiguousarray(arrays["L1_ffn_b1"].reshape(HID1 // P, P).T)
    arrays["b1_experts"] = np.ascontiguousarray(arrays["L0_ffn_b1"].reshape(EXPERTS, HID0 // P, P).transpose(2, 0, 1))
    for name in ("L0_gnn_b_rel", "L0_gnn_gamma", "L0_gnn_beta", "L1_gnn_b", "L1_gnn_b1"):
        arrays[name] = np.ascontiguousarray(arrays[name].reshape(KD, P).T)
    arrays.update(const_arrays())
    aps = {k: nc.dram_tensor("in_" + k, v.shape, mybir.dt.from_np(v.dtype), kind="ExternalInput").ap()
           for k, v in arrays.items()}
    out = nc.dram_tensor("out", (NODES_PAD, D), FP32, kind="ExternalOutput").ap()
    program(nc, aps, out)
    result = run(nc, [{"in_" + k: v for k, v in arrays.items()}], core_ids=[0])
    return np.asarray(result.results[0]["out"])[:NODES]
```
